# Optimizing a Trainium2 kernel written in Bass

```python
import numpy as np
import jax
import jax.numpy as jnp

def _softmax(x, axis=-1):
    return jax.nn.softmax(x, axis=axis)

def _gelu(x):
    return jax.nn.gelu(x, approximate=True)

def _silu(x):
    return jax.nn.silu(x)

def _sigmoid(x):
    return jax.nn.sigmoid(x)

def _layernorm(x, axis=-1, eps=1e-05):
    m = jnp.mean(x, axis=axis, keepdims=True)
    v = jnp.var(x, axis=axis, keepdims=True)
    return (x - m) / jnp.sqrt(v + eps)

def _scatter_add(tgt, idx, src, axis=0):
    return tgt.at[idx].add(src)

def _segment_sum(src, seg, n):
    return jax.ops.segment_sum(src, seg, n)
kernel_name = 'mk_hybrid_d1_jaxref_r8_98680d'

def setup_inputs(seed: int=0):
    np.random.seed(seed)
    _w = jnp.asarray

    def _L0_attn_a_setup():
        import jax, jax.numpy as jnp
        import numpy as np
        import math
        NUM_HEADS = 16

        def _alibi_bias(L, num_heads):
            slopes = jnp.power(2.0, jnp.linspace(-4.0, -0.3, num_heads))
            pos = jnp.arange(L, dtype=jnp.float32)
            return -(slopes[:, None] * pos[None, :])
        key = jax.random.key(seed)
        ks = jax.random.split(key, 9)
        B, L, D = (2, 256, 128)
        s = 0.02
        return {'x': jax.random.normal(ks[0], (B, L, D), dtype=jnp.float32), 'Wq': jax.random.normal(ks[1], (D, D), dtype=jnp.float32) * s, 'bq': jax.random.normal(ks[2], (D,), dtype=jnp.float32) * s, 'Wk': jax.random.normal(ks[3], (D, D), dtype=jnp.float32) * s, 'bk': jax.random.normal(ks[4], (D,), dtype=jnp.float32) * s, 'Wv': jax.random.normal(ks[5], (D, D), dtype=jnp.float32) * s, 'bv': jax.random.normal(ks[6], (D,), dtype=jnp.float32) * s, 'Wo': jax.random.normal(ks[7], (D, D), dtype=jnp.float32) * s, 'bo': jax.random.normal(ks[8], (D,), dtype=jnp.float32) * s}
    _L0_attn_a_in = _L0_attn_a_setup()

    def _L0_attn_b_setup():
        import jax, jax.numpy as jnp
        import numpy as np
        LN_EPS = 1e-05

        def _layernorm(x):
            mu = jnp.mean(x, axis=-1, keepdims=True)
            var = jnp.var(x, axis=-1, keepdims=True)
            return (x - mu) * jax.lax.rsqrt(var + LN_EPS)
        key = jax.random.key(seed)
        k1, k2, k3 = jax.random.split(key, 3)
        B, L, D = (2, 512, 128)
        x = jax.random.normal(k1, (B, L, D), dtype=jnp.float32)
        W_qkv = jax.random.normal(k2, (3 * D, D), dtype=jnp.float32) * 0.02
        W_o = jax.random.normal(k3, (D, D), dtype=jnp.float32) * 0.02
        log_gamma = jnp.zeros((16,), dtype=jnp.float32)
        return {'x': x, 'W_qkv': W_qkv, 'W_o': W_o, 'log_gamma': log_gamma}
    _L0_attn_b_in = _L0_attn_b_setup()

    def _L0_ffn_setup():
        import jax, jax.numpy as jnp
        import numpy as np
        TOP_K = 2
        ROUTE_SCALE = 1.0
        EPS = 1e-20
        key = jax.random.key(seed)
        ks = jax.random.split(key, 8)
        dim, hid, E, X = (128, 352, 8, 1)
        std = 0.02
        x = jax.random.normal(ks[0], (2, 256, dim), dtype=jnp.float32)
        w1 = jax.random.normal(ks[1], (E, hid, dim), dtype=jnp.float32) * std
        w2 = jax.random.normal(ks[2], (E, dim, hid), dtype=jnp.float32) * std
        w3 = jax.random.normal(ks[3], (E, hid, dim), dtype=jnp.float32) * std
        new_w1 = jax.random.normal(ks[4], (X, hid, dim), dtype=jnp.float32) * std
        new_w2 = jnp.zeros((X, dim, hid), dtype=jnp.float32)
        new_w3 = jax.random.normal(ks[5], (X, hid, dim), dtype=jnp.float32) * std
        gate_weight = jax.random.normal(ks[6], (E, dim), dtype=jnp.float32) * std
        new_gate_weight = jax.random.normal(ks[7], (X, dim), dtype=jnp.float32) * std
        gate_bias = jnp.zeros((X,), dtype=jnp.float32)
        return dict(x=x, w1=w1, w2=w2, w3=w3, new_w1=new_w1, new_w2=new_w2, new_w3=new_w3, gate_weight=gate_weight, new_gate_weight=new_gate_weight, gate_bias=gate_bias)
    _L0_ffn_in = _L0_ffn_setup()
    _d = {'L0_attn_a_x': _L0_attn_a_in['x'], 'L0_attn_a_Wq': _L0_attn_a_in['Wq'], 'L0_attn_a_bq': _L0_attn_a_in['bq'], 'L0_attn_a_Wk': _L0_attn_a_in['Wk'], 'L0_attn_a_bk': _L0_attn_a_in['bk'], 'L0_attn_a_Wv': _L0_attn_a_in['Wv'], 'L0_attn_a_bv': _L0_attn_a_in['bv'], 'L0_attn_a_Wo': _L0_attn_a_in['Wo'], 'L0_attn_a_bo': _L0_attn_a_in['bo'], 'L0_attn_b_W_qkv': _L0_attn_b_in['W_qkv'], 'L0_attn_b_W_o': _L0_attn_b_in['W_o'], 'L0_attn_b_log_gamma': _L0_attn_b_in['log_gamma'], 'L0_ffn_w1': _L0_ffn_in['w1'], 'L0_ffn_w2': _L0_ffn_in['w2'], 'L0_ffn_w3': _L0_ffn_in['w3'], 'L0_ffn_new_w1': _L0_ffn_in['new_w1'], 'L0_ffn_new_w2': _L0_ffn_in['new_w2'], 'L0_ffn_new_w3': _L0_ffn_in['new_w3'], 'L0_ffn_gate_weight': _L0_ffn_in['gate_weight'], 'L0_ffn_new_gate_weight': _L0_ffn_in['new_gate_weight'], 'L0_ffn_gate_bias': _L0_ffn_in['gate_bias']}
    _x0 = _d['L0_attn_a_x']
    _d['L0_attn_a_x'] = jax.random.normal(jax.random.fold_in(jax.random.key(seed), 1), (4, 1024, 128), dtype=_x0.dtype)
    del _x0
    return _d

def reference(L0_attn_a_x, L0_attn_a_Wq, L0_attn_a_bq, L0_attn_a_Wk, L0_attn_a_bk, L0_attn_a_Wv, L0_attn_a_bv, L0_attn_a_Wo, L0_attn_a_bo, L0_attn_b_W_qkv, L0_attn_b_W_o, L0_attn_b_log_gamma, L0_ffn_w1, L0_ffn_w2, L0_ffn_w3, L0_ffn_new_w1, L0_ffn_new_w2, L0_ffn_new_w3, L0_ffn_gate_weight, L0_ffn_new_gate_weight, L0_ffn_gate_bias):

    def _L0_attn_a_ref(x, Wq, bq, Wk, bk, Wv, bv, Wo, bo):
        import jax, jax.numpy as jnp
        import numpy as np
        import math
        NUM_HEADS = 16

        def _alibi_bias(L, num_heads):
            slopes = jnp.power(2.0, jnp.linspace(-4.0, -0.3, num_heads))
            pos = jnp.arange(L, dtype=jnp.float32)
            return -(slopes[:, None] * pos[None, :])
        B, L, D = x.shape
        H = NUM_HEADS
        hd = D // H
        scale = math.sqrt(hd)

        def proj(W, b):
            return (jnp.einsum('bld,ed->ble', x, W) + b).reshape(B, L, H, hd)
        q = proj(Wq, bq)
        k = proj(Wk, bk)
        v = proj(Wv, bv)
        scores = jnp.einsum('bqhd,bkhd->bhqk', q, k) / scale
        bias = _alibi_bias(L, H)
        scores = scores + bias[None, :, None, :]
        attn = jax.nn.softmax(scores, axis=-1)
        out = jnp.einsum('bhqk,bkhd->bqhd', attn, v).reshape(B, L, D)
        return jnp.einsum('bld,ed->ble', out, Wo) + bo

    def _L0_attn_b_ref(x, W_qkv, W_o, log_gamma):
        import jax, jax.numpy as jnp
        import numpy as np
        LN_EPS = 1e-05

        def _layernorm(x):
            mu = jnp.mean(x, axis=-1, keepdims=True)
            var = jnp.var(x, axis=-1, keepdims=True)
            return (x - mu) * jax.lax.rsqrt(var + LN_EPS)
        B, L, D = x.shape
        H = log_gamma.shape[0]
        dk = D // H
        qkv = (x @ W_qkv.T).reshape(B, L, 3, H, dk)
        q, k, v = (qkv[:, :, 0], qkv[:, :, 1], qkv[:, :, 2])
        k = _layernorm(k)
        gamma = jax.nn.sigmoid(log_gamma).reshape(1, H, 1, 1)
        qT = jnp.transpose(q, (1, 0, 2, 3))
        kT = jnp.transpose(k, (1, 0, 2, 3))
        vT = jnp.transpose(v, (1, 0, 2, 3))

        def step(S, qkv_t):
            q_t, k_t, v_t = qkv_t
            S = gamma * S + v_t[..., :, None] * k_t[..., None, :]
            y_t = jnp.einsum('bhde,bhe->bhd', S, q_t)
            return (S, y_t)
        S0 = jnp.zeros((B, H, dk, dk), dtype=x.dtype)
        _, ys = jax.lax.scan(step, S0, (qT, kT, vT))
        y = jnp.transpose(ys, (1, 0, 2, 3)).reshape(B, L, D)
        return y @ W_o.T

    def _L0_ffn_ref(x, w1, w2, w3, new_w1, new_w2, new_w3, gate_weight, new_gate_weight, gate_bias):
        import jax, jax.numpy as jnp
        import numpy as np
        TOP_K = 2
        ROUTE_SCALE = 1.0
        EPS = 1e-20
        bs, slen, dim = x.shape
        x_flat = x.reshape(-1, dim)
        ew1 = jnp.concatenate([w1, new_w1], axis=0)
        ew2 = jnp.concatenate([w2, new_w2], axis=0)
        ew3 = jnp.concatenate([w3, new_w3], axis=0)
        gate = jnp.concatenate([gate_weight, new_gate_weight], axis=0)
        e_orig = w1.shape[0]
        e_tot = gate.shape[0]
        bias = jnp.concatenate([jnp.zeros((e_orig,), x.dtype), gate_bias])
        scores = jax.nn.sigmoid((x_flat @ gate.T + bias).astype(jnp.float32))
        top_scores, selected = jax.lax.top_k(scores, TOP_K)
        top_scores = top_scores / (jnp.sum(top_scores, axis=-1, keepdims=True) + EPS)
        top_scores = top_scores * ROUTE_SCALE
        onehot = jax.nn.one_hot(selected, e_tot, dtype=jnp.float32)
        cw = jnp.einsum('tk,tke->te', top_scores, onehot)
        out = jnp.zeros_like(x_flat)
        for e in range(e_tot):
            h = jax.nn.silu(x_flat @ ew1[e].T) * (x_flat @ ew3[e].T)
            out = out + cw[:, e:e + 1] * (h @ ew2[e].T)
        return out.reshape(bs, slen, dim)
    x = L0_attn_a_x
    x = x + _L0_attn_a_ref(_layernorm(x, axis=-1), L0_attn_a_Wq, L0_attn_a_bq, L0_attn_a_Wk, L0_attn_a_bk, L0_attn_a_Wv, L0_attn_a_bv, L0_attn_a_Wo, L0_attn_a_bo)
    x = x + _L0_ffn_ref(_layernorm(x, axis=-1), L0_ffn_w1, L0_ffn_w2, L0_ffn_w3, L0_ffn_new_w1, L0_ffn_new_w2, L0_ffn_new_w3, L0_ffn_gate_weight, L0_ffn_new_gate_weight, L0_ffn_gate_bias)
    x = x + _L0_attn_b_ref(_layernorm(x, axis=-1), L0_attn_b_W_qkv, L0_attn_b_W_o, L0_attn_b_log_gamma)
    x = x + _L0_ffn_ref(_layernorm(x, axis=-1), L0_ffn_w1, L0_ffn_w2, L0_ffn_w3, L0_ffn_new_w1, L0_ffn_new_w2, L0_ffn_new_w3, L0_ffn_gate_weight, L0_ffn_new_gate_weight, L0_ffn_gate_bias)
    return x

_drawn_inputs = setup_inputs


def setup_inputs(seed=0):
    import zlib

    import numpy as np

    out = dict(_drawn_inputs(seed))
    spreads = {'L0_attn_b_log_gamma': (0.0, 0.8), 'L0_ffn_new_w2': (0.0, 0.354)}
    factors = {'L0_attn_a_Wq': 8.0,
     'L0_attn_a_bq': 8.0,
     'L0_attn_a_Wk': 8.0,
     'L0_attn_a_bk': 8.0,
     'L0_attn_a_Wv': 2.97,
     'L0_attn_a_bv': 8.0,
     'L0_attn_a_Wo': 2.967,
     'L0_attn_a_bo': 2.673,
     'L0_ffn_w1': 4.275,
     'L0_ffn_w2': 4.152,
     'L0_ffn_w3': 4.148,
     'L0_ffn_gate_weight': 3.238,
     'L0_ffn_new_gate_weight': 2.785}
    for name, (base, spread) in spreads.items():
        noise = np.random.default_rng([zlib.crc32(name.encode()), seed]).standard_normal(out[name].shape)
        drawn = base * np.exp(spread * noise) if base else spread * noise
        out[name] = jnp.asarray(drawn.astype(out[name].dtype))
    for name, factor in factors.items():
        out[name] = (out[name] * factor).astype(out[name].dtype)
    return out
```

```python
import concourse.bass as bass
from concourse import mybir
from contextlib import ExitStack

F32 = mybir.dt.float32
F32R = mybir.dt.float32r
ALU = mybir.AluOpType
ACT = mybir.ActivationFunctionType
AX = mybir.AxisListType
ds = bass.ds

P = 128
B, L, D = 4, 1024, 128
H, HD = 16, 8
TB = L // P
TILES = B * TB
G, HG = 4, 4
GE = HG * HD
BANK = 512
TH = BANK // P
QH = L // BANK
LN_EPS = 1e-5
SCORE_SCALE = 1.0 / HD ** 0.5
NE, HID = 9, 352
HT = -(-HID // P)
TOP, ROUTE_EPS = 2, 1e-20
VW = 32


class Sems:

    def __init__(self, nc, ctx, phase):
        self.make = lambda name: ctx.enter_context(nc.semaphore(f"{phase}_{name}"))

    def __call__(self, *names):
        return [self.make(n) for n in names]


def layernorm_phase(nc, phase, X, XT, ident, extra_wait=None, side_job=None, load=None):
    with ExitStack() as ctx:
        sem = Sems(nc, ctx, phase)
        sb = lambda name, shape, dt=F32: ctx.enter_context(nc.sbuf_tensor(f"{phase}_{name}", shape, dt))
        stats = sb("stats", [P, TILES, 6])
        meanvar = sb("meanvar", [P, TILES, 2])
        std = sb("std", [P, TILES])
        eps = sb("eps", [P, 1])
        xn = sb("xn", [P, 2, TH * P])
        banks = [ctx.enter_context(nc.psum_tensor(f"{phase}_t{i}", [P, BANK], F32)) for i in range(2)]
        (loaded, eps_set, stats_done, aggregated, std_done, inverted, normed, transposed, evacuated) = sem(
            "loaded", "eps_set", "stats_done", "aggregated", "std_done", "inverted", "normed", "transposed", "evacuated")
        QUADS = TILES // TH
        with nc.Block() as block:
            if load is not None:
                @block.sync
                def _(sp):
                    load(sp, loaded)

            @block.vector
            def _(dve):
                nc.vector.memset(eps[:], LN_EPS).then_inc(eps_set, 1)
                if load is not None:
                    dve.wait_ge(loaded, load.total)
                for i in range(TILES):
                    nc.vector.bn_stats(stats[:, i, :], X[:, i, :]).then_inc(stats_done, 1)
                dve.wait_ge(stats_done, TILES)
                for i in range(TILES):
                    nc.vector.bn_aggr(meanvar[:, i, :], stats[:, i, :]).then_inc(aggregated, 1)
                dve.wait_ge(std_done, 1)
                nc.vector.reciprocal(std[:, :], std[:, :]).then_inc(inverted, 1)
                dve.wait_ge(inverted, 1)
                for q in range(QUADS):
                    if q >= 2:
                        dve.wait_ge(transposed, q - 1)
                    for t in range(TH):
                        i = q * TH + t
                        last = nc.vector.tensor_scalar(xn[:, q % 2, t * P:(t + 1) * P], X[:, i, :],
                                                       meanvar[:, i, 0:1], std[:, i:i + 1],
                                                       ALU.subtract, ALU.mult)
                    last.then_inc(normed, 1)

            @block.scalar
            def _(act):
                act.wait_ge(eps_set, 1)
                act.wait_ge(aggregated, TILES)
                nc.scalar.activation(std[:, :], meanvar[:, :, 1], ACT.Sqrt, bias=eps[:, 0:1]).then_inc(std_done, 1)
                for q in range(QUADS):
                    act.wait_ge(transposed, q + 1)
                    nc.scalar.activation(XT[:, q * BANK:(q + 1) * BANK], banks[q % 2][:, :], ACT.Copy)\
                        .then_inc(evacuated, 1)

            @block.tensor
            def _(pe):
                for q in range(QUADS):
                    pe.wait_ge(normed, q + 1)
                    if q >= 2:
                        pe.wait_ge(evacuated, q - 1)
                    for t in range(TH):
                        last = nc.tensor.transpose(banks[q % 2][:, t * P:(t + 1) * P],
                                                   xn[:, q % 2, t * P:(t + 1) * P], ident[:, :])
                    last.then_inc(transposed, 1)

            if side_job is not None:
                side_job(block)


def attention_phase(nc, X, XT, ident, c, w):
    AUX = 3 * GE
    NROW_S = AUX + 2
    NROW_T = NROW_S + 2 * HG
    with ExitStack() as ctx:
        sem = Sems(nc, ctx, "attn")
        sb = lambda name, shape, dt=F32: ctx.enter_context(nc.sbuf_tensor(f"attn_{name}", shape, dt))
        ps = lambda name, shape: ctx.enter_context(nc.psum_tensor(f"attn_{name}", shape, F32))
        Wq3 = sb("Wq3", [D, G, AUX]); Wk3 = sb("Wk3", [D, G, AUX])
        bq3 = sb("bq3", [AUX, G]); bk3 = sb("bk3", [AUX, G]); bq3s = sb("bq3s", [AUX, G])
        WvT = sb("WvT", [D, D]); WoT = sb("WoT", [D, D])
        bvb = sb("bvb", [P, D]); bob = sb("bob", [P, D])
        masks = sb("masks", [AUX, HG])
        V = sb("V", [P, TILES, D])
        Vp = sb("Vp", [P, TB, H, VW])
        Q = [sb(f"Q{g}", [P, L], F32R) for g in range(G)]
        K = [sb(f"K{g}", [P, HG, L], F32R) for g in range(G)]
        Tq = sb("Tq", [AUX, L]); Tk = sb("Tk", [AUX, L]); Kc = sb("Kc", [AUX, L])
        E = sb("E", [P, 2, HG, BANK])
        hmax = sb("hmax", [P, TB * HG, 2])
        nmax = sb("nmax", [P, TB, HG])
        M2 = sb("M2", [P, TB, VW])
        U = sb("U", [P, L])
        rden = sb("rden", [P, TH * HG])
        On = sb("On", [P, TB, D])
        OnT = sb("OnT", [P, L])

        bankT = ps("bankT", [P, HG, BANK])
        bankS = [ps(f"bankS{i}", [P, BANK]) for i in range(2)]
        bankO = ps("bankO", [P, BANK])
        bankM = ps("bankM", [P, BANK])

        (w_loaded, const_loaded, consts_done, bias_set, zero_done, ones_done, x_biased) = sem(
            "w_loaded", "const_loaded", "consts_done", "bias_set", "zero_done", "ones_done", "x_biased")
        (proj_ready, proj_taken, q_high, k_high, k_low, k_copies, q_done, k_done) = sem(
            "proj_ready", "proj_taken", "q_high", "k_high", "k_low", "k_copies", "q_done", "k_done")
        (score_ready, max_taken, max_joined, max_high, aux_in, aux_ready, aux_taken) = sem(
            "score_ready", "max_taken", "max_joined", "max_high", "aux_in", "aux_ready", "aux_taken")
        (tscore_ready, exp_done, pv_done, u_taken) = sem("tscore_ready", "exp_done", "pv_done", "u_taken")
        (ut_ready, rden_done, on_done, ont_ready, ont_taken, y_ready, y_added) = sem(
            "ut_ready", "rden_done", "on_done", "ont_ready", "ont_taken", "y_ready", "y_added")
        (v_ready, v_taken, vp_done, vproj_a, vproj_b) = sem("v_ready", "v_taken", "vp_done", "vproj_a", "vproj_b")

        S_UNITS = TB * HG * 2
        BLOCKS = QH * TB
        PER_BLOCK = 5

        def score_units(k):
            return range(min(PER_BLOCK * k, S_UNITS), min(PER_BLOCK * (k + 1), S_UNITS))

        MISC = {1: ("K", 0), 2: ("K", 1), 3: ("Q", 0), 4: ("Q", 1), 5: ("T", 0), 6: ("T", 1),
                8: ("G", 0), 9: ("G", 1), 11: ("Y", 0), 12: ("Y", 1), 14: ("A", 0), 15: ("A", 1)}

        def misc(k, s, project, score, after):
            kind, h = MISC.get(k, (None, 0))
            ok = {"K": project, "Q": project, "A": score, "T": after, "G": after and s == 0,
                  "Y": after and s == 0}.get(kind, False)
            return (kind, h) if ok else None

        def taken(kind, n, h):
            return {"K": lambda: (proj_taken, 4 * (n + 2) + h + 1), "Q": lambda: (proj_taken, 4 * (n + 2) + h + 3),
                    "A": lambda: (aux_taken, 2 * (n + 1) + h + 1), "T": lambda: (on_done, 2 * (n - 1) + h + 1),
                    "G": lambda: (ont_taken, (n - 4) // 4 * 2 + h + 1 if isinstance(n, int) else None),
                    "Y": lambda: (y_added, (n - 4) // 4 * 2 + h + 1 if isinstance(n, int) else None)}[kind]()

        with nc.Block() as block:
            @block.sync
            def _(sp):
                for dst, src in ((Wq3[:], w["Wq3"]), (Wk3[:], w["Wk3"]), (bq3[:], w["bq3"]), (bk3[:], w["bk3"]),
                                 (WvT[:], w["WvT"]), (WoT[:], w["WoT"]), (masks[:], c["masks"]),
                                 (bvb[:], w["bv"].partition_broadcast(P)), (bob[:], w["bo"].partition_broadcast(P))):
                    sp.dma_start(dst, src).then_inc(w_loaded, 16)
                for g in range(G):
                    if g:
                        sp.wait_ge(consts_done, g)
                    sp.dma_start(E[AUX:NROW_T, :, :, :].rearrange("p a h q -> p (a h q)"),
                                 c["key_aux"][g]).then_inc(const_loaded, 16)
            W_LOADS = 9 * 16

            @block.scalar
            def _(act):
                for g in range(G):
                    act.wait_ge(const_loaded, 16 * (g + 1))
                    nc.scalar.activation(K[g][AUX:NROW_T, :, :].rearrange("p h k -> p (h k)"),
                                         E[AUX:NROW_T, :, :, :].rearrange("p a h q -> p (a h q)"),
                                         ACT.Copy).then_inc(consts_done, 1)
                act.wait_ge(w_loaded, W_LOADS)
                nc.scalar.mul(bq3s[:], bq3[:], SCORE_SCALE).then_inc(bias_set, 1)
                for g in range(G):
                    nc.scalar.activation(Q[g][AUX:P, :], XT[AUX:P, 0:L], ACT.Copy, scale=0.0, bias=1.0)\
                        .then_inc(ones_done, 1)

            @block.gpsimd
            def _(pool):
                nc.gpsimd.memset(Vp[:].rearrange("p t h c -> p (t h c)"), 0.0).then_inc(zero_done, 1)
                nc.gpsimd.memset(M2[:].rearrange("p t c -> p (t c)"), 0.0).then_inc(zero_done, 1)
                pool.wait_ge(zero_done, 2)
                nc.gpsimd.memset(Vp[:, :, :, HD:HD + 1], 1.0).then_inc(zero_done, 1)
                nc.gpsimd.memset(M2[:, :, 0:2], 1.0).then_inc(zero_done, 1)
                pool.wait_ge(w_loaded, W_LOADS)
                for i in range(TILES):
                    nc.gpsimd.tensor_tensor(X[:, i, :], X[:, i, :], bob[:], ALU.add).then_inc(x_biased, 1)

            @block.tensor
            def _(pe):
                pe.wait_ge(w_loaded, W_LOADS)
                for q in range(TILES // TH):
                    if q >= 2:
                        pe.wait_ge(v_taken, q - 1)
                    for t in range(TH):
                        i = q * TH + t
                        last = nc.tensor.matmul(bankS[q % 2][:, t * D:(t + 1) * D], XT[:, i * P:(i + 1) * P],
                                                WvT[:], start=True, stop=True)
                    last.then_inc(v_ready, 1)

            @block.vector
            def _(dve):
                dve.wait_ge(w_loaded, W_LOADS)
                for q in range(TILES // TH):
                    dve.wait_ge(v_ready, q + 1)
                    nc.vector.tensor_tensor(V[:, q * TH:(q + 1) * TH, :],
                                            bankS[q % 2][:].rearrange("p (t e) -> p t e", t=TH),
                                            bvb[:].unsqueeze(1).broadcast_to([P, TH, D]), ALU.add).then_inc(v_taken, 1)

        with nc.Block() as block:
            @block.tensor
            def _(pe):
                def project(n, g, b, kind, h):
                    W = (Wk3 if kind == "K" else Wq3)
                    tokens = XT[:, b * L + h * BANK:b * L + (h + 1) * BANK] if isinstance(b, int) else \
                        XT[:, ds(b * L + h * BANK, BANK)]
                    nc.tensor.matmul(bankM[0:AUX, :], W[:, g, :], tokens, start=True, stop=True)\
                        .then_inc(proj_ready, 1)

                def aux(n, h):
                    if h == 0:
                        pe.wait_ge(aux_in, n + 1)
                    for t in range(TH):
                        last = nc.tensor.matmul(bankM[AUX:P, t * P:(t + 1) * P], M2[:, h * TH + t, :], ident[:],
                                                start=True, stop=True)
                    last.then_inc(aux_ready, 1)

                def score_unit(n, g, m):
                    qt, j, kh = m // (2 * HG), m // 2 % HG, m % 2
                    if m == 0:
                        pe.wait_ge(k_done, n + 1)
                        pe.wait_ge(q_done, n + 1)
                    if not (isinstance(n, int) and n == 0 and m < 2):
                        pe.wait_ge(max_taken, S_UNITS * n + m - 1)
                    nc.tensor.matmul(bankS[m % 2][:], Q[g][0:NROW_S, qt * P:(qt + 1) * P],
                                     K[g][0:NROW_S, j, kh * BANK:(kh + 1) * BANK],
                                     start=True, stop=True).then_inc(score_ready, 1)

                def tscore_pair(n, g, k, p, first):
                    qh, kt = k // TB, k % TB
                    if kt == 0 and p == 0:
                        pe.wait_ge(aux_taken, 2 * n + qh + 1)
                    if not (first and k == 0):
                        pe.wait_ge(exp_done, 2 * BLOCKS * n + 2 * k + p - 1)
                    for j in (2 * p, 2 * p + 1):
                        last = nc.tensor.matmul(bankT[:, j, :], K[g][0:NROW_T, j, kt * P:(kt + 1) * P],
                                                Q[g][0:NROW_T, qh * BANK:(qh + 1) * BANK], start=True, stop=True)
                    last.then_inc(tscore_ready, 1)

                def values(n, g, k, b):
                    qh, kt = k // TB, k % TB
                    if k == 0 and g == 0:
                        pe.wait_ge(vp_done, b + 1)
                    if kt == 0 and not (isinstance(n, int) and n == 0 and qh == 0):
                        pe.wait_ge(u_taken, 2 * n + qh)
                    pe.wait_ge(exp_done, 2 * BLOCKS * n + 2 * k + 2)
                    for j in range(HG):
                        last = nc.tensor.matmul(bankO[32 * j:32 * j + VW, :], Vp[:, kt, g * HG + j, :],
                                                E[:, k % 2, j, :], start=(kt == 0), stop=(kt == TB - 1))
                    last.then_inc(pv_done, 1)

                def transpose_u(n, h):
                    pe.wait_ge(u_taken, 2 * n + h + 1)
                    for t in range(TH):
                        last = nc.tensor.transpose(bankM[:, t * P:(t + 1) * P],
                                                   U[:, (h * TH + t) * P:(h * TH + t + 1) * P], ident[:])
                    last.then_inc(ut_ready, 1)

                def transpose_on(n, h):
                    if h == 0:
                        pe.wait_ge(on_done, 2 * n + 2)
                    for t in range(TH):
                        last = nc.tensor.transpose(bankM[:, t * P:(t + 1) * P], On[:, h * TH + t, :], ident[:])
                    last.then_inc(ont_ready, 1)

                def out_project(b, h):
                    if h == 0:
                        pe.wait_ge(ont_taken, 2 * b + 2)
                    for t in range(TH):
                        last = nc.tensor.matmul(bankM[:, t * D:(t + 1) * D],
                                                OnT[:, (h * TH + t) * P:(h * TH + t + 1) * P], WoT[:],
                                                start=True, stop=True)
                    last.then_inc(y_ready, 1)

                def step(b, s, project_next, score_next, after, first=False):
                    n = 4 * b + s
                    g1, g2 = (s + 1) % 4, (s + 2) % 4
                    b2 = b + (s + 2) // 4
                    for k in range(BLOCKS):
                        units = list(score_units(k)) if score_next else []
                        if units:
                            score_unit(n + 1, g1, units[0])
                        tscore_pair(n, s, k, 0, first)
                        if len(units) > 1:
                            score_unit(n + 1, g1, units[1])
                        tscore_pair(n, s, k, 1, first)
                        if k > 0:
                            values(n, s, k - 1, b)
                        elif not first:
                            if s == 0:
                                values(n - 1, 3, BLOCKS - 1, b - 1)
                            else:
                                values(n - 1, s - 1, BLOCKS - 1, b)
                        if len(units) > 2:
                            score_unit(n + 1, g1, units[2])
                        unit = misc(k, s, project_next, score_next, after)
                        if unit:
                            kind, h = unit
                            pe.wait_ge(*self_free())
                            if kind in "KQ":
                                project(n + 2, g2, b2, kind, h)
                                free_at[0] = (proj_taken, 4 * (n + 2) + (2 if kind == "Q" else 0) + h + 1)
                            elif kind == "A":
                                aux(n + 1, h)
                                free_at[0] = (aux_taken, 2 * (n + 1) + h + 1)
                            elif kind == "T":
                                transpose_u(n - 1, h)
                                free_at[0] = (on_done, 2 * (n - 1) + h + 1)
                            elif kind == "G":
                                transpose_on(n - 1, h)
                                free_at[0] = (ont_taken, 2 * (b - 1) + h + 1)
                            else:
                                out_project(b - 1, h)
                                free_at[0] = (y_added, 2 * (b - 1) + h + 1)
                        for m in units[3:]:
                            score_unit(n + 1, g1, m)

                free_at = [None]

                def self_free():
                    return free_at[0]

                for n in range(2):
                    for i, (kind, h) in enumerate((("K", 0), ("K", 1), ("Q", 0), ("Q", 1))):
                        if free_at[0]:
                            pe.wait_ge(*free_at[0])
                        project(n, n, 0, kind, h)
                        free_at[0] = (proj_taken, 4 * n + i + 1)
                for m in range(S_UNITS):
                    score_unit(0, 0, m)
                for h in range(2):
                    pe.wait_ge(*free_at[0])
                    aux(0, h)
                    free_at[0] = (aux_taken, h + 1)
                step(0, 0, True, True, False, first=True)
                with pe.Fori(0, B - 1) as b:
                    free_at[0] = (aux_taken, 8 * b + 4)
                    step(b, 1, True, True, True)
                    step(b, 2, True, True, True)
                    step(b, 3, True, True, True)
                    step(b + 1, 0, True, True, True)
                free_at[0] = (aux_taken, 2 * 13 + 2)
                step(B - 1, 1, True, True, True)
                step(B - 1, 2, False, True, True)
                step(B - 1, 3, False, False, True)
                n = 4 * B - 1
                values(n, 3, BLOCKS - 1, B - 1)
                for h in range(2):
                    pe.wait_ge(*free_at[0])
                    transpose_u(n, h)
                    free_at[0] = (on_done, 2 * n + h + 1)
                for h in range(2):
                    pe.wait_ge(*free_at[0])
                    transpose_on(n, h)
                    free_at[0] = (ont_taken, 2 * (B - 1) + h + 1)
                for h in range(2):
                    pe.wait_ge(*free_at[0])
                    out_project(B - 1, h)
                    free_at[0] = (y_added, 2 * (B - 1) + h + 1)

            @block.scalar
            def _(act):
                def take_projection(n, g, kind, h):
                    i = (2 if kind == "Q" else 0) + h
                    act.wait_ge(proj_ready, 4 * n + i + 1)
                    T, bias, scale = (Tk, bk3, 1.0) if kind == "K" else (Tq, bq3s, SCORE_SCALE)
                    if h == 0 and not (isinstance(n, int) and n == 0):
                        act.wait_ge(k_low if kind == "K" else q_done, n)
                    nc.scalar.activation(T[:, h * BANK:(h + 1) * BANK], bankM[0:AUX, :], ACT.Identity,
                                         bias=bias[:, g:g + 1], scale=scale).then_inc(proj_taken, 1)

                def take_aux(n, g, h):
                    act.wait_ge(aux_ready, 2 * n + h + 1)
                    nc.scalar.activation(Q[g][AUX:NROW_T, h * BANK:(h + 1) * BANK], bankM[AUX:NROW_T, :], ACT.Copy)\
                        .then_inc(aux_taken, 1)

                def exponentials(n, k, p, first):
                    act.wait_ge(tscore_ready, 2 * BLOCKS * n + 2 * k + p + 1)
                    if not (first and k < 2):
                        act.wait_ge(pv_done, BLOCKS * n + k - 1)
                    nc.scalar.activation(E[:, k % 2, 2 * p:2 * p + 2, :], bankT[:, 2 * p:2 * p + 2, :], ACT.Exp)\
                        .then_inc(exp_done, 1)

                def take_u(n, h):
                    act.wait_ge(pv_done, BLOCKS * n + TB * (h + 1))
                    nc.scalar.activation(U[:, h * BANK:(h + 1) * BANK], bankO[:], ACT.Copy).then_inc(u_taken, 1)

                def take_ont(b, h):
                    act.wait_ge(ont_ready, 2 * b + h + 1)
                    nc.scalar.activation(OnT[:, h * BANK:(h + 1) * BANK], bankM[:], ACT.Copy).then_inc(ont_taken, 1)

                def step(b, s, project_next, score_next, after, first=False):
                    n = 4 * b + s
                    for k in range(BLOCKS):
                        exponentials(n, k, 0, first)
                        exponentials(n, k, 1, first)
                        if k == 0 and not first:
                            take_u(n - 1, 1)
                        if k == TB:
                            take_u(n, 0)
                        unit = misc(k, s, project_next, score_next, after)
                        if unit:
                            kind, h = unit
                            if kind in "KQ":
                                take_projection(n + 2, (s + 2) % 4, kind, h)
                            elif kind == "A":
                                take_aux(n + 1, (s + 1) % 4, h)
                            elif kind == "G":
                                take_ont(b - 1, h)

                for n in range(2):
                    for kind in "KQ":
                        for h in range(2):
                            take_projection(n, n, kind, h)
                for h in range(2):
                    take_aux(0, 0, h)
                step(0, 0, True, True, False, first=True)
                with act.Fori(0, B - 1) as b:
                    step(b, 1, True, True, True)
                    step(b, 2, True, True, True)
                    step(b, 3, True, True, True)
                    step(b + 1, 0, True, True, True)
                step(B - 1, 1, True, True, True)
                step(B - 1, 2, False, True, True)
                step(B - 1, 3, False, False, True)
                take_u(4 * B - 1, 1)
                for h in range(2):
                    take_ont(B - 1, h)

            @block.vector
            def _(dve):
                def high_part(n, g, kind):
                    static = isinstance(n, int)
                    dve.wait_ge(proj_taken, 4 * n + (4 if kind == "Q" else 2))
                    if kind == "K":
                        if not (static and n == 0):
                            dve.wait_ge(k_done, n)
                        nc.vector.tensor_copy(Kc[:].bitcast(F32R), Tk[:]).then_inc(k_high, 1)
                    else:
                        if not (static and n < 4):
                            dve.wait_ge(tscore_ready, 2 * BLOCKS * (n - 3))
                        nc.vector.tensor_copy(Q[g][0:AUX, :], Tq[:]).then_inc(q_high, 1)

                def take_max(n, m):
                    qt, j, kh = m // (2 * HG), m // 2 % HG, m % 2
                    dve.wait_ge(score_ready, S_UNITS * n + m + 1)
                    if m == 0 and not (isinstance(n, int) and n == 0):
                        dve.wait_ge(max_joined, n)
                    nc.vector.reduce_max(hmax[:, qt * HG + j, kh:kh + 1], bankS[m % 2][:], AX.X)\
                        .then_inc(max_taken, 1)

                def join_max(n):
                    dve.wait_ge(max_taken, S_UNITS * (n + 1))
                    nc.vector.tensor_reduce(nmax[:].rearrange("p t j -> p (t j)"), hmax[:], AX.X, ALU.max,
                                            negate=True).then_inc(max_joined, 1)
                    dve.wait_ge(max_joined, n + 1)
                    if not (isinstance(n, int) and n == 0):
                        dve.wait_ge(aux_ready, 2 * n)
                    nc.vector.tensor_copy(M2[:, :, 2:2 + HG].bitcast(F32R), nmax[:]).then_inc(max_high, 1)
                    dve.wait_ge(max_high, n + 1)
                    nc.vector.tensor_tensor(M2[:, :, 2 + HG:2 + 2 * HG], nmax[:], M2[:, :, 2:2 + HG], ALU.subtract)\
                        .then_inc(aux_in, 1)

                def normalise(n, g, h):
                    dve.wait_ge(ut_ready, 2 * n + h + 1)
                    u = bankM[:].rearrange("p (tj c) -> p tj c", c=VW)
                    nc.vector.reciprocal(rden[:], u[:, :, HD]).then_inc(rden_done, 1)
                    dve.wait_ge(rden_done, 2 * n + h + 1)
                    out = On[:, h * TH:(h + 1) * TH, g * GE:(g + 1) * GE].rearrange("p t (j e) -> p t j e", e=HD)
                    nc.vector.tensor_tensor(out, u[:, :, 0:HD].rearrange("p (t j) e -> p t j e", t=TH),
                                            rden[:].rearrange("p (t j) -> p t j", t=TH).unsqueeze(3)
                                            .broadcast_to([P, TH, HG, HD]), ALU.mult).then_inc(on_done, 1)
                    dve.wait_ge(on_done, 2 * n + h + 1)

                def add_output(b, h):
                    dve.wait_ge(y_ready, 2 * b + h + 1)
                    x = X[:, ds(b * TB + h * TH, TH), :]
                    nc.vector.tensor_tensor(x, bankM[:].rearrange("p (t e) -> p t e", t=TH), x, ALU.add)\
                        .then_inc(y_added, 1)

                def pad_values(b):
                    if not (isinstance(b, int) and b == 0):
                        dve.wait_ge(pv_done, 4 * BLOCKS * b)
                    nc.vector.tensor_copy(Vp[:, :, :, 0:HD],
                                          V[:, ds(b * TB, TB), :].rearrange("p t (h e) -> p t h e", e=HD))\
                        .then_inc(vp_done, 1)

                def step(b, s, project_next, score_next, after, first=False):
                    n = 4 * b + s
                    for k in range(BLOCKS):
                        units = list(score_units(k)) if score_next else []
                        for m in units[:2]:
                            take_max(n + 1, m)
                        if k == 0 and s == 0 and not first:
                            pad_values(b)
                        for m in units[2:]:
                            take_max(n + 1, m)
                        if k == 13 and score_next:
                            join_max(n + 1)
                        if project_next and k == 3:
                            high_part(n + 2, (s + 2) % 4, "K")
                        if project_next and k == 5:
                            high_part(n + 2, (s + 2) % 4, "Q")
                        unit = misc(k, s, project_next, score_next, after)
                        if unit and unit[0] == "T":
                            normalise(n - 1, (s - 1) % 4, unit[1])
                        if unit and unit[0] == "Y":
                            add_output(b - 1, unit[1])

                for n in range(2):
                    high_part(n, n, "K")
                    high_part(n, n, "Q")
                pad_values(0)
                for m in range(S_UNITS):
                    take_max(0, m)
                join_max(0)
                step(0, 0, True, True, False, first=True)
                with dve.Fori(0, B - 1) as b:
                    step(b, 1, True, True, True)
                    step(b, 2, True, True, True)
                    step(b, 3, True, True, True)
                    step(b + 1, 0, True, True, True)
                step(B - 1, 1, True, True, True)
                step(B - 1, 2, False, True, True)
                step(B - 1, 3, False, False, True)
                for h in range(2):
                    normalise(4 * B - 1, 3, h)
                for h in range(2):
                    add_output(B - 1, h)

            @block.gpsimd
            def _(pool):
                def low_parts(n, g):
                    static = isinstance(n, int)
                    pool.wait_ge(k_high, n + 1)
                    nc.gpsimd.tensor_tensor(Kc[GE:2 * GE, :], Tk[GE:2 * GE, :], Kc[GE:2 * GE, :], ALU.subtract)\
                        .then_inc(k_low, 1)
                    pool.wait_ge(k_low, n + 1)
                    if not (static and n < 4):
                        pool.wait_ge(tscore_ready, 2 * BLOCKS * (n - 3))
                    for j in range(HG):
                        last = nc.gpsimd.tensor_tensor(K[g][0:AUX, j, :], Kc[:], masks[:, j:j + 1].broadcast_to([AUX, L]),
                                                       ALU.mult)
                    last.then_inc(k_done, 1)
                    pool.wait_ge(k_done, n + 1)
                    pool.wait_ge(q_high, n + 1)
                    nc.gpsimd.tensor_tensor(Q[g][2 * GE:3 * GE, :], Tq[2 * GE:3 * GE, :],
                                            Q[g][2 * GE:3 * GE, :].bitcast(F32), ALU.subtract).then_inc(q_done, 1)

                low_parts(0, 0)
                low_parts(1, 1)
                low_parts(2, 2)
                with pool.Fori(0, B - 1) as b:
                    low_parts(4 * b + 3, 3)
                    low_parts(4 * b + 4, 0)
                    low_parts(4 * b + 5, 1)
                    low_parts(4 * b + 6, 2)
                low_parts(15, 3)


def expert_phase(nc, phase, X, XT, number_in, w):
    with ExitStack() as ctx:
        sem = Sems(nc, ctx, phase)
        sb = lambda name, shape, dt=F32: ctx.enter_context(nc.sbuf_tensor(f"{phase}_{name}", shape, dt))
        w1H, w1L, w3H, w3L = [sb(n, [D, NE * HID], F32R) for n in ("w1H", "w1L", "w3H", "w3L")]
        w2 = sb("w2", [P, NE, HT, D])
        stage = sb("stage", [D, 2, NE * HID])
        XH = sb("XH", [D, B * L], F32R); XL = sb("XL", [D, B * L], F32R)
        gateT = sb("gateT", [D, NE]); gbias = sb("gbias", [P, NE]); number = sb("number", [P, NE])
        scores = sb("scores", [P, TILES, NE])
        top = sb("top", [P, TILES, 8])
        where = sb("where", [P, TILES, 8], mybir.dt.uint32)
        wheref = sb("wheref", [P, TILES, TOP])
        rsum = sb("rsum", [P, TILES]); share = sb("share", [P, TILES, TOP])
        hit = sb("hit", [P, TOP, TILES, NE])
        cw = sb("cw", [P, TILES, NE])
        gated = sb("gated", [P, 2, BANK])
        hidden = sb("hidden", [P, 2, HT, BANK])
        ps = lambda name: ctx.enter_context(nc.psum_tensor(f"{phase}_{name}", [P, BANK], F32))
        bank1 = [ps(f"bank1{i}") for i in range(HT)]
        bank3 = [ps(f"bank3{i}") for i in range(HT)]
        bankY = [ps(f"bankY{i}") for i in range(2)]
        (small_in, w1_in, w3_in, w2_in, split, routed, sig, found, chain) = sem(
            "small_in", "w1_in", "w3_in", "w2_in", "split", "routed", "sig", "found", "chain")
        (up_ready, silu_done, hidden_done, y_ready, y_added) = sem(
            "up_ready", "silu_done", "hidden_done", "y_ready", "y_added")
        CHUNKS = B * L // BANK

        with nc.Block() as block:
            @block.sync
            def _(sp):
                for dst, src in ((gateT[:], w["gateT"]), (gbias[:], w["gbias"].partition_broadcast(P)),
                                 (number[:], number_in.partition_broadcast(P))):
                    sp.dma_start(dst, src).then_inc(small_in, 16)
                sp.dma_start(stage[:, 0, :], w["w1T"]).then_inc(w1_in, 16)
                sp.dma_start(stage[:, 1, :], w["w3T"]).then_inc(w3_in, 16)
                sp.dma_start(w2[:], w["w2T"]).then_inc(w2_in, 16)

            @block.tensor
            def _(pe):
                pe.wait_ge(small_in, 48)
                for i in range(TILES):
                    last = nc.tensor.matmul(bank1[0][:, i * NE:(i + 1) * NE], XT[:, i * P:(i + 1) * P], gateT[:],
                                            start=True, stop=True)
                last.then_inc(routed, 1)

            @block.scalar
            def _(act):
                act.wait_ge(chain, 1)
                nc.scalar.activation(scores[:].rearrange("p t e -> p (t e)"),
                                     scores[:].rearrange("p t e -> p (t e)"), ACT.Sigmoid).then_inc(sig, 1)

            @block.gpsimd
            def _(pool):
                pool.wait_ge(split, 1)
                nc.gpsimd.tensor_tensor(XL[:], XT[:], XH[:].bitcast(F32), ALU.subtract)

            @block.vector
            def _(dve):
                count = [0]

                def link(ins):
                    count[0] += 1
                    ins.then_inc(chain, 1)
                    dve.wait_ge(chain, count[0])

                nc.vector.tensor_copy(XH[:], XT[:]).then_inc(split, 1)
                dve.wait_ge(routed, 1)
                link(nc.vector.tensor_tensor(scores[:], bank1[0][:, 0:TILES * NE].rearrange("p (t e) -> p t e", e=NE),
                                             gbias[:].unsqueeze(1).broadcast_to([P, TILES, NE]), ALU.add))
                dve.wait_ge(w1_in, 16)
                nc.vector.tensor_copy(w1H[:], stage[:, 0, :]).then_inc(split, 1)
                dve.wait_ge(split, 2)
                nc.vector.tensor_tensor(w1L[:], stage[:, 0, :], w1H[:].bitcast(F32), ALU.subtract)
                dve.wait_ge(w3_in, 16)
                nc.vector.tensor_copy(w3H[:], stage[:, 1, :]).then_inc(split, 1)
                dve.wait_ge(split, 3)
                nc.vector.tensor_tensor(w3L[:], stage[:, 1, :], w3H[:].bitcast(F32), ALU.subtract)
                dve.wait_ge(sig, 1)
                for i in range(TILES):
                    nc.vector.max(top[:, i, :], scores[:, i, :]).then_inc(found, 1)
                dve.wait_ge(found, TILES)
                for i in range(TILES):
                    nc.vector.max_index(where[:, i, :], top[:, i, :], scores[:, i, :]).then_inc(found, 1)
                dve.wait_ge(found, 2 * TILES)
                nc.vector.tensor_copy(wheref[:], where[:, :, 0:TOP])
                link(nc.vector.tensor_tensor(rsum[:], top[:, :, 0], top[:, :, 1], ALU.add))
                link(nc.vector.tensor_scalar(rsum[:], rsum[:], ROUTE_EPS, None, ALU.add))
                link(nc.vector.reciprocal(rsum[:], rsum[:]))
                link(nc.vector.tensor_tensor(share[:], top[:, :, 0:TOP], rsum[:].unsqueeze(2)
                                             .broadcast_to([P, TILES, TOP]), ALU.mult))
                for c in range(TOP):
                    link(nc.vector.tensor_tensor(hit[:, c], wheref[:, :, c:c + 1].broadcast_to([P, TILES, NE]),
                                                 number[:].unsqueeze(1).broadcast_to([P, TILES, NE]), ALU.is_equal))
                    link(nc.vector.tensor_tensor(hit[:, c], hit[:, c], share[:, :, c:c + 1]
                                                 .broadcast_to([P, TILES, NE]), ALU.mult))
                nc.vector.tensor_tensor(cw[:], hit[:, 0], hit[:, 1], ALU.add)

        with nc.Block() as block:
            rows = [P, P, HID - 2 * P]

            @block.tensor
            def _(pe):
                pe.wait_ge(w2_in, 16)

                def up(c, e, t, first):
                    n = HT * (NE * c + e) + t
                    tokens = ds(c * BANK, BANK)
                    cols = slice(e * HID + t * P, e * HID + t * P + rows[t])
                    if not (first and e == 0):
                        pe.wait_ge(hidden_done, n - HT + 1)
                    for bank, wH, wL in ((bank1[t], w1H, w1L), (bank3[t], w3H, w3L)):
                        for i, (lhs, rhs) in enumerate(((wH, XH), (wH, XL), (wL, XH))):
                            last = nc.tensor.matmul(bank[0:rows[t], :], lhs[:, cols], rhs[:, tokens],
                                                    start=(i == 0), stop=(i == 2))
                    last.then_inc(up_ready, 1)

                def down(c, e, first):
                    pe.wait_ge(hidden_done, HT * (NE * c + e) + HT)
                    if not (first and e < 2):
                        pe.wait_ge(y_added, NE * c + e - 1 if e >= 2 else NE * c - e)
                    for t in range(TH):
                        for ht in range(HT):
                            last = nc.tensor.matmul(bankY[e % 2][:, t * D:(t + 1) * D],
                                                    hidden[0:rows[ht], e % 2, ht, t * P:(t + 1) * P],
                                                    w2[0:rows[ht], e, ht, :], start=(ht == 0), stop=(ht == HT - 1))
                    last.then_inc(y_ready, 1)

                def chunk(c, first=False):
                    for e in range(NE):
                        up(c, e, 0, first)
                        if e:
                            down(c, e - 1, first)
                        elif not first:
                            down(c - 1, NE - 1, False)
                        up(c, e, 1, first)
                        up(c, e, 2, first)

                chunk(0, first=True)
                with pe.Fori(1, CHUNKS) as c:
                    chunk(c)
                down(CHUNKS - 1, NE - 1, False)

            @block.scalar
            def _(act):
                def chunk(c, first=False):
                    for e in range(NE):
                        for t in range(HT):
                            n = HT * (NE * c + e) + t
                            act.wait_ge(up_ready, n + 1)
                            i = (HT * e + t) % 2
                            if not (first and HT * e + t < 2):
                                act.wait_ge(hidden_done, n - 1 if HT * e + t >= 1 else n)
                            nc.scalar.activation(gated[0:rows[t], i, :], bank1[t][0:rows[t], :], ACT.Silu)\
                                .then_inc(silu_done, 1)

                chunk(0, first=True)
                with act.Fori(1, CHUNKS) as c:
                    chunk(c)

            @block.vector
            def _(dve):
                def add(c, e):
                    dve.wait_ge(y_ready, NE * c + e + 1)
                    for t in range(TH):
                        x = X[:, ds(c * TH + t, 1), :].rearrange("p t e -> p (t e)")
                        last = nc.vector.scalar_tensor_tensor(
                            out=x, in0=bankY[e % 2][:, t * D:(t + 1) * D],
                            scalar=cw[:, ds(c * TH + t, 1), e:e + 1].rearrange("p t e -> p (t e)"),
                            in1=x, op0=ALU.mult, op1=ALU.add)
                    last.then_inc(y_added, 1)

                def chunk(c, first=False):
                    for e in range(NE):
                        for t in range(HT):
                            n = HT * (NE * c + e) + t
                            dve.wait_ge(silu_done, n + 1)
                            if t == 0 and not (first and e < 2):
                                dve.wait_ge(y_ready, NE * c + e - 1 if e >= 2 else NE * c - e)
                            nc.vector.tensor_tensor(hidden[0:rows[t], e % 2, t, :], bank3[t][0:rows[t], :],
                                                    gated[0:rows[t], (HT * e + t) % 2, :], ALU.mult)\
                                .then_inc(hidden_done, 1)
                            if t == 1 and e:
                                add(c, e - 1)
                            elif t == 1 and not first:
                                add(c - 1, NE - 1)

                chunk(0, first=True)
                with dve.Fori(1, CHUNKS) as c:
                    chunk(c)
                add(CHUNKS - 1, NE - 1)


def decay_phase(nc, X, XT, ident, c, w):
    R = B * P
    with ExitStack() as ctx:
        sem = Sems(nc, ctx, "decay")
        sb = lambda name, shape, dt=F32: ctx.enter_context(nc.sbuf_tensor(f"decay_{name}", shape, dt))
        ps = lambda name: ctx.enter_context(nc.psum_tensor(f"decay_{name}", [P, BANK], F32))
        WqT = sb("WqT", [D, D]); WkT = sb("WkT", [D, D]); WvT = sb("WvT", [D, D]); WoT = sb("WoT", [D, D])
        masks = sb("masks", [P, HG])
        same = sb("same", [P, D])
        lag = sb("lag", [P, P])
        causal = sb("causal", [P, P])
        ahead = sb("ahead", [P, P])
        behind = sb("behind", [P, 1])
        lgr = sb("lgr", [P, H]); lgc = sb("lgc", [P, 1])
        tr = sb("tr", [P, 2, H]); tc = sb("tc", [P, 2])
        eps = sb("eps", [P, 1])
        Dm = sb("Dm", [P, H, P])
        Gq = sb("Gq", [P, P])
        Gk = sb("Gk", [P, H])
        Gs = sb("Gs", [P, 1])
        XTc = sb("XTc", [D, 2, R])
        qT = sb("qT", [P, 2, R]); qg = sb("qg", [P, 2, R])
        kraw = sb("kraw", [P, R]); kc = sb("kc", [P, R]); ksq = sb("ksq", [P, R])
        kmean = sb("kmean", [P, B * H]); kstd = sb("kstd", [P, B * H])
        kn = sb("kn", [P, R]); kg = sb("kg", [P, 2, R]); v = sb("v", [P, 2, R])
        km = sb("km", [P, 2, HG, R])
        Am = sb("Am", [P, 2, HG, P])
        S = sb("S", [P, 2, R]); Sadd = sb("Sadd", [P, R])
        y = sb("y", [P, R]); yT = sb("yT", [P, R])
        bankA = [ps("bankA0"), ps("bankA1")]
        bankY, bankS, bankQ, bankK, bankV, bankT = [ps(n) for n in ("bankY", "bankS", "bankQ", "bankK", "bankV", "bankT")]
        (loaded, act_setup, dve_setup, chain) = sem("loaded", "act_setup", "dve_setup", "chain")
        (x_in, q_ready, k_ready, v_ready, q_taken, k_taken, v_taken, qg_done) = sem(
            "x_in", "q_ready", "k_ready", "v_ready", "q_taken", "k_taken", "v_taken", "qg_done")
        (ksum_done, kmean_done, kc_done, ksq_done, kvar_done, kstd_done, krstd_done, kn_done, kg_done) = sem(
            "ksum_done", "kmean_done", "kc_done", "ksq_done", "kvar_done", "kstd_done", "krstd_done", "kn_done",
            "kg_done")
        (kt_ready, km_done, a_ready, am_done, am_used, s_ready, sadd_done, s_done, y_taken) = sem(
            "kt_ready", "km_done", "a_ready", "am_done", "am_used", "s_ready", "sadd_done", "s_done",
            "y_taken")
        (yt_ready, yt_taken, o_ready, o_added) = sem("yt_ready", "yt_taken", "o_ready", "o_added")
        XTv = XT[:].rearrange("d (b c t) -> d b c t", b=B, c=TB)
        Xv = X[:].rearrange("p (b c) e -> p b c e", b=B)
        heads = lambda a: a.rearrange("p (n e) -> p n e", e=HD)

        with nc.Block() as block:
            loads = ((WqT[:], w["b_WqT"]), (WkT[:], w["b_WkT"]), (WvT[:], w["b_WvT"]), (WoT[:], w["b_WoT"]),
                     (masks[:], c["masks_b"]), (same[:], c["same_head"]), (lag[:], c["lag"]),
                     (causal[:], c["causal"]), (ahead[:], c["ahead"]), (behind[:], c["behind"]),
                     (lgr[:], w["log_gamma"].partition_broadcast(P)), (lgc[:], w["log_gamma_rows"]))

            @block.sync
            def _(sp):
                for dst, src in loads:
                    sp.dma_start(dst, src).then_inc(loaded, 16)

            @block.vector
            def _(dve):
                dve.wait_ge(loaded, 16 * len(loads))
                for i, (x, t) in enumerate(((lgr[:], (tr[:, 0, :], tr[:, 1, :])), (lgc[:], (tc[:, 0:1], tc[:, 1:2])))):
                    nc.vector.tensor_scalar(t[1], x, 0.0, None, ALU.min)
                    nc.vector.tensor_scalar(t[0], x, 0.0, None, ALU.max).then_inc(chain, 1)
                    dve.wait_ge(chain, 2 * i + 1)
                    nc.vector.tensor_tensor(t[0], t[1], t[0], ALU.subtract).then_inc(chain, 1)
                    dve.wait_ge(chain, 2 * i + 2)
                nc.vector.memset(eps[:], LN_EPS)
                nc.vector.memset(S[:, 0, :], 0.0).then_inc(dve_setup, 1)
                dve.wait_ge(act_setup, 2)
                nc.vector.tensor_tensor(lgr[:], tr[:, 1, :], tr[:, 0, :], ALU.subtract)
                nc.vector.tensor_tensor(lgc[:], tc[:, 1:2], tc[:, 0:1], ALU.subtract).then_inc(dve_setup, 1)
                dve.wait_ge(act_setup, 5)
                nc.vector.tensor_tensor(Dm[:], Dm[:], causal[:].unsqueeze(1).broadcast_to([P, H, P]), ALU.mult)

            @block.scalar
            def _(act):
                act.wait_ge(dve_setup, 1)
                nc.scalar.activation(tr[:, 0, :], tr[:, 0, :], ACT.Exp).then_inc(chain, 1)
                nc.scalar.activation(tc[:, 0:1], tc[:, 0:1], ACT.Exp).then_inc(chain, 1)
                act.wait_ge(chain, 6)
                nc.scalar.activation(tr[:, 0, :], tr[:, 0, :], ACT.Ln, bias=1.0).then_inc(act_setup, 1)
                nc.scalar.activation(tc[:, 0:1], tc[:, 0:1], ACT.Ln, bias=1.0).then_inc(act_setup, 1)
                act.wait_ge(dve_setup, 2)
                nc.scalar.activation(Gq[:], ahead[:], ACT.Exp, scale=lgc[:, 0:1]).then_inc(act_setup, 1)
                nc.scalar.activation(Gs[:], lgc[:], ACT.Exp, scale=float(P))
                nc.scalar.activation(Gk[:], lgr[:], ACT.Exp, scale=behind[:, 0:1]).then_inc(act_setup, 1)
                for h in range(H):
                    last = nc.scalar.activation(Dm[:, h, :], lag[:], ACT.Exp, scale=lgr[:, h:h + 1])
                last.then_inc(act_setup, 1)

        with nc.Block() as block:
            def steps(eng, prepare, work):
                prepare(0, 0)
                prepare(1, 1); work(0, 0)
                with eng.Fori(0, (TB - 2) // 2) as i:
                    prepare(2 * i + 2, 0); work(2 * i + 1, 1)
                    prepare(2 * i + 3, 1); work(2 * i + 2, 0)
                work(TB - 1, 1)

            static = lambda n, below: isinstance(n, int) and n < below

            @block.tensor
            def _(pe):
                def prepare(n, p):
                    pe.wait_ge(x_in, n + 1)
                    if not static(n, 1):
                        pe.wait_ge(q_taken, n)
                    nc.tensor.matmul(bankQ[:], WqT[:], XTc[:, p, :], start=True, stop=True).then_inc(q_ready, 1)
                    for bank, W, ready, free in ((bankK, WkT, k_ready, k_taken), (bankV, WvT, v_ready, v_taken)):
                        if not static(n, 1):
                            pe.wait_ge(free, n)
                        for b in range(B):
                            last = nc.tensor.matmul(bank[:, b * P:(b + 1) * P], XTc[:, p, b * P:(b + 1) * P], W[:],
                                                    start=True, stop=True)
                        last.then_inc(ready, 1)

                def transpose_keys(n, p):
                    pe.wait_ge(kn_done, n + 1)
                    if not static(n, 1):
                        if not static(n, 2):
                            pe.wait_ge(o_added, n - 1)
                        pe.wait_ge(km_done, n)
                    for b in range(B):
                        last = nc.tensor.transpose(bankT[:, b * P:(b + 1) * P], kn[:, b * P:(b + 1) * P], ident[:])
                    last.then_inc(kt_ready, 1)

                def scores(n, p, u):
                    b, g = u // G, u % G
                    if u == 0:
                        pe.wait_ge(km_done, n + 1)
                        pe.wait_ge(q_taken, n + 1)
                    if not (static(n, 1) and u < 2):
                        pe.wait_ge(am_done, B * G * n + u - 1)
                    for j in range(HG):
                        last = nc.tensor.matmul(bankA[u % 2][:, j * P:(j + 1) * P],
                                                km[g * GE:(g + 1) * GE, p, j, b * P:(b + 1) * P],
                                                qT[g * GE:(g + 1) * GE, p, b * P:(b + 1) * P], start=True, stop=True)
                    last.then_inc(a_ready, 1)

                def past(n, p, b):
                    if b == 0:
                        pe.wait_ge(qg_done, n + 1)
                        if not static(n, 1):
                            pe.wait_ge(s_done, n)
                            pe.wait_ge(y_taken, n)
                    nc.tensor.matmul(bankY[:, b * P:(b + 1) * P], qg[:, p, b * P:(b + 1) * P],
                                     S[:, p, b * P:(b + 1) * P], start=True, stop=False)

                def within(n, p, u):
                    b, g = u // G, u % G
                    if u == 0:
                        pe.wait_ge(v_taken, n + 1)
                    pe.wait_ge(am_done, B * G * n + u + 1)
                    for j in range(HG):
                        col = b * P + g * GE + j * HD
                        last = nc.tensor.matmul(bankY[:, col:col + HD], Am[:, u % 2, j, :], v[:, p, col:col + HD],
                                                start=False, stop=(g == G - 1 and j == HG - 1))
                    last.then_inc(am_used, 1)

                def state(n, p):
                    pe.wait_ge(kg_done, n + 1)
                    if not static(n, 1):
                        pe.wait_ge(sadd_done, n)
                    for b in range(B):
                        cols = slice(b * P, (b + 1) * P)
                        last = nc.tensor.matmul(bankS[:, cols], kg[:, p, cols], v[:, p, cols], start=True, stop=True)
                    last.then_inc(s_ready, 1)

                def output(n, p):
                    pe.wait_ge(y_taken, n + 1)
                    for b in range(B):
                        last = nc.tensor.transpose(bankT[:, b * P:(b + 1) * P], y[:, b * P:(b + 1) * P], ident[:])
                    last.then_inc(yt_ready, 1)
                    pe.wait_ge(yt_taken, n + 1)
                    for b in range(B):
                        last = nc.tensor.matmul(bankT[:, b * P:(b + 1) * P], yT[:, b * P:(b + 1) * P], WoT[:],
                                                start=True, stop=True)
                    last.then_inc(o_ready, 1)

                def work(n, p):
                    last_chunk = isinstance(n, int) and n == TB - 1
                    scores(n, p, 0)
                    for u in range(B * G):
                        if u + 1 < B * G:
                            scores(n, p, u + 1)
                        if u % G == 0:
                            past(n, p, u // G)
                        within(n, p, u)
                        if u == 5:
                            state(n, p)
                        if u == 10 and not last_chunk:
                            transpose_keys(n + 1, 1 - p)
                    pe.wait_ge(km_done, n + 1 if last_chunk else n + 2)
                    output(n, p)

                def prepare_first(n, p):
                    prepare(n, p)
                    if isinstance(n, int) and n == 0:
                        transpose_keys(0, 0)

                steps(pe, prepare_first, work)

            @block.scalar
            def _(act):
                def prepare(n, p):
                    act.wait_ge(k_ready, n + 1)
                    if not static(n, 1):
                        act.wait_ge(kc_done, n)
                        act.wait_ge(ksum_done, n)
                    nc.scalar.copy(kraw[:], bankK[:]).then_inc(k_taken, 1)
                    act.wait_ge(q_ready, n + 1)
                    if not static(n, 2):
                        act.wait_ge(am_used, B * G * (n - 1))
                        act.wait_ge(qg_done, n - 1)
                        act.wait_ge(s_ready, n - 1)
                    nc.scalar.copy(qT[:, p, :], bankQ[:]).then_inc(q_taken, 1)
                    act.wait_ge(v_ready, n + 1)
                    nc.scalar.copy(v[:, p, :], bankV[:]).then_inc(v_taken, 1)
                    act.wait_ge(kvar_done, n + 1)
                    nc.scalar.activation(kstd[:], kstd[:], ACT.Sqrt, scale=1.0 / HD, bias=eps[:, 0:1])\
                        .then_inc(kstd_done, 1)
                    if static(n, 1):
                        mask_keys(n, p)

                def mask_keys(n, p):
                    act.wait_ge(kt_ready, n + 1)
                    for j in range(HG):
                        last = nc.scalar.activation(km[:, p, j, :], bankT[:], ACT.Copy, scale=masks[:, j:j + 1])
                    last.then_inc(km_done, 1)

                def work(n, p):
                    if not (isinstance(n, int) and n == TB - 1):
                        mask_keys(n + 1, 1 - p)
                    act.wait_ge(am_used, B * G * (n + 1))
                    if not static(n, 1):
                        act.wait_ge(yt_ready, n)
                    nc.scalar.copy(y[:], bankY[:]).then_inc(y_taken, 1)
                    act.wait_ge(yt_ready, n + 1)
                    if not static(n, 1):
                        act.wait_ge(o_ready, n)
                    nc.scalar.copy(yT[:], bankT[:]).then_inc(yt_taken, 1)

                steps(act, prepare, work)

            @block.vector
            def _(dve):
                def prepare(n, p):
                    if not static(n, 2):
                        dve.wait_ge(v_ready, n - 1)
                    nc.vector.tensor_copy(XTc[:, p, :].rearrange("d (b t) -> d b t", b=B),
                                          XTv[:, :, ds(n, 1), :].rearrange("d b c t -> d b (c t)")).then_inc(x_in, 1)
                    dve.wait_ge(k_taken, n + 1)
                    if not static(n, 1):
                        dve.wait_ge(kc_done, n)
                    nc.vector.reduce_sum(kmean[:], heads(kraw[:]), AX.X).then_inc(ksum_done, 1)
                    dve.wait_ge(ksum_done, n + 1)
                    nc.vector.tensor_scalar(kmean[:], kmean[:], 1.0 / HD, None, ALU.mult).then_inc(kmean_done, 1)
                    dve.wait_ge(ksq_done, n + 1)
                    nc.vector.reduce_sum(kstd[:], heads(ksq[:]), AX.X).then_inc(kvar_done, 1)
                    dve.wait_ge(kstd_done, n + 1)
                    nc.vector.reciprocal(kstd[:], kstd[:]).then_inc(krstd_done, 1)

                def decay(n, p, u):
                    dve.wait_ge(a_ready, B * G * n + u + 1)
                    if not (static(n, 1) and u < 2):
                        dve.wait_ge(am_used, B * G * n + u - 1)
                    nc.vector.tensor_tensor(Am[:, u % 2].rearrange("p j t -> p (j t)"), bankA[u % 2][:],
                                            Dm[:, (u % G) * HG:(u % G + 1) * HG, :].rearrange("p j t -> p (j t)"),
                                            ALU.mult).then_inc(am_done, 1)

                def work(n, p):
                    for u in range(B * G):
                        decay(n, p, u)
                        if u == 7:
                            dve.wait_ge(s_ready, n + 1)
                            nc.vector.tensor_tensor(Sadd[:].rearrange("p (b e) -> p b e", b=B),
                                                    bankS[:].rearrange("p (b e) -> p b e", b=B),
                                                    same[:].unsqueeze(1).broadcast_to([P, B, D]), ALU.mult)\
                                .then_inc(sadd_done, 1)
                            dve.wait_ge(sadd_done, n + 1)
                            if not static(n, 1):
                                dve.wait_ge(am_used, B * G * (n))
                            nc.vector.scalar_tensor_tensor(out=S[:, 1 - p, :], in0=S[:, p, :], scalar=Gs[:, 0:1],
                                                           in1=Sadd[:], op0=ALU.mult, op1=ALU.add).then_inc(s_done, 1)
                    dve.wait_ge(o_ready, n + 1)
                    x = Xv[:, :, ds(n, 1), :].rearrange("p b c e -> p b (c e)")
                    nc.vector.tensor_tensor(x, bankT[:].rearrange("p (b e) -> p b e", b=B), x, ALU.add)\
                        .then_inc(o_added, 1)

                steps(dve, prepare, work)

            @block.gpsimd
            def _(pool):
                def prepare(n, p):
                    pool.wait_ge(kmean_done, n + 1)
                    spread = lambda a: a.unsqueeze(2).broadcast_to([P, B * H, HD])
                    if not static(n, 1):
                        pool.wait_ge(kvar_done, n)
                    nc.gpsimd.tensor_tensor(heads(kc[:]), heads(kraw[:]), spread(kmean[:]), ALU.subtract)\
                        .then_inc(kc_done, 1)
                    pool.wait_ge(kc_done, n + 1)
                    nc.gpsimd.tensor_tensor(ksq[:], kc[:], kc[:], ALU.mult).then_inc(ksq_done, 1)
                    pool.wait_ge(q_taken, n + 1)
                    if not static(n, 2):
                        pool.wait_ge(am_used, B * G * (n - 1))
                        pool.wait_ge(s_ready, n - 1)
                    nc.gpsimd.tensor_tensor(qg[:, p, :].rearrange("p (b t) -> p b t", b=B),
                                            qT[:, p, :].rearrange("p (b t) -> p b t", b=B),
                                            Gq[:].unsqueeze(1).broadcast_to([P, B, P]), ALU.mult).then_inc(qg_done, 1)
                    pool.wait_ge(krstd_done, n + 1)
                    if not static(n, 1):
                        pool.wait_ge(kt_ready, n)
                    nc.gpsimd.tensor_tensor(heads(kn[:]), heads(kc[:]), spread(kstd[:]), ALU.mult).then_inc(kn_done, 1)
                    pool.wait_ge(kn_done, n + 1)
                    nc.gpsimd.tensor_tensor(kg[:, p, :].rearrange("p (b h e) -> p b h e", b=B, h=H),
                                            kn[:].rearrange("p (b h e) -> p b h e", b=B, h=H),
                                            Gk[:].unsqueeze(1).unsqueeze(3).broadcast_to([P, B, H, HD]),
                                            ALU.mult).then_inc(kg_done, 1)

                steps(pool, prepare, lambda n, p: None)


def build_program(nc, x, c, w, out, stop=None):
    with ExitStack() as ctx:
        sb = lambda name, shape, dt=F32: ctx.enter_context(nc.sbuf_tensor(name, shape, dt))
        X = sb("X", [P, TILES, D])
        ident = sb("ident", [P, P])
        x_tiles = x.rearrange("b (t p) d -> p (b t) d", p=P)

        def load(sp, loaded):
            sp.dma_start(ident[:], c["ident"]).then_inc(loaded, 16)
            for b in range(B):
                sp.dma_start(X[:, b * TB:(b + 1) * TB, :], x_tiles[:, b * TB:(b + 1) * TB, :]).then_inc(loaded, 16)
        load.total = 16 * (B + 1)

        with ExitStack() as ph:
            XT = ph.enter_context(nc.sbuf_tensor("XT", [P, B * L], F32))
            layernorm_phase(nc, "ln0", X, XT, ident, load=load)
            attention_phase(nc, X, XT, ident, c, w)
        if stop != "a":
            with ExitStack() as ph:
                XT = ph.enter_context(nc.sbuf_tensor("XT1", [P, B * L], F32))
                layernorm_phase(nc, "ln1", X, XT, ident)
                expert_phase(nc, "ffn1", X, XT, c["number"], w)
        if stop not in ("a", "f1"):
            with ExitStack() as ph:
                XT = ph.enter_context(nc.sbuf_tensor("XT2", [P, B * L], F32))
                layernorm_phase(nc, "ln2", X, XT, ident)
                decay_phase(nc, X, XT, ident, c, w)
        if stop not in ("a", "f1", "b"):
            with ExitStack() as ph:
                XT = ph.enter_context(nc.sbuf_tensor("XT3", [P, B * L], F32))
                layernorm_phase(nc, "ln3", X, XT, ident)
                expert_phase(nc, "ffn2", X, XT, c["number"], w)

        with ExitStack() as ph:
            stored = ph.enter_context(nc.semaphore("stored"))
            with nc.Block() as block:
                @block.sync
                def _(sp):
                    out_tiles = out.rearrange("b (t p) d -> p (b t) d", p=P)
                    for b in range(B):
                        sp.dma_start(out_tiles[:, b * TB:(b + 1) * TB, :], X[:, b * TB:(b + 1) * TB, :])\
                            .then_inc(stored, 16)
                    sp.wait_ge(stored, 16 * B)


def shape_constants():
    import numpy as np
    rows = np.arange(3 * GE)
    masks = (rows[:, None] % GE // HD == np.arange(HG)[None, :]).astype(np.float32)
    slopes = np.power(np.float32(2.0), np.linspace(-4.0, -0.3, H, dtype=np.float32)).astype(np.float32)
    bias = -(slopes[:, None] * np.arange(L, dtype=np.float32)[None, :]).astype(np.float32)
    high = (bias.view(np.uint32) & np.uint32(0xFFFFF000)).view(np.float32)
    low = bias - high
    aux = np.zeros((G, 2 + 2 * HG, HG, L), np.float32)
    for g in range(G):
        for j in range(HG):
            aux[g, 0, j], aux[g, 1, j] = high[g * HG + j], low[g * HG + j]
            aux[g, 2 + j, j] = 1.0
            aux[g, 2 + HG + j, j] = 1.0
    row = np.arange(P)
    more = {"masks_b": (row[:, None] % GE // HD == np.arange(HG)[None, :]),
            "same_head": row[:, None] // HD == row[None, :] // HD,
            "lag": np.maximum(row[None, :] - row[:, None], 0), "causal": row[None, :] >= row[:, None],
            "ahead": np.broadcast_to(row[None, :] + 1, (P, P)), "behind": (P - 1 - row)[:, None],
            "number": np.arange(NE)}
    more = {k: np.ascontiguousarray(v.astype(np.float32)) for k, v in more.items()}
    return more | {"masks": masks, "key_aux": aux.reshape(G, 2 + 2 * HG, HG * L), "ident": np.eye(P, dtype=np.float32)}


def lay_out(inputs):
    import numpy as np
    a = {k: np.asarray(v) for k, v in inputs.items()}
    thrice = lambda W: np.ascontiguousarray(np.tile(W.T.reshape(D, G, 1, GE), (1, 1, 3, 1)).reshape(D, G, 3 * GE))
    thrice_b = lambda v: np.ascontiguousarray(np.tile(v.reshape(G, 1, GE), (1, 3, 1)).reshape(G, 3 * GE).T)
    return {"Wq3": thrice(a["L0_attn_a_Wq"]), "Wk3": thrice(a["L0_attn_a_Wk"]),
            "bq3": thrice_b(a["L0_attn_a_bq"]), "bk3": thrice_b(a["L0_attn_a_bk"]),
            "WvT": np.ascontiguousarray(a["L0_attn_a_Wv"].T), "WoT": np.ascontiguousarray(a["L0_attn_a_Wo"].T),
            "bv": a["L0_attn_a_bv"], "bo": a["L0_attn_a_bo"]} | lay_out_rest(a)


def lay_out_rest(a):
    import numpy as np
    cat = lambda x, y: np.concatenate([a["L0_ffn_" + x], a["L0_ffn_" + y]], axis=0)
    up = lambda W: np.ascontiguousarray(W.transpose(2, 0, 1).reshape(D, NE * HID))
    w2 = np.zeros((P, NE, HT, D), np.float32)
    down = cat("w2", "new_w2").transpose(2, 0, 1)
    for t in range(HT):
        rows = min(P, HID - t * P)
        w2[:rows, :, t] = down[t * P:t * P + rows]
    Wqkv = a["L0_attn_b_W_qkv"]
    turn = lambda W: np.ascontiguousarray(W.T)
    log_gamma = a["L0_attn_b_log_gamma"]
    return {"w1T": up(cat("w1", "new_w1")), "w3T": up(cat("w3", "new_w3")), "w2T": w2,
            "gateT": turn(cat("gate_weight", "new_gate_weight")),
            "gbias": np.concatenate([np.zeros(NE - 1, np.float32), a["L0_ffn_gate_bias"]]),
            "b_WqT": turn(Wqkv[0:D]), "b_WkT": turn(Wqkv[D:2 * D]), "b_WvT": turn(Wqkv[2 * D:3 * D]),
            "b_WoT": turn(a["L0_attn_b_W_o"]), "log_gamma": log_gamma,
            "log_gamma_rows": np.ascontiguousarray(np.repeat(log_gamma, HD)[:, None])}


def kernel(**inputs):
    import numpy as _np
    import concourse.bacc as _bacc
    from concourse import mybir as _mybir
    from concourse.bass_utils import run_bass_kernel_spmd as _run

    nc = _bacc.Bacc("TRN2", target_bir_lowering=False, num_devices=1)
    arrays = {}

    def declare(prefix, named):
        aps = {}
        for name, a in named.items():
            a = _np.ascontiguousarray(a)
            arrays[prefix + name] = a
            aps[name] = nc.dram_tensor(prefix + name, a.shape, _mybir.dt.from_np(a.dtype), kind="ExternalInput").ap()
        return aps

    x = declare("in_", {"x": _np.asarray(inputs["L0_attn_a_x"])})["x"]
    c = declare("const_", shape_constants())
    w = declare("weight_", lay_out(inputs))
    out = nc.dram_tensor("out_dram", (B, L, D), _mybir.dt.float32, kind="ExternalOutput").ap()
    build_program(nc, x, c, w, out)
    r = _run(nc, [arrays], core_ids=[0])
    return r.results[0]["out_dram"]
```

```python
import concourse.bass as bass
from concourse import mybir
from contextlib import ExitStack

F32 = mybir.dt.float32
F32R = mybir.dt.float32r
ALU = mybir.AluOpType
ACT = mybir.ActivationFunctionType
AX = mybir.AxisListType
ds = bass.ds

P = 128
B, L, D = 4, 1024, 128
H, HD = 16, 8
TB = L // P
TILES = B * TB
G, HG = 4, 4
GE = HG * HD
BANK = 512
TH = BANK // P
QH = L // BANK
LN_EPS = 1e-5
SCORE_SCALE = 1.0 / HD ** 0.5
NE, HID = 9, 352
HT = -(-HID // P)
TOP, ROUTE_EPS = 2, 1e-20
HALVES = 2
HALF = TILES // HALVES
HALF_SLOTS = HALF * TOP + NE - 1
SLOT_TILES = HALVES * HALF_SLOTS
VW = 32


class Sems:

    def __init__(self, nc, ctx, phase):
        self.nc, self.made = nc, []
        self.make = lambda name: ctx.enter_context(nc.semaphore(f"{phase}_{name}"))
        ctx.callback(self.clear)

    def __call__(self, *names):
        made = [self.make(n) for n in names]
        self.made += made
        return made

    def clear(self):
        with self.nc.Block() as block:
            @block.sync
            def _(sp):
                for s in self.made:
                    sp.sem_clear(s)


def layernorm_phase(nc, phase, X, XT, ident, load=None, side_job=None, ident_in=None):
    with ExitStack() as ctx:
        sem = Sems(nc, ctx, phase)
        sb = lambda name, shape, dt=F32: ctx.enter_context(nc.sbuf_tensor(f"{phase}_{name}", shape, dt))
        stats = sb("stats", [P, TILES, 6])
        meanvar = sb("meanvar", [P, TILES, 2])
        std = sb("std", [P, TILES])
        rstd = sb("rstd", [P, TILES])
        eps = sb("eps", [P, 1])
        BANKS = 4
        xn = sb("xn", [P, BANKS, TH * P])
        banks = [ctx.enter_context(nc.psum_tensor(f"{phase}_t{i}", [P, BANK], F32)) for i in range(BANKS)]
        (eps_set, stats_done, aggregated, std_done, inverted, normed, transposed, evacuated) = sem(
            "eps_set", "stats_done", "aggregated", "std_done", "inverted", "normed", "transposed", "evacuated")
        loaded = sem(*[f"loaded{b}" for b in range(B)]) if load else None
        QUADS = TILES // TH
        with nc.Block() as block:
            if load:
                @block.sync
                def _(sp):
                    load(sp, loaded)

            @block.vector
            def _(dve):
                nc.vector.memset(eps[:], LN_EPS).then_inc(eps_set, 1)

                def statistics(b):
                    if load:
                        dve.wait_ge(loaded[b], 16)
                    tiles = range(b * TB, (b + 1) * TB)
                    for i in tiles:
                        nc.vector.bn_stats(stats[:, i, :], X[:, i, :]).then_inc(stats_done, 1)
                    for i in tiles:
                        dve.wait_ge(stats_done, i + 1)
                        nc.vector.bn_aggr(meanvar[:, i, :], stats[:, i, :]).then_inc(aggregated, 1)

                def normalise(b):
                    dve.wait_ge(std_done, b + 1)
                    cols = slice(b * TB, (b + 1) * TB)
                    nc.vector.reciprocal(rstd[:, cols], std[:, cols]).then_inc(inverted, 1)
                    dve.wait_ge(inverted, b + 1)
                    for q in range(b * TB // TH, (b + 1) * TB // TH):
                        if q >= BANKS:
                            dve.wait_ge(transposed, q - BANKS + 1)
                        for t in range(TH):
                            i = q * TH + t
                            last = nc.vector.tensor_scalar(xn[:, q % BANKS, t * P:(t + 1) * P], X[:, i, :],
                                                           meanvar[:, i, 0:1], rstd[:, i:i + 1],
                                                           ALU.subtract, ALU.mult)
                        last.then_inc(normed, 1)

                statistics(0)
                for b in range(1, B):
                    statistics(b)
                    normalise(b - 1)
                normalise(B - 1)

            @block.scalar
            def _(act):
                def deviations(b):
                    if b == 0:
                        act.wait_ge(eps_set, 1)
                    act.wait_ge(aggregated, TB * (b + 1))
                    nc.scalar.activation(std[:, b * TB:(b + 1) * TB], meanvar[:, b * TB:(b + 1) * TB, 1], ACT.Sqrt,
                                         bias=eps[:, 0:1]).then_inc(std_done, 1)

                def evacuate(q):
                    act.wait_ge(transposed, q + 1)
                    nc.scalar.activation(XT[:, q * BANK:(q + 1) * BANK], banks[q % BANKS][:, :], ACT.Copy)\
                        .then_inc(evacuated, 1)

                deviations(0)
                for b in range(1, B):
                    deviations(b)
                    for q in range((b - 1) * TB // TH, b * TB // TH):
                        evacuate(q)
                for q in range((B - 1) * TB // TH, QUADS):
                    evacuate(q)

            @block.tensor
            def _(pe):
                if ident_in is not None:
                    pe.wait_ge(ident_in, 16)
                for q in range(QUADS):
                    pe.wait_ge(normed, q + 1)
                    if q >= BANKS:
                        pe.wait_ge(evacuated, q - BANKS + 1)
                    for t in range(TH):
                        last = nc.tensor.transpose(banks[q % BANKS][:, t * P:(t + 1) * P],
                                                   xn[:, q % BANKS, t * P:(t + 1) * P], ident[:, :])
                    last.then_inc(transposed, 1)

            if side_job is not None:
                side_job(block)


def attention_phase(nc, X, XT, ident, ident_in, c, w, load):
    AUX = 3 * GE
    NROW_S = AUX + 2
    NROW_T = NROW_S + 2 * HG
    ROTATE = 3

    def last_user(u, units):
        return u - ROTATE if u >= ROTATE else max(v for v in range(units) if v % ROTATE == u) - units

    with ExitStack() as ctx:
        sem = Sems(nc, ctx, "attn")
        sb = lambda name, shape, dt=F32: ctx.enter_context(nc.sbuf_tensor(f"attn_{name}", shape, dt))
        ps = lambda name, shape: ctx.enter_context(nc.psum_tensor(f"attn_{name}", shape, F32))
        Wq3 = sb("Wq3", [D, G, AUX]); Wk3 = sb("Wk3", [D, G, AUX])
        bq3 = sb("bq3", [AUX, G]); bk3 = sb("bk3", [AUX, G]); bq3s = sb("bq3s", [AUX, G])
        WvT = sb("WvT", [D, D]); WoT = sb("WoT", [D, D])
        bvb = sb("bvb", [P, D]); bob = sb("bob", [P, D])
        masks = sb("masks", [AUX, HG])
        V = sb("V", [P, TILES, D])
        Vp = sb("Vp", [P, TB, H, VW])
        Q = [sb(f"Q{g}", [P, L], F32R) for g in range(G)]
        K = [sb(f"K{g}", [P, HG, L], F32R) for g in range(G)]
        Tq = sb("Tq", [AUX, L]); Tk = sb("Tk", [AUX, L]); Kc = sb("Kc", [AUX, L])
        E = sb("E", [P, 2, HG, BANK])
        hmax = sb("hmax", [P, 2, TB * HG, QH])
        nmax = sb("nmax", [P, TB, HG])
        M2 = sb("M2", [P, TB, VW])
        U = sb("U", [P, L])
        rden = sb("rden", [P, TH * HG])
        On = sb("On", [P, TB, D])
        ones = U
        OnT = sb("OnT", [P, L])

        (w_loaded, const_loaded, bias_set, zero_done, x_biased) = sem(
            "w_loaded", "const_loaded", "bias_set", "zero_done", "x_biased")
        (proj_ready, proj_taken, q_high, k_high, k_low, k_copies, q_done, k_done) = sem(
            "proj_ready", "proj_taken", "q_high", "k_high", "k_low", "k_copies", "q_done", "k_done")
        (score_ready, max_taken, max_joined, max_high, aux_in, aux_ready, aux_taken) = sem(
            "score_ready", "max_taken", "max_joined", "max_high", "aux_in", "aux_ready", "aux_taken")
        (tscore_ready, exp_done, pv_done, u_taken) = sem("tscore_ready", "exp_done", "pv_done", "u_taken")
        (ut_ready, rden_done, on_done, ont_ready, ont_taken, y_ready, y_added) = sem(
            "ut_ready", "rden_done", "on_done", "ont_ready", "ont_taken", "y_ready", "y_added")
        (v_ready, v_taken, vp_done) = sem("v_ready", "v_taken", "vp_done")

        S_UNITS = TB * HG * QH
        T_UNITS = QH * TB * HG
        BLOCKS = QH * TB
        PER_BLOCK = S_UNITS // BLOCKS
        AHEAD = 3

        def score_units(k, now, later):
            m = PER_BLOCK * (k + AHEAD)
            ahead, m = 1 + m // S_UNITS, m % S_UNITS
            return [(ahead, m + i) for i in range(PER_BLOCK)] if (now, later)[ahead - 1] else []

        MISC = {1: ("K", 0), 2: ("K", 1), 3: ("Q", 0), 4: ("Q", 1), 5: ("T", 0), 6: ("T", 1),
                8: ("G", 0), 9: ("G", 1), 11: ("Y", 0), 12: ("Y", 1), 14: ("A", 0), 15: ("A", 1)}

        def misc(k, s, project, score, after):
            kind, h = MISC.get(k, (None, 0))
            ok = {"K": project, "Q": project, "A": score, "T": after, "G": after and s == 0,
                  "Y": after and s == 0}.get(kind, False)
            return (kind, h) if ok else None

        weights = ((Wq3[:], w["Wq3"]), (Wk3[:], w["Wk3"]), (bq3[:], w["bq3"]), (bk3[:], w["bk3"]),
                   (WvT[:], w["WvT"]), (WoT[:], w["WoT"]), (masks[:], c["masks"]),
                   (bvb[:], w["bv"].partition_broadcast(P)), (bob[:], w["bo"].partition_broadcast(P)))

        def load_all(sp, loaded):
            load(sp, loaded)
            for dst, src in weights:
                sp.dma_start(dst, src).then_inc(w_loaded, 16)
            sp.wait_ge(w_loaded, 16 * len(weights))

        def constants(block):
            @block.gpsimd
            def _(pool):
                for g in range(G):
                    pool.dma_start(K[g][AUX:NROW_T, :, :].rearrange("p h k -> p (h k)"), c["key_aux"][g])\
                        .then_inc(const_loaded, 16)
                count = [0]

                def alone(ins):
                    count[0] += 1
                    ins.then_inc(zero_done, 1)
                    pool.wait_ge(zero_done, count[0])

                alone(nc.gpsimd.memset(ones[AUX:P, :], 1.0))
                for g in range(G):
                    alone(nc.gpsimd.tensor_tensor(Q[g][AUX:P, :], ones[AUX:P, :], ones[AUX:P, :], ALU.mult))
                alone(nc.gpsimd.memset(Vp[:].rearrange("p t h c -> p (t h c)"), 0.0))
                alone(nc.gpsimd.memset(M2[:].rearrange("p t c -> p (t c)"), 0.0))
                alone(nc.gpsimd.memset(Vp[:, :, :, HD:HD + 1], 1.0))
                alone(nc.gpsimd.memset(M2[:, :, 0:2], 1.0))
                pool.wait_ge(const_loaded, 16 * G)

        layernorm_phase(nc, "ln0", X, XT, ident, load=load_all, side_job=constants, ident_in=ident_in)

        bankT = [ps(f"bankT{i}", [P, BANK]) for i in range(ROTATE)]
        bankS = [ps(f"bankS{i}", [P, BANK]) for i in range(ROTATE)]
        bankO = ps("bankO", [P, BANK])
        bankM = ps("bankM", [P, BANK])

        with nc.Block() as block:
            @block.tensor
            def _(pe):
                def project(n, g, b, kind, h):
                    W = (Wk3 if kind == "K" else Wq3)
                    tokens = XT[:, b * L + h * BANK:b * L + (h + 1) * BANK] if isinstance(b, int) else \
                        XT[:, ds(b * L + h * BANK, BANK)]
                    nc.tensor.matmul(bankM[0:AUX, :], W[:, g, :], tokens, start=True, stop=True)\
                        .then_inc(proj_ready, 1)

                def aux(n, h):
                    if h == 0:
                        pe.wait_ge(aux_in, n + 1)
                    for t in range(TH):
                        last = nc.tensor.matmul(bankM[AUX:P, t * P:(t + 1) * P], M2[:, h * TH + t, :], ident[:],
                                                start=True, stop=True)
                    last.then_inc(aux_ready, 1)

                def score_unit(n, g, m):
                    qt, j, kh = m // (HG * QH), m // QH % HG, m % QH
                    if m == 0:
                        pe.wait_ge(k_done, n + 1)
                        pe.wait_ge(q_done, n + 1)
                    if not (isinstance(n, int) and n == 0 and m < ROTATE):
                        pe.wait_ge(max_taken, S_UNITS * n + last_user(m, S_UNITS) + 1)
                    nc.tensor.matmul(bankS[m % ROTATE][:], Q[g][0:NROW_S, qt * P:(qt + 1) * P],
                                     K[g][0:NROW_S, j, kh * BANK:(kh + 1) * BANK],
                                     start=True, stop=True).then_inc(score_ready, 1)

                def tscore(n, g, k, j, first):
                    qh, kt, u = k // TB, k % TB, HG * k + j
                    if kt == 0 and j == 0:
                        pe.wait_ge(aux_taken, 2 * n + qh + 1)
                    if not (first and u < ROTATE):
                        pe.wait_ge(exp_done, T_UNITS * n + last_user(u, T_UNITS) + 1)
                    nc.tensor.matmul(bankT[u % ROTATE][:], K[g][0:NROW_T, j, kt * P:(kt + 1) * P],
                                     Q[g][0:NROW_T, qh * BANK:(qh + 1) * BANK], start=True, stop=True)\
                        .then_inc(tscore_ready, 1)

                def value_tiles(q):
                    if q:
                        pe.wait_ge(v_taken, q)
                    for t in range(TH):
                        i = q * TH + t
                        last = nc.tensor.matmul(bankO[:, t * D:(t + 1) * D], XT[:, i * P:(i + 1) * P], WvT[:],
                                                start=True, stop=True)
                    last.then_inc(v_ready, 1)

                def values(n, g, k, b):
                    qh, kt = k // TB, k % TB
                    if k == 0 and g == 0:
                        pe.wait_ge(vp_done, b + 1)
                    if kt == 0:
                        if isinstance(n, int) and n == 0 and qh == 0:
                            pe.wait_ge(v_taken, TILES // TH)
                        else:
                            pe.wait_ge(u_taken, 2 * n + qh)
                    pe.wait_ge(exp_done, HG * (BLOCKS * n + k + 1))
                    for j in range(HG):
                        last = nc.tensor.matmul(bankO[32 * j:32 * j + VW, :], Vp[:, kt, g * HG + j, :],
                                                E[:, k % 2, j, :], start=(kt == 0), stop=(kt == TB - 1))
                    last.then_inc(pv_done, 1)

                def transpose_u(n, h):
                    pe.wait_ge(u_taken, 2 * n + h + 1)
                    for t in range(TH):
                        last = nc.tensor.transpose(bankM[:, t * P:(t + 1) * P],
                                                   U[:, (h * TH + t) * P:(h * TH + t + 1) * P], ident[:])
                    last.then_inc(ut_ready, 1)

                def transpose_on(n, h):
                    if h == 0:
                        pe.wait_ge(on_done, 2 * n + 2)
                    for t in range(TH):
                        last = nc.tensor.transpose(bankM[:, t * P:(t + 1) * P], On[:, h * TH + t, :], ident[:])
                    last.then_inc(ont_ready, 1)

                def out_project(b, h):
                    if h == 0:
                        pe.wait_ge(ont_taken, 2 * b + 2)
                    for t in range(TH):
                        last = nc.tensor.matmul(bankM[:, t * D:(t + 1) * D],
                                                OnT[:, (h * TH + t) * P:(h * TH + t + 1) * P], WoT[:],
                                                start=True, stop=True)
                    last.then_inc(y_ready, 1)

                def step(b, s, project_next, score_next, after, first=False):
                    n = 4 * b + s
                    g2 = (s + 2) % 4
                    b2 = b + (s + 2) // 4
                    for k in range(BLOCKS):
                        units = score_units(k, score_next, project_next)
                        tscore(n, s, k, 0, first)
                        for j in range(HG):
                            if j:
                                tscore(n, s, k, j, first)
                            for ahead, m in units[j:j + 1]:
                                score_unit(n + ahead, (s + ahead) % 4, m)
                            if j == 1 and k > 0:
                                values(n, s, k - 1, b)
                            elif j == 1 and not first:
                                if s == 0:
                                    values(n - 1, 3, BLOCKS - 1, b - 1)
                                else:
                                    values(n - 1, s - 1, BLOCKS - 1, b)
                        unit = misc(k, s, project_next, score_next, after)
                        if unit:
                            kind, h = unit
                            pe.wait_ge(*free_at[0])
                            if kind in "KQ":
                                project(n + 2, g2, b2, kind, h)
                                free_at[0] = (proj_taken, 4 * (n + 2) + (2 if kind == "Q" else 0) + h + 1)
                            elif kind == "A":
                                aux(n + 1, h)
                                free_at[0] = (aux_taken, 2 * (n + 1) + h + 1)
                            elif kind == "T":
                                transpose_u(n - 1, h)
                                free_at[0] = (on_done, 2 * (n - 1) + h + 1)
                            elif kind == "G":
                                transpose_on(n - 1, h)
                                free_at[0] = (ont_taken, 2 * (b - 1) + h + 1)
                            else:
                                out_project(b - 1, h)
                                free_at[0] = (y_added, 2 * (b - 1) + h + 1)

                free_at = [None]

                for n in range(2):
                    for i, (kind, h) in enumerate((("K", 0), ("K", 1), ("Q", 0), ("Q", 1))):
                        if free_at[0]:
                            pe.wait_ge(*free_at[0])
                        project(n, n, 0, kind, h)
                        free_at[0] = (proj_taken, 4 * n + i + 1)
                for m in range(S_UNITS):
                    score_unit(0, 0, m)
                    if m % 8 == 7:
                        value_tiles(m // 8)
                for h in range(2):
                    pe.wait_ge(*free_at[0])
                    aux(0, h)
                    free_at[0] = (aux_taken, h + 1)
                for m in range(PER_BLOCK * AHEAD):
                    score_unit(1, 1, m)
                step(0, 0, True, True, False, first=True)
                with pe.Fori(0, B - 1) as b:
                    free_at[0] = (aux_taken, 8 * b + 4)
                    step(b, 1, True, True, True)
                    step(b, 2, True, True, True)
                    step(b, 3, True, True, True)
                    step(b + 1, 0, True, True, True)
                free_at[0] = (aux_taken, 2 * 13 + 2)
                step(B - 1, 1, True, True, True)
                step(B - 1, 2, False, True, True)
                step(B - 1, 3, False, False, True)
                n = 4 * B - 1
                values(n, 3, BLOCKS - 1, B - 1)
                for h in range(2):
                    pe.wait_ge(*free_at[0])
                    transpose_u(n, h)
                    free_at[0] = (on_done, 2 * n + h + 1)
                for h in range(2):
                    pe.wait_ge(*free_at[0])
                    transpose_on(n, h)
                    free_at[0] = (ont_taken, 2 * (B - 1) + h + 1)
                for h in range(2):
                    pe.wait_ge(*free_at[0])
                    out_project(B - 1, h)
                    free_at[0] = (y_added, 2 * (B - 1) + h + 1)

            @block.scalar
            def _(act):
                def take_projection(n, g, kind, h):
                    i = (2 if kind == "Q" else 0) + h
                    act.wait_ge(proj_ready, 4 * n + i + 1)
                    T, bias, scale = (Tk, bk3, 1.0) if kind == "K" else (Tq, bq3s, SCORE_SCALE)
                    if h == 0 and not (isinstance(n, int) and n == 0):
                        act.wait_ge(k_low if kind == "K" else q_done, n)
                    nc.scalar.activation(T[:, h * BANK:(h + 1) * BANK], bankM[0:AUX, :], ACT.Identity,
                                         bias=bias[:, g:g + 1], scale=scale).then_inc(proj_taken, 1)

                def take_aux(n, g, h):
                    act.wait_ge(aux_ready, 2 * n + h + 1)
                    nc.scalar.activation(Q[g][AUX:NROW_T, h * BANK:(h + 1) * BANK], bankM[AUX:NROW_T, :], ACT.Copy)\
                        .then_inc(aux_taken, 1)

                def exponential(n, k, j, first):
                    act.wait_ge(tscore_ready, HG * (BLOCKS * n + k) + j + 1)
                    if not (first and k < 2):
                        act.wait_ge(pv_done, BLOCKS * n + k - 1)
                    nc.scalar.activation(E[:, k % 2, j, :], bankT[(HG * k + j) % ROTATE][:], ACT.Exp).then_inc(exp_done, 1)

                def take_u(n, h):
                    act.wait_ge(pv_done, BLOCKS * n + TB * (h + 1))
                    nc.scalar.activation(U[:, h * BANK:(h + 1) * BANK], bankO[:], ACT.Copy).then_inc(u_taken, 1)

                def take_ont(b, h):
                    act.wait_ge(ont_ready, 2 * b + h + 1)
                    nc.scalar.activation(OnT[:, h * BANK:(h + 1) * BANK], bankM[:], ACT.Copy).then_inc(ont_taken, 1)

                def step(b, s, project_next, score_next, after, first=False):
                    n = 4 * b + s
                    for k in range(BLOCKS):
                        for j in range(HG):
                            exponential(n, k, j, first)
                        if k == 0 and not first:
                            take_u(n - 1, 1)
                        if k == TB:
                            take_u(n, 0)
                        unit = misc(k, s, project_next, score_next, after)
                        if unit:
                            kind, h = unit
                            if kind in "KQ":
                                take_projection(n + 2, (s + 2) % 4, kind, h)
                            elif kind == "A":
                                take_aux(n + 1, (s + 1) % 4, h)
                            elif kind == "G":
                                take_ont(b - 1, h)

                nc.scalar.mul(bq3s[:], bq3[:], SCORE_SCALE).then_inc(bias_set, 1)
                act.wait_ge(bias_set, 1)
                for n in range(2):
                    for kind in "KQ":
                        for h in range(2):
                            take_projection(n, n, kind, h)
                for q in range(TILES // TH):
                    act.wait_ge(v_ready, q + 1)
                    nc.scalar.activation(V[:, q * TH:(q + 1) * TH, :].rearrange("p t e -> p (t e)"), bankO[:],
                                         ACT.Copy).then_inc(v_taken, 1)
                for h in range(2):
                    take_aux(0, 0, h)
                step(0, 0, True, True, False, first=True)
                with act.Fori(0, B - 1) as b:
                    step(b, 1, True, True, True)
                    step(b, 2, True, True, True)
                    step(b, 3, True, True, True)
                    step(b + 1, 0, True, True, True)
                step(B - 1, 1, True, True, True)
                step(B - 1, 2, False, True, True)
                step(B - 1, 3, False, False, True)
                take_u(4 * B - 1, 1)
                for h in range(2):
                    take_ont(B - 1, h)

            @block.vector
            def _(dve):
                def high_part(n, g, kind):
                    static = isinstance(n, int)
                    dve.wait_ge(proj_taken, 4 * n + (4 if kind == "Q" else 2))
                    if kind == "K":
                        if not (static and n == 0):
                            dve.wait_ge(k_done, n)
                        nc.vector.tensor_copy(Kc[:].bitcast(F32R), Tk[:]).then_inc(k_high, 1)
                    else:
                        if not (static and n < 4):
                            dve.wait_ge(tscore_ready, HG * BLOCKS * (n - 3))
                        nc.vector.tensor_copy(Q[g][0:AUX, :], Tq[:]).then_inc(q_high, 1)

                def take_max(n, g, m):
                    dve.wait_ge(score_ready, S_UNITS * n + m + 1)
                    nc.vector.reduce_max(hmax[:, g % 2, m // QH, m % QH:m % QH + 1], bankS[m % ROTATE][:], AX.X)\
                        .then_inc(max_taken, 1)

                def split_max(n, g):
                    dve.wait_ge(max_taken, S_UNITS * (n + 1))
                    nc.vector.tensor_reduce(nmax[:].rearrange("p t j -> p (t j)"), hmax[:, g % 2], AX.X, ALU.max,
                                            negate=True).then_inc(max_joined, 1)
                    dve.wait_ge(max_joined, n + 1)
                    if not (isinstance(n, int) and n == 0):
                        dve.wait_ge(aux_ready, 2 * n)
                    nc.vector.tensor_copy(M2[:, :, 2:2 + HG].bitcast(F32R), nmax[:]).then_inc(max_high, 1)
                    dve.wait_ge(max_high, n + 1)
                    nc.vector.tensor_tensor(M2[:, :, 2 + HG:2 + 2 * HG], nmax[:], M2[:, :, 2:2 + HG],
                                            ALU.subtract).then_inc(aux_in, 1)

                def normalise(n, g, h):
                    dve.wait_ge(ut_ready, 2 * n + h + 1)
                    u = bankM[:].rearrange("p (tj c) -> p tj c", c=VW)
                    nc.vector.reciprocal(rden[:], u[:, :, HD]).then_inc(rden_done, 1)
                    dve.wait_ge(rden_done, 2 * n + h + 1)
                    out = On[:, h * TH:(h + 1) * TH, g * GE:(g + 1) * GE].rearrange("p t (j e) -> p t j e", e=HD)
                    nc.vector.tensor_tensor(out, u[:, :, 0:HD].rearrange("p (t j) e -> p t j e", t=TH),
                                            rden[:].rearrange("p (t j) -> p t j", t=TH).unsqueeze(3)
                                            .broadcast_to([P, TH, HG, HD]), ALU.mult).then_inc(on_done, 1)
                    dve.wait_ge(on_done, 2 * n + h + 1)

                def add_output(b, h):
                    dve.wait_ge(y_ready, 2 * b + h + 1)
                    dve.wait_ge(x_biased, TILES)
                    x = X[:, ds(b * TB + h * TH, TH), :]
                    nc.vector.tensor_tensor(x, bankM[:].rearrange("p (t e) -> p t e", t=TH), x, ALU.add)\
                        .then_inc(y_added, 1)

                def pad_values(b):
                    if isinstance(b, int) and b == 0:
                        dve.wait_ge(v_taken, TILES // TH)
                    else:
                        dve.wait_ge(pv_done, 4 * BLOCKS * b)
                    heads = lambda a: a.rearrange("p t (h e) -> p t h e", e=HD)
                    nc.vector.tensor_tensor(Vp[:, :, :, 0:HD], heads(V[:, ds(b * TB, TB), :]),
                                            heads(bvb[:].unsqueeze(1).broadcast_to([P, TB, D])), ALU.add)\
                        .then_inc(vp_done, 1)

                def step(b, s, project_next, score_next, after, first=False):
                    n = 4 * b + s
                    for k in range(BLOCKS):
                        units = score_units(k, score_next, project_next)
                        if k == 0 and s == 0 and not first:
                            for ahead, m in units[:1]:
                                take_max(n + ahead, (s + ahead) % 4, m)
                            units = units[1:]
                            pad_values(b)
                        for ahead, m in units:
                            take_max(n + ahead, (s + ahead) % 4, m)
                            if m == S_UNITS - 1:
                                split_max(n + 1, (s + 1) % 4)
                        if project_next and k == 3:
                            high_part(n + 2, (s + 2) % 4, "K")
                        if project_next and k == 5:
                            high_part(n + 2, (s + 2) % 4, "Q")
                        unit = misc(k, s, project_next, score_next, after)
                        if unit and unit[0] == "T":
                            normalise(n - 1, (s - 1) % 4, unit[1])
                        if unit and unit[0] == "Y":
                            add_output(b - 1, unit[1])

                for n in range(2):
                    high_part(n, n, "K")
                    high_part(n, n, "Q")
                for m in range(S_UNITS):
                    take_max(0, 0, m)
                split_max(0, 0)
                pad_values(0)
                for m in range(PER_BLOCK * AHEAD):
                    take_max(1, 1, m)
                step(0, 0, True, True, False, first=True)
                with dve.Fori(0, B - 1) as b:
                    step(b, 1, True, True, True)
                    step(b, 2, True, True, True)
                    step(b, 3, True, True, True)
                    step(b + 1, 0, True, True, True)
                step(B - 1, 1, True, True, True)
                step(B - 1, 2, False, True, True)
                step(B - 1, 3, False, False, True)
                for h in range(2):
                    normalise(4 * B - 1, 3, h)
                for h in range(2):
                    add_output(B - 1, h)

            @block.gpsimd
            def _(pool):
                def low_parts(n, g):
                    static = isinstance(n, int)
                    pool.wait_ge(k_high, n + 1)
                    nc.gpsimd.tensor_tensor(Kc[GE:2 * GE, :], Tk[GE:2 * GE, :], Kc[GE:2 * GE, :], ALU.subtract)\
                        .then_inc(k_low, 1)
                    pool.wait_ge(k_low, n + 1)
                    if not (static and n < 4):
                        pool.wait_ge(tscore_ready, HG * BLOCKS * (n - 3))
                    for j in range(HG):
                        last = nc.gpsimd.tensor_tensor(K[g][0:AUX, j, :], Kc[:], masks[:, j:j + 1].broadcast_to([AUX, L]),
                                                       ALU.mult)
                    last.then_inc(k_done, 1)
                    pool.wait_ge(k_done, n + 1)
                    pool.wait_ge(q_high, n + 1)
                    nc.gpsimd.tensor_tensor(Q[g][2 * GE:3 * GE, :], Tq[2 * GE:3 * GE, :],
                                            Q[g][2 * GE:3 * GE, :].bitcast(F32), ALU.subtract).then_inc(q_done, 1)

                low_parts(0, 0)
                low_parts(1, 1)
                pool.wait_ge(q_done, 2)
                for i in range(TILES):
                    nc.gpsimd.tensor_tensor(X[:, i, :], X[:, i, :], bob[:], ALU.add).then_inc(x_biased, 1)
                pool.wait_ge(x_biased, TILES)
                low_parts(2, 2)
                with pool.Fori(0, B - 1) as b:
                    low_parts(4 * b + 3, 3)
                    low_parts(4 * b + 4, 0)
                    low_parts(4 * b + 5, 1)
                    low_parts(4 * b + 6, 2)
                low_parts(15, 3)


def routing_phase(nc, phase, X, XT, XN, share, slots, expert_of, scratch, ident, c, w, W, first):
    with ExitStack() as ctx:
        sem = Sems(nc, ctx, "ln_" + phase)
        sb = lambda name, shape, dt=F32: ctx.enter_context(nc.sbuf_tensor(f"ln_{phase}_{name}", shape, dt))
        ps = lambda name: ctx.enter_context(nc.psum_tensor(f"ln_{phase}_{name}", [P, BANK], F32))
        stats = sb("stats", [P, TILES, 6])
        meanvar = sb("meanvar", [P, TILES, 2])
        std = sb("std", [P, TILES])
        rstd = sb("rstd", [P, TILES])
        eps = sb("eps", [P, 1])
        BANKS = 4
        banks = [ps(f"t{i}") for i in range(BANKS)]
        logits = [ps(f"logits{i}") for i in range(2)]
        before_bank, total_bank = ps("before"), ps("total")
        gateT = sb("gateT", [D, NE]); gbias = sb("gbias", [P, NE]); number = sb("number", [P, NE])
        earlier = sb("earlier", [P, P]); ones = sb("ones", [P, P])
        steps = sb("steps", [P, HALF])
        tile_number = sb("tile_number", [P, HALF_SLOTS])
        scores = sb("scores", [P, TILES, NE])
        top = sb("top", [P, TILES, 8])
        where = sb("where", [P, TILES, 8], mybir.dt.uint32)
        wheref = sb("wheref", [P, TILES, TOP])
        rsum = sb("rsum", [P, TILES])
        hit = sb("hit", [P, TOP, TILES, NE])
        hits = sb("hits", [P, TILES, NE])
        PAD = HALF // 2
        sums = [sb(f"sums{i}", [P, HALVES, PAD + HALF, NE]) for i in range(2)]
        rank = sb("rank", [P, TILES, NE])
        EPAD = 8
        ends = [sb(f"ends{i}", [P, HALVES, EPAD + NE]) for i in range(2)]
        filled = sb("filled", [P, HALVES, NE, HALF])
        tiles_of = sb("tiles_of", [P, HALVES, NE]); start = sb("start", [P, HALVES, NE])
        place = sb("place", [P, TOP, TILES, NE]); placef = sb("placef", [P, TILES, TOP])
        passed = sb("passed", [P, HALVES, HALF_SLOTS, NE - 1]); expertf = sb("expertf", [P, SLOT_TILES])
        zeros = sb("zeros", [P, BANK]) if first else None
        (eps_set, stats_done, aggregated, std_done, inverted, normed, transposed, evacuated) = sem(
            "eps_set", "stats_done", "aggregated", "std_done", "inverted", "normed", "transposed", "evacuated")
        (small_in, routed, biased, scored, found, chain, hits_done, counted, zeroed, cleared) = sem(
            "small_in", "routed", "biased", "scored", "found", "chain", "hits_done", "counted", "zeroed", "cleared")
        QB = TB // TH
        quads = lambda b: range(b * QB, (b + 1) * QB)
        small = ((gateT[:], w["gateT"]), (gbias[:], w["gbias"].partition_broadcast(P)),
                 (number[:], c["number"].partition_broadcast(P)), (earlier[:], c["earlier"]),
                 (steps[:], c["steps"].partition_broadcast(P)),
                 (tile_number[:], c["tile_number"].partition_broadcast(P)))

        with nc.Block() as block:
            @block.sync
            def _(sp):
                for dst, src in small:
                    sp.dma_start(dst, src).then_inc(small_in, 16)
                if first:
                    sp.wait_ge(zeroed, 1)
                    n = SLOT_TILES * P * D // P // BANK
                    for place in ("tokens", "results"):
                        sp.dma_start(scratch[place].rearrange("(p a) d -> p (a d)", p=P)
                                     .rearrange("p (n m) -> p n m", m=BANK),
                                     zeros[:].unsqueeze(1).broadcast_to([P, n, BANK])).then_inc(cleared, 16)
                    for name in ("w1", "w3", "w2"):
                        sp.dma_start(W[name][:], w[name + "T"]).then_inc(W["in"], 16)
                    sp.wait_ge(cleared, 32)

            @block.vector
            def _(dve):
                nc.vector.memset(eps[:], LN_EPS).then_inc(eps_set, 1)
                if first:
                    nc.vector.memset(zeros[:], 0.0).then_inc(zeroed, 1)
                nc.vector.memset(ones[:], 1.0)
                for i in range(2):
                    nc.vector.memset(sums[i][:, :, 0:PAD, :], 0.0)
                    nc.vector.memset(ends[i][:, :, 0:EPAD], 0.0)

                def statistics(b):
                    tiles = range(b * TB, (b + 1) * TB)
                    for i in tiles:
                        nc.vector.bn_stats(stats[:, i, :], X[:, i, :]).then_inc(stats_done, 1)
                    for i in tiles:
                        dve.wait_ge(stats_done, i + 1)
                        nc.vector.bn_aggr(meanvar[:, i, :], stats[:, i, :]).then_inc(aggregated, 1)

                def normalise(b):
                    dve.wait_ge(std_done, b + 1)
                    cols = slice(b * TB, (b + 1) * TB)
                    nc.vector.reciprocal(rstd[:, cols], std[:, cols]).then_inc(inverted, 1)
                    dve.wait_ge(inverted, b + 1)
                    for q in quads(b):
                        for i in range(q * TH, (q + 1) * TH):
                            last = nc.vector.tensor_scalar(XN[:, i, :], X[:, i, :], meanvar[:, i, 0:1],
                                                           rstd[:, i:i + 1], ALU.subtract, ALU.mult)
                        last.then_inc(normed, 1)

                def add_bias(b):
                    if b == 0:
                        dve.wait_ge(small_in, 16 * len(small))
                    dve.wait_ge(routed, b + 1)
                    nc.vector.tensor_tensor(scores[:, b * TB:(b + 1) * TB, :],
                                            logits[b % 2][:, 0:TB * NE].rearrange("p (t e) -> p t e", e=NE),
                                            gbias[:].unsqueeze(1).broadcast_to([P, TB, NE]), ALU.add)\
                        .then_inc(biased, 1)

                def choose(b):
                    dve.wait_ge(scored, b + 1)
                    for i in range(b * TB, (b + 1) * TB):
                        nc.vector.max(top[:, i, :], scores[:, i, :]).then_inc(found, 1)
                    dve.wait_ge(found, (2 * b + 1) * TB)
                    for i in range(b * TB, (b + 1) * TB):
                        nc.vector.max_index(where[:, i, :], top[:, i, :], scores[:, i, :]).then_inc(found, 1)

                count = [0]

                def link(ins):
                    count[0] += 1
                    ins.then_inc(chain, 1)
                    dve.wait_ge(chain, count[0])

                statistics(0)
                statistics(1)
                normalise(0)
                statistics(2)
                normalise(1)
                statistics(3)
                normalise(2)
                add_bias(0)
                normalise(3)
                add_bias(1)
                choose(0)
                add_bias(2)
                choose(1)
                add_bias(3)
                choose(2)
                choose(3)
                dve.wait_ge(found, 2 * TILES)
                link(nc.vector.tensor_copy(wheref[:], where[:, :, 0:TOP]))
                for k in range(TOP):
                    last = nc.vector.tensor_tensor(hit[:, k], wheref[:, :, k:k + 1].broadcast_to([P, TILES, NE]),
                                                   number[:].unsqueeze(1).broadcast_to([P, TILES, NE]), ALU.is_equal)
                link(last)
                nc.vector.tensor_tensor(hits[:], hit[:, 0], hit[:, 1], ALU.add).then_inc(hits_done, 1)

                link(nc.vector.tensor_tensor(rsum[:], top[:, :, 0], top[:, :, 1], ALU.add))
                link(nc.vector.tensor_scalar(rsum[:], rsum[:], ROUTE_EPS, None, ALU.add))
                link(nc.vector.reciprocal(rsum[:], rsum[:]))
                nc.vector.tensor_tensor(share[:], top[:, :, 0:TOP], rsum[:].unsqueeze(2)
                                        .broadcast_to([P, TILES, TOP]), ALU.mult)

                dve.wait_ge(counted, 2)
                totals = total_bank[:, 0:TILES * NE].rearrange("p (h t e) -> p h t e", h=HALVES, e=NE)
                link(nc.vector.tensor_copy(sums[0][:, :, PAD:, :], totals))
                i, reach = 0, 1
                while reach < HALF:
                    link(nc.vector.tensor_tensor(sums[1 - i][:, :, PAD:, :], sums[i][:, :, PAD:, :],
                                                 sums[i][:, :, PAD - reach:PAD + HALF - reach, :], ALU.add))
                    i, reach = 1 - i, 2 * reach
                upto = sums[i]
                rank_h = rank[:].rearrange("p (h t) e -> p h t e", h=HALVES)
                link(nc.vector.tensor_tensor(rank_h, upto[:, :, PAD:, :], totals, ALU.subtract))
                link(nc.vector.tensor_tensor(rank[:], rank[:], before_bank[:, 0:TILES * NE]
                                             .rearrange("p (t e) -> p t e", e=NE), ALU.add))
                for h in range(HALVES):
                    last = nc.vector.tensor_tensor(
                        filled[:, h], upto[:, h, PAD + HALF - 1, :].unsqueeze(2).broadcast_to([P, NE, HALF]),
                        steps[:].unsqueeze(1).broadcast_to([P, NE, HALF]), ALU.is_gt)
                link(last)
                link(nc.vector.reduce_sum(tiles_of[:], filled[:], AX.X))
                link(nc.vector.tensor_copy(ends[0][:, :, EPAD:], tiles_of[:]))
                i, reach = 0, 1
                while reach < NE:
                    link(nc.vector.tensor_tensor(ends[1 - i][:, :, EPAD:], ends[i][:, :, EPAD:],
                                                 ends[i][:, :, EPAD - reach:EPAD + NE - reach], ALU.add))
                    i, reach = 1 - i, 2 * reach
                end = ends[i]
                link(nc.vector.tensor_tensor(start[:], end[:, :, EPAD:], tiles_of[:], ALU.subtract))
                for h in range(HALVES):
                    last = nc.vector.tensor_scalar(start[:, h], start[:, h], float(h * HALF_SLOTS), float(P),
                                                   ALU.add, ALU.mult)
                link(last)
                for h in range(HALVES):
                    last = nc.vector.tensor_tensor(rank_h[:, h], rank_h[:, h],
                                                   start[:, h].unsqueeze(1).broadcast_to([P, HALF, NE]), ALU.add)
                link(last)
                for k in range(TOP):
                    last = nc.vector.tensor_tensor(place[:, k], hit[:, k], rank[:], ALU.mult)
                link(last)
                for k in range(TOP):
                    last = nc.vector.reduce_sum(placef[:, :, k], place[:, k], AX.X)
                link(last)
                nc.vector.tensor_copy(slots[:], placef[:])
                for h in range(HALVES):
                    last = nc.vector.tensor_tensor(
                        passed[:, h], end[:, h, EPAD:EPAD + NE - 1].unsqueeze(1)
                        .broadcast_to([P, HALF_SLOTS, NE - 1]),
                        tile_number[:].unsqueeze(2).broadcast_to([P, HALF_SLOTS, NE - 1]), ALU.is_le)
                link(last)
                link(nc.vector.reduce_sum(expertf[:], passed[:].rearrange("p h s e -> p (h s) e"), AX.X))
                nc.vector.tensor_copy(expert_of[:], expertf[:])

            @block.scalar
            def _(act):
                def deviations(b):
                    if b == 0:
                        act.wait_ge(eps_set, 1)
                    act.wait_ge(aggregated, TB * (b + 1))
                    nc.scalar.activation(std[:, b * TB:(b + 1) * TB], meanvar[:, b * TB:(b + 1) * TB, 1], ACT.Sqrt,
                                         bias=eps[:, 0:1]).then_inc(std_done, 1)

                def evacuate(b):
                    for q in quads(b):
                        act.wait_ge(transposed, q + 1)
                        nc.scalar.activation(XT[:, q * BANK:(q + 1) * BANK], banks[q % BANKS][:, :], ACT.Copy)\
                            .then_inc(evacuated, 1)

                def sigmoids(b):
                    act.wait_ge(biased, b + 1)
                    s = scores[:, b * TB:(b + 1) * TB, :].rearrange("p t e -> p (t e)")
                    nc.scalar.activation(s, s, ACT.Sigmoid).then_inc(scored, 1)

                deviations(0)
                deviations(1)
                evacuate(0)
                deviations(2)
                evacuate(1)
                deviations(3)
                evacuate(2)
                sigmoids(0)
                evacuate(3)
                sigmoids(1)
                sigmoids(2)
                sigmoids(3)

            @block.tensor
            def _(pe):
                def transposes(b):
                    for q in quads(b):
                        pe.wait_ge(normed, q + 1)
                        if q >= BANKS:
                            pe.wait_ge(evacuated, q - BANKS + 1)
                        for t in range(TH):
                            last = nc.tensor.transpose(banks[q % BANKS][:, t * P:(t + 1) * P],
                                                       XN[:, q * TH + t, :], ident[:, :])
                        last.then_inc(transposed, 1)

                def route(b):
                    if b == 0:
                        pe.wait_ge(small_in, 16 * len(small))
                    pe.wait_ge(evacuated, (b + 1) * QB)
                    if b >= 2:
                        pe.wait_ge(biased, b - 1)
                    for t in range(TB):
                        i = b * TB + t
                        last = nc.tensor.matmul(logits[b % 2][:, t * NE:(t + 1) * NE], XT[:, i * P:(i + 1) * P],
                                                gateT[:], start=True, stop=True)
                    last.then_inc(routed, 1)

                transposes(0)
                transposes(1)
                route(0)
                transposes(2)
                route(1)
                transposes(3)
                route(2)
                route(3)
                pe.wait_ge(hits_done, 1)
                for bank, lhs in ((before_bank, earlier), (total_bank, ones)):
                    nc.tensor.matmul(bank[:, 0:TILES * NE], lhs[:], hits[:].rearrange("p t e -> p (t e)"),
                                     start=True, stop=True).then_inc(counted, 1)


def expert_phase(nc, phase, X, XT, scratch, ident, c, w, W, first):
    with ExitStack() as ctx:
        sem = Sems(nc, ctx, phase)
        sb = lambda name, shape, dt=F32: ctx.enter_context(nc.sbuf_tensor(f"{phase}_{name}", shape, dt))
        share = sb("share", [P, TILES, TOP])
        slots = sb("slots", [P, TILES, TOP], mybir.dt.uint32)
        expert_of = sb("expert_of", [P, SLOT_TILES], mybir.dt.int32)
        XN = sb("XN", [P, TILES, D])
        routing_phase(nc, phase, X, XT, XN, share, slots, expert_of, scratch, ident, c, w, W, first)

        tokens, results = scratch["tokens"], scratch["results"]
        w1, w3, w2 = [W[n][:].rearrange("p (e m) -> p e m", e=NE) for n in ("w1", "w3", "w2")]
        PH = HT * P
        x = sb("x", [P, 2, TH, D])
        xT = sb("xT", [P, 2, BANK])
        gated = sb("gated", [P, 2, HID]); hidden = sb("hidden", [P, 2, PH])
        hT = sb("hT", [P, 2, PH])
        y = sb("y", [P, 2, TH, D])
        ps = lambda name: ctx.enter_context(nc.psum_tensor(f"{phase}_{name}", [P, BANK], F32))
        bankX, bankH = ps("bankX"), ps("bankH")
        bank1, bank3, bankY = [[ps(f"{n}{i}") for i in range(2)] for n in ("bank1", "bank3", "bankY")]
        (turned, x_ready, up_ready, silu_done, hidden_done, ht_ready, ht_taken, y_ready, y_taken, pad_set) = sem(
            "turned", "x_ready", "up_ready", "silu_done", "hidden_done", "ht_ready", "ht_taken", "y_ready",
            "y_taken", "pad_set")
        x_in, y_stored = sem("x_in0", "x_in1"), sem("y_stored0", "y_stored1")
        GROUPS = SLOT_TILES // TH
        STEP = 2 * TH
        STEPS = SLOT_TILES // STEP
        HALF_STEPS = STEPS // HALVES
        assert HALF_SLOTS % STEP == 0
        RING = 4
        pair = sb("pair", [P, RING, TOP, D])
        scattered = sem(*[f"scattered{h}" for h in range(HALVES)])
        gathered = sem(*[f"gathered{i}" for i in range(RING)])
        chain = sem(*[f"chain{h}" for h in range(HALVES)])
        added = sem(*[f"added{h}" for h in range(HALVES)])

        of_group = lambda a, g: a[ds(g * TH * P, TH * P), :].rearrange("(t p) d -> p t d", p=P)

        with nc.Block() as block:
            @block.sync
            def _(sp):
                def load(g, p, first=False):
                    if not first:
                        sp.wait_ge(turned, g - 1)
                    sp.dma_start(x[:, p], of_group(tokens, g)).then_inc(x_in[p], 16)

                sp.wait_ge(scattered[0], 16 * HALF * TOP)
                load(0, 0, True)
                load(1, 1, True)
                with sp.Fori(1, HALF_STEPS) as i:
                    load(2 * i, 0)
                    load(2 * i + 1, 1)
                for h in range(1, HALVES):
                    sp.wait_ge(scattered[h], 16 * HALF * TOP)
                    with sp.Fori(h * HALF_STEPS, (h + 1) * HALF_STEPS) as i:
                        load(2 * i, 0)
                        load(2 * i + 1, 1)

            @block.tensor
            def _(pe):
                load_expert = lambda j: pe.value_load(expert_of[0:1, ds(j, 1)], min_val=0, max_val=NE - 1)
                experts = [None] * STEP

                def turn(i, p, first=False):
                    g = 2 * i + p
                    pe.wait_ge(x_in[p], 16 * i + 16)
                    if not (first and g == 0):
                        pe.wait_ge(x_ready, g)
                    for t in range(TH):
                        last = nc.tensor.transpose(bankX[:, t * P:(t + 1) * P], x[:, p, t, :], ident[:])
                    last.then_inc(turned, 1)

                def up(i, k, first=False):
                    j, p = STEP * i + k, k // TH
                    if k % TH == 0:
                        pe.wait_ge(x_ready, 2 * i + p + 1)
                    if not (first and k < 2):
                        pe.wait_ge(hidden_done, j - 1)
                    e = experts[k] = load_expert(j)
                    for bank, W13 in ((bank1[k % 2], w1), (bank3[k % 2], w3)):
                        last = nc.tensor.matmul(bank[:, 0:HID], xT[:, p, (k % TH) * P:(k % TH + 1) * P],
                                                W13[:, ds(e, 1), :], start=True, stop=True)
                    last.then_inc(up_ready, 1)

                def turn_hidden(j, k, first=False):
                    pe.wait_ge(hidden_done, j + 1)
                    if not (first and k == 0):
                        pe.wait_ge(ht_taken, j)
                    for t in range(HT):
                        last = nc.tensor.transpose(bankH[:, t * P:(t + 1) * P], hidden[:, k % 2, t * P:(t + 1) * P],
                                                   ident[:])
                    last.then_inc(ht_ready, 1)

                def down(j, g, k, e, first=False):
                    pe.wait_ge(ht_taken, j + 1)
                    if k % TH == 0 and not first:
                        pe.wait_ge(y_taken, g - 1)
                    w2e = w2[:, ds(e, 1), :].rearrange("p e m -> p (e m)")
                    for t in range(HT):
                        last = nc.tensor.matmul(bankY[k // TH][:, (k % TH) * P:(k % TH + 1) * P],
                                                hT[:, k % 2, t * P:(t + 1) * P], w2e[:, t * D:(t + 1) * D],
                                                start=(t == 0), stop=(t == HT - 1))
                    last.then_inc(y_ready, 1)

                def step(i, first=False, final=False):
                    for k in range(STEP):
                        j = STEP * i + k
                        up(i, k, first)
                        if k or not first:
                            turn_hidden(j - 1, (k - 1) % STEP, first)
                        if k >= 2:
                            down(j - 2, 2 * i + (k - 2) // TH, k - 2, experts[k - 2], first)
                        elif not first:
                            down(j - 2, 2 * i - 1, STEP + k - 2, load_expert(j - 2))
                        if k == 1:
                            turn(i, 1, first)
                        if k == TH + 1 and not final:
                            turn(i + 1, 0)

                if first:
                    pe.wait_ge(W["in"], 48)
                turn(0, 0, True)
                step(0, first=True)
                with pe.Fori(1, STEPS - 1) as i:
                    step(i)
                step(STEPS - 1, final=True)
                turn_hidden(SLOT_TILES - 1, STEP - 1)
                down(SLOT_TILES - 2, GROUPS - 1, STEP - 2, experts[STEP - 2])
                down(SLOT_TILES - 1, GROUPS - 1, STEP - 1, experts[STEP - 1])

            @block.scalar
            def _(act):
                def take_tokens(g, p, first=False):
                    act.wait_ge(turned, g + 1)
                    if not first:
                        act.wait_ge(up_ready, TH * (g - 1))
                    nc.scalar.copy(xT[:, p, :], bankX[:]).then_inc(x_ready, 1)

                def silu(j, k, first=False):
                    act.wait_ge(up_ready, j + 1)
                    if not (first and k < 2):
                        act.wait_ge(hidden_done, j - 1)
                    nc.scalar.activation(gated[:, k % 2, :], bank1[k % 2][:, 0:HID], ACT.Silu).then_inc(silu_done, 1)

                def take_hidden(j, k, first=False):
                    act.wait_ge(ht_ready, j + 1)
                    if not (first and k < 2):
                        act.wait_ge(y_ready, j - 1)
                    nc.scalar.copy(hT[:, k % 2, :], bankH[:, 0:PH]).then_inc(ht_taken, 1)

                def store(g, p):
                    act.wait_ge(y_taken, g + 1)
                    act.dma_start(of_group(results, g), y[:, p]).then_inc(y_stored[p], 16)

                def step(i, first=False, final=False):
                    for k in range(STEP):
                        j = STEP * i + k
                        silu(j, k, first)
                        if k == TH - 1 and not first:
                            store(2 * i - 1, 1)
                        if k == STEP - 1:
                            store(2 * i, 0)
                        if k or not first:
                            take_hidden(j - 1, (k - 1) % STEP, first)
                        if k == 1:
                            take_tokens(2 * i + 1, 1, first)
                        if k == TH + 1 and not final:
                            take_tokens(2 * i + 2, 0)

                take_tokens(0, 0, True)
                step(0, first=True)
                with act.Fori(1, STEPS - 1) as i:
                    step(i)
                step(STEPS - 1, final=True)
                take_hidden(SLOT_TILES - 1, STEP - 1)
                store(GROUPS - 1, 1)

            @block.vector
            def _(dve):
                def multiply(j, k, first=False):
                    dve.wait_ge(silu_done, j + 1)
                    if not (first and k < 2):
                        dve.wait_ge(ht_ready, j - 1)
                    nc.vector.tensor_tensor(hidden[:, k % 2, 0:HID], bank3[k % 2][:, 0:HID], gated[:, k % 2, :],
                                            ALU.mult).then_inc(hidden_done, 1)

                def take_results(i, p, first=False):
                    dve.wait_ge(y_ready, TH * (2 * i + p) + TH)
                    if not first:
                        dve.wait_ge(y_stored[p], 16 * i)
                    nc.vector.tensor_copy(y[:, p].rearrange("p t d -> p (t d)"), bankY[p][:]).then_inc(y_taken, 1)

                def step(i, first=False):
                    for k in range(STEP):
                        multiply(STEP * i + k, k, first)
                        if k == TH + 2:
                            take_results(i, 0, first)
                        if k == 2 and not first:
                            take_results(i - 1, 1, isinstance(i, int) and i == 1)

                for k in range(2):
                    last = nc.vector.memset(hidden[:, k, HID:PH], 0.0)
                step(0, first=True)
                step(1)
                with dve.Fori(2, STEPS) as i:
                    step(i)
                take_results(STEPS - 1, 1)

                for t in range(HALF, TILES):
                    dve.wait_ge(gathered[t % RING], 16 * TOP * (t // RING + 1))
                    for k in range(TOP):
                        if k:
                            dve.wait_ge(chain[1], t - HALF + 1)
                        nc.vector.scalar_tensor_tensor(out=X[:, t, :], in0=pair[:, t % RING, k, :],
                                                       scalar=share[:, t, k:k + 1], in1=X[:, t, :],
                                                       op0=ALU.mult, op1=ALU.add).then_inc(
                            added[1] if k else chain[1], 1)

            @block.gpsimd
            def _(pool):
                for h in range(HALVES):
                    for t in range(h * HALF, (h + 1) * HALF):
                        for k in range(TOP):
                            pool.indirect_dma_start(tokens[:, :], bass.IndirectOffsetOnAxis(slots[:, t, k:k + 1], 0),
                                                    XN[:, t, :], None).then_inc(scattered[h], 16)

                def gather(t):
                    if t >= RING:
                        pool.wait_ge(added[(t - RING) // HALF], (t - RING) % HALF + 1)
                    for k in range(TOP):
                        pool.indirect_dma_start(pair[:, t % RING, k, :], None, results[:, :],
                                                bass.IndirectOffsetOnAxis(slots[:, t, k:k + 1], 0))\
                            .then_inc(gathered[t % RING], 16)

                def add(t):
                    rows = pair[:, t % RING]
                    pool.wait_ge(gathered[t % RING], 16 * TOP * (t // RING + 1))
                    nc.gpsimd.tensor_tensor(rows, rows, share[:, t, :].unsqueeze(2).broadcast_to([P, TOP, D]),
                                            ALU.mult).then_inc(chain[0], 1)
                    pool.wait_ge(chain[0], 2 * t + 1)
                    nc.gpsimd.tensor_tensor(rows[:, 0, :], rows[:, 0, :], rows[:, 1, :], ALU.add)\
                        .then_inc(chain[0], 1)
                    pool.wait_ge(chain[0], 2 * t + 2)
                    nc.gpsimd.tensor_tensor(X[:, t, :], X[:, t, :], rows[:, 0, :], ALU.add).then_inc(added[0], 1)

                def half_stored(h):
                    for p in range(2):
                        pool.wait_ge(y_stored[p], 16 * HALF_STEPS * (h + 1))

                half_stored(0)
                for t in range(HALF):
                    gather(t)
                    if t >= RING - 1:
                        add(t - RING + 1)
                for t in range(HALF - RING + 1, HALF):
                    add(t)
                half_stored(1)
                for t in range(HALF, TILES):
                    gather(t)


def decay_phase(nc, X, XT, ident, c, w):
    layernorm_phase(nc, "ln2", X, XT, ident)
    R = B * P
    with ExitStack() as ctx:
        sem = Sems(nc, ctx, "decay")
        sb = lambda name, shape, dt=F32: ctx.enter_context(nc.sbuf_tensor(f"decay_{name}", shape, dt))
        ps = lambda name: ctx.enter_context(nc.psum_tensor(f"decay_{name}", [P, BANK], F32))
        WqT = sb("WqT", [D, D]); WkT = sb("WkT", [D, D]); WvT = sb("WvT", [D, D]); WoT = sb("WoT", [D, D])
        masks = sb("masks", [P, HG])
        same = sb("same", [P, D])
        lag = sb("lag", [P, P])
        causal = sb("causal", [P, P])
        ahead = sb("ahead", [P, P])
        behind = sb("behind", [P, 1])
        lgr = sb("lgr", [P, H]); lgc = sb("lgc", [P, 1])
        tr = sb("tr", [P, 2, H]); tc = sb("tc", [P, 2])
        eps = sb("eps", [P, 1])
        Dm = sb("Dm", [P, HG, G, P])
        Gq = sb("Gq", [P, P])
        Gk = sb("Gk", [P, H])
        Gs = sb("Gs", [P, 1])
        XTc = sb("XTc", [D, 2, R])
        qT = sb("qT", [P, R]); qg = sb("qg", [P, 2, R])
        qm = sb("qm", [P, 2, G, R])
        kraw = sb("kraw", [P, R]); kc = sb("kc", [P, R]); ksq = sb("ksq", [P, R])
        kmean = sb("kmean", [P, B * H]); kstd = sb("kstd", [P, B * H])
        kn = sb("kn", [P, R]); kg = sb("kg", [P, 2, R]); v = sb("v", [P, 2, R])
        km = sb("km", [P, 2, HG, R])
        Am = sb("Am", [P, 2, G, P])
        S = sb("S", [P, 2, R]); Sadd = sb("Sadd", [P, R])
        vj = sb("vj", [P, 2, HG, R])
        yT = sb("yT", [P, R])
        bankA = [ps("bankA0"), ps("bankA1")]
        bankY, bankS, bankQ, bankK, bankV, bankT = [ps(n) for n in ("bankY", "bankS", "bankQ", "bankK", "bankV", "bankT")]
        (loaded, act_setup, dve_setup, chain) = sem("loaded", "act_setup", "dve_setup", "chain")
        (x_in, q_ready, k_ready, v_ready, q_taken, k_taken, v_taken, qg_done) = sem(
            "x_in", "q_ready", "k_ready", "v_ready", "q_taken", "k_taken", "v_taken", "qg_done")
        (ksum_done, kmean_done, kc_done, ksq_done, kvar_done, kstd_done, krstd_done, kn_done, kg_done) = sem(
            "ksum_done", "kmean_done", "kc_done", "ksq_done", "kvar_done", "kstd_done", "krstd_done", "kn_done",
            "kg_done")
        (kt_ready, km_done, a_ready, am_done, am_used, s_ready, sadd_done, s_done, y_taken) = sem(
            "kt_ready", "km_done", "a_ready", "am_done", "am_used", "s_ready", "sadd_done", "s_done",
            "y_taken")
        (o_ready, o_added) = sem("o_ready", "o_added")
        XTv = XT[:].rearrange("d (b c t) -> d b c t", b=B, c=TB)
        Xv = X[:].rearrange("p (b c) e -> p b c e", b=B)
        heads = lambda a: a.rearrange("p (n e) -> p n e", e=HD)

        with nc.Block() as block:
            loads = ((WqT[:], w["b_WqT"]), (WkT[:], w["b_WkT"]), (WvT[:], w["b_WvT"]), (WoT[:], w["b_WoT"]),
                     (masks[:], c["masks_b"]), (same[:], c["same_head"]), (lag[:], c["lag"]),
                     (causal[:], c["causal"]), (ahead[:], c["ahead"]), (behind[:], c["behind"]),
                     (lgr[:], w["log_gamma"].partition_broadcast(P)), (lgc[:], w["log_gamma_rows"]))

            @block.sync
            def _(sp):
                for dst, src in loads:
                    sp.dma_start(dst, src).then_inc(loaded, 16)

            @block.vector
            def _(dve):
                dve.wait_ge(loaded, 16 * len(loads))
                for i, (x, t) in enumerate(((lgr[:], (tr[:, 0, :], tr[:, 1, :])), (lgc[:], (tc[:, 0:1], tc[:, 1:2])))):
                    nc.vector.tensor_scalar(t[1], x, 0.0, None, ALU.min)
                    nc.vector.tensor_scalar(t[0], x, 0.0, None, ALU.max).then_inc(chain, 1)
                    dve.wait_ge(chain, 2 * i + 1)
                    nc.vector.tensor_tensor(t[0], t[1], t[0], ALU.subtract).then_inc(chain, 1)
                    dve.wait_ge(chain, 2 * i + 2)
                nc.vector.memset(eps[:], LN_EPS)
                nc.vector.memset(vj[:], 0.0)
                nc.vector.memset(qm[:], 0.0)
                nc.vector.memset(S[:, 0, :], 0.0).then_inc(dve_setup, 1)
                dve.wait_ge(act_setup, 2)
                nc.vector.tensor_tensor(lgr[:], tr[:, 1, :], tr[:, 0, :], ALU.subtract)
                nc.vector.tensor_tensor(lgc[:], tc[:, 1:2], tc[:, 0:1], ALU.subtract).then_inc(dve_setup, 1)
                dve.wait_ge(act_setup, 5)
                Dh = Dm[:].rearrange("p j g t -> p (j g) t")
                nc.vector.tensor_tensor(Dh, Dh, causal[:].unsqueeze(1).broadcast_to([P, H, P]), ALU.mult)

            @block.scalar
            def _(act):
                act.wait_ge(dve_setup, 1)
                nc.scalar.activation(tr[:, 0, :], tr[:, 0, :], ACT.Exp).then_inc(chain, 1)
                nc.scalar.activation(tc[:, 0:1], tc[:, 0:1], ACT.Exp).then_inc(chain, 1)
                act.wait_ge(chain, 6)
                nc.scalar.activation(tr[:, 0, :], tr[:, 0, :], ACT.Ln, bias=1.0).then_inc(act_setup, 1)
                nc.scalar.activation(tc[:, 0:1], tc[:, 0:1], ACT.Ln, bias=1.0).then_inc(act_setup, 1)
                act.wait_ge(dve_setup, 2)
                nc.scalar.activation(Gq[:], ahead[:], ACT.Exp, scale=lgc[:, 0:1]).then_inc(act_setup, 1)
                nc.scalar.activation(Gs[:], lgc[:], ACT.Exp, scale=float(P))
                nc.scalar.activation(Gk[:], lgr[:], ACT.Exp, scale=behind[:, 0:1]).then_inc(act_setup, 1)
                for h in range(H):
                    last = nc.scalar.activation(Dm[:, h % HG, h // HG, :], lag[:], ACT.Exp, scale=lgr[:, h:h + 1])
                last.then_inc(act_setup, 1)

        with nc.Block() as block:
            def steps(eng, prepare, work):
                prepare(0, 0)
                work(0, 0)
                with eng.Fori(0, (TB - 2) // 2) as i:
                    work(2 * i + 1, 1)
                    work(2 * i + 2, 0)
                work(TB - 1, 1)

            static = lambda n, below: isinstance(n, int) and n < below
            final = lambda n: isinstance(n, int) and n == TB - 1
            UNITS = B * HG

            @block.tensor
            def _(pe):
                def project(n, p):
                    pe.wait_ge(x_in, n + 1)
                    for bank, W, ready, free in ((bankK, WkT, k_ready, k_taken), (bankV, WvT, v_ready, v_taken)):
                        if not static(n, 1):
                            pe.wait_ge(free, n)
                        for b in range(B):
                            last = nc.tensor.matmul(bank[:, b * P:(b + 1) * P], XTc[:, p, b * P:(b + 1) * P], W[:],
                                                    start=True, stop=True)
                        last.then_inc(ready, 1)
                    if not static(n, 1):
                        pe.wait_ge(q_taken, n)
                    nc.tensor.matmul(bankQ[:], WqT[:], XTc[:, p, :], start=True, stop=True).then_inc(q_ready, 1)

                def transpose_keys(n, p):
                    pe.wait_ge(kn_done, n + 1)
                    if not static(n, 1):
                        pe.wait_ge(km_done, n)
                        if not static(n, 2):
                            pe.wait_ge(o_added, n - 1)
                    for b in range(B):
                        last = nc.tensor.transpose(bankT[:, b * P:(b + 1) * P], kn[:, b * P:(b + 1) * P], ident[:])
                    last.then_inc(kt_ready, 1)

                def scores(n, p, u):
                    b, j = u // HG, u % HG
                    if u == 0:
                        pe.wait_ge(km_done, n + 1)
                        pe.wait_ge(q_taken, n + 1)
                    if not (static(n, 1) and u < 2):
                        pe.wait_ge(am_done, UNITS * n + u - 1)
                    nc.tensor.matmul(bankA[u % 2][:], km[:, p, j, b * P:(b + 1) * P], qm[:, p, :, b * P:(b + 1) * P],
                                     start=True, stop=True).then_inc(a_ready, 1)

                def past(n, p, b):
                    if b == 0:
                        pe.wait_ge(qg_done, n + 1)
                        if not static(n, 1):
                            pe.wait_ge(s_done, n)
                            pe.wait_ge(y_taken, n)
                    nc.tensor.matmul(bankY[:, b * P:(b + 1) * P], S[:, p, b * P:(b + 1) * P],
                                     qg[:, p, b * P:(b + 1) * P], start=True, stop=False)

                def within(n, p, u):
                    b, j = u // HG, u % HG
                    if u == 0:
                        pe.wait_ge(v_taken, n + 1)
                    pe.wait_ge(am_done, UNITS * n + u + 1)
                    for g in range(G):
                        rows = slice(g * GE, (g + 1) * GE)
                        last = nc.tensor.matmul(bankY[rows, b * P:(b + 1) * P],
                                                vj[:, p, j, b * P + g * GE:b * P + (g + 1) * GE], Am[:, u % 2, g, :],
                                                start=False, stop=(j == HG - 1), tile_position=(0, g * GE))
                    last.then_inc(am_used, 1)

                def state(n, p):
                    pe.wait_ge(kg_done, n + 1)
                    if not static(n, 1):
                        pe.wait_ge(sadd_done, n)
                    for b in range(B):
                        cols = slice(b * P, (b + 1) * P)
                        last = nc.tensor.matmul(bankS[:, cols], kg[:, p, cols], v[:, p, cols], start=True, stop=True)
                    last.then_inc(s_ready, 1)

                def project_output(n):
                    pe.wait_ge(y_taken, n + 1)
                    for b in range(B):
                        last = nc.tensor.matmul(bankT[:, b * P:(b + 1) * P], yT[:, b * P:(b + 1) * P], WoT[:],
                                                start=True, stop=True)
                    last.then_inc(o_ready, 1)

                def work(n, p):
                    scores(n, p, 0)
                    for u in range(UNITS):
                        if u + 1 < UNITS:
                            scores(n, p, u + 1)
                        if u % HG == 0:
                            past(n, p, u // HG)
                        within(n, p, u)
                        if u == 3 and not static(n, 1):
                            project_output(n - 1)
                        if not final(n):
                            if u == 1:
                                project(n + 1, 1 - p)
                            if u == 13:
                                transpose_keys(n + 1, 1 - p)
                        if u == 5:
                            state(n, p)

                def prepare(n, p):
                    project(n, p)
                    transpose_keys(n, p)

                steps(pe, prepare, work)
                project_output(TB - 1)

            @block.scalar
            def _(act):
                def take_projections(n, p):
                    act.wait_ge(k_ready, n + 1)
                    if not static(n, 1):
                        act.wait_ge(kc_done, n)
                        act.wait_ge(ksum_done, n)
                    nc.scalar.copy(kraw[:], bankK[:]).then_inc(k_taken, 1)
                    act.wait_ge(v_ready, n + 1)
                    nc.scalar.copy(v[:, p, :], bankV[:])
                    by_head = lambda a, j: a.rearrange("p (n j e) -> p n j e", j=HG, e=HD)[:, :, j, :]
                    for j in range(HG):
                        last = nc.scalar.copy(by_head(vj[:, p, j, :], j), by_head(bankV[:], j))
                    last.then_inc(v_taken, 1)
                    act.wait_ge(q_ready, n + 1)
                    if not static(n, 1):
                        act.wait_ge(qg_done, n)
                    nc.scalar.copy(qT[:], bankQ[:])
                    for g in range(G):
                        rows = slice(g * GE, (g + 1) * GE)
                        last = nc.scalar.copy(qm[rows, p, g, :], bankQ[rows, :])
                    last.then_inc(q_taken, 1)

                def deviations(n, p):
                    act.wait_ge(kvar_done, n + 1)
                    nc.scalar.activation(kstd[:], kstd[:], ACT.Sqrt, scale=1.0 / HD, bias=eps[:, 0:1])\
                        .then_inc(kstd_done, 1)

                def mask_keys(n, p):
                    act.wait_ge(kt_ready, n + 1)
                    for j in range(HG):
                        last = nc.scalar.activation(km[:, p, j, :], bankT[:], ACT.Copy, scale=masks[:, j:j + 1])
                    last.then_inc(km_done, 1)

                def take_y(n):
                    act.wait_ge(am_used, UNITS * (n + 1))
                    if not static(n, 1):
                        act.wait_ge(o_ready, n)
                    nc.scalar.copy(yT[:], bankY[:]).then_inc(y_taken, 1)

                def prepare(n, p):
                    take_projections(n, p)
                    deviations(n, p)
                    mask_keys(n, p)

                def work(n, p):
                    if not final(n):
                        prepare(n + 1, 1 - p)
                    take_y(n)

                steps(act, prepare, work)

            @block.vector
            def _(dve):
                def take_tokens(n, p):
                    if not static(n, 2):
                        dve.wait_ge(q_ready, n - 1)
                    nc.vector.tensor_copy(XTc[:, p, :].rearrange("d (b t) -> d b t", b=B),
                                          XTv[:, :, ds(n, 1), :].rearrange("d b c t -> d b (c t)")).then_inc(x_in, 1)

                def key_means(n):
                    dve.wait_ge(k_taken, n + 1)
                    if not static(n, 1):
                        dve.wait_ge(kc_done, n)
                    nc.vector.reduce_sum(kmean[:], heads(kraw[:]), AX.X).then_inc(ksum_done, 1)
                    dve.wait_ge(ksum_done, n + 1)
                    nc.vector.tensor_scalar(kmean[:], kmean[:], 1.0 / HD, None, ALU.mult).then_inc(kmean_done, 1)

                def key_squares(n):
                    dve.wait_ge(ksq_done, n + 1)
                    nc.vector.reduce_sum(kstd[:], heads(ksq[:]), AX.X).then_inc(kvar_done, 1)

                def key_inverses(n):
                    dve.wait_ge(kstd_done, n + 1)
                    nc.vector.reciprocal(kstd[:], kstd[:]).then_inc(krstd_done, 1)

                def decay(n, u):
                    dve.wait_ge(a_ready, UNITS * n + u + 1)
                    if not (static(n, 1) and u < 2):
                        dve.wait_ge(am_used, UNITS * n + u - 1)
                    nc.vector.tensor_tensor(Am[:, u % 2].rearrange("p g t -> p (g t)"), bankA[u % 2][:],
                                            Dm[:, u % HG].rearrange("p g t -> p (g t)"),
                                            ALU.mult).then_inc(am_done, 1)

                def next_state(n, p):
                    dve.wait_ge(s_ready, n + 1)
                    nc.vector.tensor_tensor(Sadd[:].rearrange("p (b e) -> p b e", b=B),
                                            bankS[:].rearrange("p (b e) -> p b e", b=B),
                                            same[:].unsqueeze(1).broadcast_to([P, B, D]), ALU.mult)\
                        .then_inc(sadd_done, 1)
                    dve.wait_ge(sadd_done, n + 1)
                    if not static(n, 1):
                        dve.wait_ge(am_used, UNITS * n)
                    nc.vector.scalar_tensor_tensor(out=S[:, 1 - p, :], in0=S[:, p, :], scalar=Gs[:, 0:1],
                                                   in1=Sadd[:], op0=ALU.mult, op1=ALU.add).then_inc(s_done, 1)

                def add_output(n):
                    dve.wait_ge(o_ready, n + 1)
                    x = Xv[:, :, ds(n, 1), :].rearrange("p b c e -> p b (c e)")
                    nc.vector.tensor_tensor(x, bankT[:].rearrange("p (b e) -> p b e", b=B), x, ALU.add)\
                        .then_inc(o_added, 1)

                def prepare(n, p):
                    take_tokens(n, p)
                    key_means(n)
                    key_squares(n)
                    key_inverses(n)

                def work(n, p):
                    if not final(n):
                        take_tokens(n + 1, 1 - p)
                    for u in range(UNITS):
                        decay(n, u)
                        if not final(n):
                            if u == 4:
                                key_means(n + 1)
                            if u == 8:
                                key_squares(n + 1)
                            if u == 10:
                                key_inverses(n + 1)
                        if u == 5 and not static(n, 1):
                            add_output(n - 1)
                        if u == 7:
                            next_state(n, p)

                steps(dve, prepare, work)
                add_output(TB - 1)

            @block.gpsimd
            def _(pool):
                def prepare(n, p):
                    pool.wait_ge(kmean_done, n + 1)
                    spread = lambda a: a.unsqueeze(2).broadcast_to([P, B * H, HD])
                    if not static(n, 1):
                        pool.wait_ge(kvar_done, n)
                    nc.gpsimd.tensor_tensor(heads(kc[:]), heads(kraw[:]), spread(kmean[:]), ALU.subtract)\
                        .then_inc(kc_done, 1)
                    pool.wait_ge(kc_done, n + 1)
                    nc.gpsimd.tensor_tensor(ksq[:], kc[:], kc[:], ALU.mult).then_inc(ksq_done, 1)
                    pool.wait_ge(q_taken, n + 1)
                    if not static(n, 2):
                        pool.wait_ge(am_used, UNITS * (n - 1))
                        pool.wait_ge(s_ready, n - 1)
                    nc.gpsimd.tensor_tensor(qg[:, p, :].rearrange("p (b t) -> p b t", b=B),
                                            qT[:].rearrange("p (b t) -> p b t", b=B),
                                            Gq[:].unsqueeze(1).broadcast_to([P, B, P]), ALU.mult).then_inc(qg_done, 1)
                    pool.wait_ge(krstd_done, n + 1)
                    if not static(n, 1):
                        pool.wait_ge(kt_ready, n)
                    nc.gpsimd.tensor_tensor(heads(kn[:]), heads(kc[:]), spread(kstd[:]), ALU.mult).then_inc(kn_done, 1)
                    pool.wait_ge(kn_done, n + 1)
                    nc.gpsimd.tensor_tensor(kg[:, p, :].rearrange("p (b h e) -> p b h e", b=B, h=H),
                                            kn[:].rearrange("p (b h e) -> p b h e", b=B, h=H),
                                            Gk[:].unsqueeze(1).unsqueeze(3).broadcast_to([P, B, H, HD]),
                                            ALU.mult).then_inc(kg_done, 1)

                steps(pool, prepare, lambda n, p: None if final(n) else prepare(n + 1, 1 - p))


def build_program(nc, x, c, w, out, stop=None):
    nc.disable_value_cache = True
    with ExitStack() as ctx:
        sb = lambda name, shape, dt=F32: ctx.enter_context(nc.sbuf_tensor(name, shape, dt))
        X = sb("X", [P, TILES, D])
        XT = sb("XT", [P, B * L])
        ident = sb("ident", [P, P])
        ident_in = ctx.enter_context(nc.semaphore("ident_in"))
        x_tiles = x.rearrange("b (t p) d -> p (b t) d", p=P)

        def load(sp, loaded):
            for b in range(B):
                sp.dma_start(X[:, b * TB:(b + 1) * TB, :], x_tiles[:, b * TB:(b + 1) * TB, :]).then_inc(loaded[b], 16)
            sp.dma_start(ident[:], c["ident"]).then_inc(ident_in, 16)

        W = {}
        scratch = {name: nc.dram_tensor(name, (SLOT_TILES * P, D), F32, kind="Internal").ap()
                   for name in ("tokens", "results")}

        def experts(phase, XT, first):
            if first:
                for name, n in (("w1", NE * HID), ("w3", NE * HID), ("w2", NE * HT * D)):
                    W[name] = sb(name, [P, n])
                W["in"] = ctx.enter_context(nc.semaphore("weights_in"))
            expert_phase(nc, phase, X, XT, scratch, ident, c, w, W, first)

        for i, (name, phase) in enumerate((
                ("a", lambda XT: attention_phase(nc, X, XT, ident, ident_in, c, w, load)),
                ("ffn", lambda XT: experts("ffn1", XT, True)),
                ("decay", lambda XT: decay_phase(nc, X, XT, ident, c, w)),
                ("ffn2", lambda XT: experts("ffn2", XT, stop == "ffn2")))):
            if stop in ("decay", "ffn", "ffn2"):
                if name != stop:
                    continue
                lds = [ctx.enter_context(nc.semaphore(f"tl{k}")) for k in range(B)]
                with nc.Block() as block:
                    @block.sync
                    def _(sp):
                        load(sp, lds)
                        for k in range(B):
                            sp.wait_ge(lds[k], 16)
                        sp.wait_ge(ident_in, 16)
            phase(XT)
            if stop == name:
                break

        with ExitStack() as ph:
            stored = ph.enter_context(nc.semaphore("stored"))
            with nc.Block() as block:
                @block.sync
                def _(sp):
                    out_tiles = out.rearrange("b (t p) d -> p (b t) d", p=P)
                    for b in range(B):
                        sp.dma_start(out_tiles[:, b * TB:(b + 1) * TB, :], X[:, b * TB:(b + 1) * TB, :])\
                            .then_inc(stored, 16)
                    sp.wait_ge(stored, 16 * B)


def shape_constants():
    import numpy as np
    rows = np.arange(3 * GE)
    masks = (rows[:, None] % GE // HD == np.arange(HG)[None, :]).astype(np.float32)
    slopes = np.power(np.float32(2.0), np.linspace(-4.0, -0.3, H, dtype=np.float32)).astype(np.float32)
    bias = -(slopes[:, None] * np.arange(L, dtype=np.float32)[None, :]).astype(np.float32)
    high = (bias.view(np.uint32) & np.uint32(0xFFFFF000)).view(np.float32)
    low = bias - high
    aux = np.zeros((G, 2 + 2 * HG, HG, L), np.float32)
    for g in range(G):
        for j in range(HG):
            aux[g, 0, j], aux[g, 1, j] = high[g * HG + j], low[g * HG + j]
            aux[g, 2 + j, j] = 1.0
            aux[g, 2 + HG + j, j] = 1.0
    row = np.arange(P)
    more = {"masks_b": (row[:, None] % GE // HD == np.arange(HG)[None, :]),
            "same_head": row[:, None] // HD == row[None, :] // HD,
            "lag": np.maximum(row[None, :] - row[:, None], 0), "causal": row[None, :] >= row[:, None],
            "ahead": np.broadcast_to(row[None, :] + 1, (P, P)), "behind": (P - 1 - row)[:, None],
            "number": np.arange(NE), "earlier": row[:, None] < row[None, :], "steps": P * np.arange(HALF),
            "tile_number": np.arange(HALF_SLOTS)}
    more = {k: np.ascontiguousarray(v.astype(np.float32)) for k, v in more.items()}
    return more | {"masks": masks, "key_aux": aux.reshape(G, 2 + 2 * HG, HG * L), "ident": np.eye(P, dtype=np.float32)}


def lay_out(inputs):
    import numpy as np
    a = {k: np.asarray(v) for k, v in inputs.items()}
    thrice = lambda W: np.ascontiguousarray(np.tile(W.T.reshape(D, G, 1, GE), (1, 1, 3, 1)).reshape(D, G, 3 * GE))
    thrice_b = lambda v: np.ascontiguousarray(np.tile(v.reshape(G, 1, GE), (1, 3, 1)).reshape(G, 3 * GE).T)
    return {"Wq3": thrice(a["L0_attn_a_Wq"]), "Wk3": thrice(a["L0_attn_a_Wk"]),
            "bq3": thrice_b(a["L0_attn_a_bq"]), "bk3": thrice_b(a["L0_attn_a_bk"]),
            "WvT": np.ascontiguousarray(a["L0_attn_a_Wv"].T), "WoT": np.ascontiguousarray(a["L0_attn_a_Wo"].T),
            "bv": a["L0_attn_a_bv"], "bo": a["L0_attn_a_bo"]} | lay_out_rest(a)


def lay_out_rest(a):
    import numpy as np
    cat = lambda x, y: np.concatenate([a["L0_ffn_" + x], a["L0_ffn_" + y]], axis=0)
    up = lambda W: np.ascontiguousarray(W.transpose(2, 0, 1).reshape(D, NE * HID))
    w2 = np.zeros((P, NE, HT, D), np.float32)
    down = cat("w2", "new_w2").transpose(2, 0, 1)
    for t in range(HT):
        rows = min(P, HID - t * P)
        w2[:rows, :, t] = down[t * P:t * P + rows]
    Wqkv = a["L0_attn_b_W_qkv"]
    turn = lambda W: np.ascontiguousarray(W.T)
    log_gamma = a["L0_attn_b_log_gamma"]
    return {"w1T": up(cat("w1", "new_w1")), "w3T": up(cat("w3", "new_w3")), "w2T": w2.reshape(P, -1),
            "gateT": turn(cat("gate_weight", "new_gate_weight")),
            "gbias": np.concatenate([np.zeros(NE - 1, np.float32), a["L0_ffn_gate_bias"]]),
            "b_WqT": turn(Wqkv[0:D]), "b_WkT": turn(Wqkv[D:2 * D]), "b_WvT": turn(Wqkv[2 * D:3 * D]),
            "b_WoT": turn(a["L0_attn_b_W_o"]), "log_gamma": log_gamma,
            "log_gamma_rows": np.ascontiguousarray(np.repeat(log_gamma, HD)[:, None])}


def kernel(**inputs):
    import numpy as _np
    import concourse.bacc as _bacc
    from concourse import mybir as _mybir
    from concourse.bass_utils import run_bass_kernel_spmd as _run

    nc = _bacc.Bacc("TRN2", target_bir_lowering=False, num_devices=1)
    arrays = {}

    def declare(prefix, named):
        aps = {}
        for name, a in named.items():
            a = _np.ascontiguousarray(a)
            arrays[prefix + name] = a
            aps[name] = nc.dram_tensor(prefix + name, a.shape, _mybir.dt.from_np(a.dtype), kind="ExternalInput").ap()
        return aps

    x = declare("in_", {"x": _np.asarray(inputs["L0_attn_a_x"])})["x"]
    c = declare("const_", shape_constants())
    w = declare("weight_", lay_out(inputs))
    out = nc.dram_tensor("out_dram", (B, L, D), _mybir.dt.float32, kind="ExternalOutput").ap()
    build_program(nc, x, c, w, out)
    r = _run(nc, [arrays], core_ids=[0])
    return r.results[0]["out_dram"]
```

```python
import concourse.bass as bass
from concourse import mybir
from contextlib import ExitStack

F32 = mybir.dt.float32
F32R = mybir.dt.float32r
ALU = mybir.AluOpType
ACT = mybir.ActivationFunctionType
AX = mybir.AxisListType
ds = bass.ds

P = 128
B, L, D = 4, 1024, 128
H, HD = 16, 8
TB = L // P
TILES = B * TB
G, HG = 4, 4
GE = HG * HD
BANK = 512
TH = BANK // P
QH = L // BANK
LN_EPS = 1e-5
SCORE_SCALE = 1.0 / HD ** 0.5
NE, HID = 9, 352
HT = -(-HID // P)
TOP, ROUTE_EPS = 2, 1e-20
HALVES = 2
HALF = TILES // HALVES
HALF_SLOTS = HALF * TOP + NE - 1
SLOT_TILES = HALVES * HALF_SLOTS
VW = 32


class Sems:

    def __init__(self, nc, ctx, phase):
        self.nc, self.made = nc, []
        self.make = lambda name: ctx.enter_context(nc.semaphore(f"{phase}_{name}"))
        ctx.callback(self.clear)

    def __call__(self, *names):
        made = [self.make(n) for n in names]
        self.made += made
        return made

    def clear(self):
        with self.nc.Block() as block:
            @block.sync
            def _(sp):
                for s in self.made:
                    sp.sem_clear(s)


def layernorm_phase(nc, phase, X, XT, ident, load=None, side_job=None, act_job=None, ident_in=None):
    with ExitStack() as ctx:
        sem = Sems(nc, ctx, phase)
        sb = lambda name, shape, dt=F32: ctx.enter_context(nc.sbuf_tensor(f"{phase}_{name}", shape, dt))
        stats = sb("stats", [P, TILES, 6])
        meanvar = sb("meanvar", [P, TILES, 2])
        std = sb("std", [P, TILES])
        rstd = sb("rstd", [P, TILES])
        eps = sb("eps", [P, 1])
        BANKS = 4
        xn = sb("xn", [P, BANKS, TH * P])
        banks = [ctx.enter_context(nc.psum_tensor(f"{phase}_t{i}", [P, BANK], F32)) for i in range(BANKS)]
        (eps_set, stats_done, aggregated, std_done, inverted, normed, transposed, evacuated) = sem(
            "eps_set", "stats_done", "aggregated", "std_done", "inverted", "normed", "transposed", "evacuated")
        loaded = sem(*[f"loaded{b}" for b in range(B)]) if load else None
        QUADS = TILES // TH
        with nc.Block() as block:
            if load:
                @block.sync
                def _(sp):
                    load(sp, loaded)

            @block.vector
            def _(dve):
                nc.vector.memset(eps[:], LN_EPS).then_inc(eps_set, 1)

                def statistics(b):
                    if load:
                        dve.wait_ge(loaded[b], 16)
                    tiles = range(b * TB, (b + 1) * TB)
                    for i in tiles:
                        nc.vector.bn_stats(stats[:, i, :], X[:, i, :]).then_inc(stats_done, 1)
                    for i in tiles:
                        dve.wait_ge(stats_done, i + 1)
                        nc.vector.bn_aggr(meanvar[:, i, :], stats[:, i, :]).then_inc(aggregated, 1)

                def normalise(b):
                    dve.wait_ge(std_done, b + 1)
                    cols = slice(b * TB, (b + 1) * TB)
                    nc.vector.reciprocal(rstd[:, cols], std[:, cols]).then_inc(inverted, 1)
                    dve.wait_ge(inverted, b + 1)
                    for q in range(b * TB // TH, (b + 1) * TB // TH):
                        if q >= BANKS:
                            dve.wait_ge(transposed, q - BANKS + 1)
                        for t in range(TH):
                            i = q * TH + t
                            last = nc.vector.tensor_scalar(xn[:, q % BANKS, t * P:(t + 1) * P], X[:, i, :],
                                                           meanvar[:, i, 0:1], rstd[:, i:i + 1],
                                                           ALU.subtract, ALU.mult)
                        last.then_inc(normed, 1)

                statistics(0)
                for b in range(1, B):
                    statistics(b)
                    normalise(b - 1)
                normalise(B - 1)

            @block.scalar
            def _(act):
                def deviations(b):
                    if b == 0:
                        act.wait_ge(eps_set, 1)
                    act.wait_ge(aggregated, TB * (b + 1))
                    nc.scalar.activation(std[:, b * TB:(b + 1) * TB], meanvar[:, b * TB:(b + 1) * TB, 1], ACT.Sqrt,
                                         bias=eps[:, 0:1]).then_inc(std_done, 1)

                def evacuate(q):
                    act.wait_ge(transposed, q + 1)
                    nc.scalar.activation(XT[:, q * BANK:(q + 1) * BANK], banks[q % BANKS][:, :], ACT.Copy)\
                        .then_inc(evacuated, 1)

                deviations(0)
                for b in range(1, B):
                    deviations(b)
                    for q in range((b - 1) * TB // TH, b * TB // TH):
                        evacuate(q)
                if act_job is not None:
                    act_job(act)
                for q in range((B - 1) * TB // TH, QUADS):
                    evacuate(q)

            @block.tensor
            def _(pe):
                if ident_in is not None:
                    pe.wait_ge(ident_in, 16)
                for q in range(QUADS):
                    pe.wait_ge(normed, q + 1)
                    if q >= BANKS:
                        pe.wait_ge(evacuated, q - BANKS + 1)
                    for t in range(TH):
                        last = nc.tensor.transpose(banks[q % BANKS][:, t * P:(t + 1) * P],
                                                   xn[:, q % BANKS, t * P:(t + 1) * P], ident[:, :])
                    last.then_inc(transposed, 1)

            if side_job is not None:
                side_job(block)


def attention_phase(nc, X, XT, ident, ident_in, c, w, load, scratch):
    AUX = 3 * GE
    NROW_S = AUX + 2
    NROW_T = NROW_S + 2 * HG
    ROTATE = 3

    def last_user(u, units):
        return u - ROTATE if u >= ROTATE else max(v for v in range(units) if v % ROTATE == u) - units

    with ExitStack() as ctx:
        sem = Sems(nc, ctx, "attn")
        sb = lambda name, shape, dt=F32: ctx.enter_context(nc.sbuf_tensor(f"attn_{name}", shape, dt))
        ps = lambda name, shape: ctx.enter_context(nc.psum_tensor(f"attn_{name}", shape, F32))
        Wq3 = sb("Wq3", [D, G, AUX]); Wk3 = sb("Wk3", [D, G, AUX])
        bq3 = sb("bq3", [AUX, G]); bk3 = sb("bk3", [AUX, G]); bq3s = sb("bq3s", [AUX, G])
        WvT = sb("WvT", [D, D]); WoT = sb("WoT", [D, D])
        bvb = sb("bvb", [P, D]); bob = sb("bob", [P, D])
        masks = sb("masks", [AUX, HG])
        V = sb("V", [P, TILES, D])
        Vp = sb("Vp", [P, TB, H, VW])
        Q = [sb(f"Q{g}", [P, L], F32R) for g in range(G)]
        K = [sb(f"K{g}", [P, HG, L], F32R) for g in range(G)]
        Tq = sb("Tq", [AUX, L]); Tk = sb("Tk", [AUX, L]); Kc = sb("Kc", [AUX, L])
        E = sb("E", [P, 2, HG, BANK])
        hmax = sb("hmax", [P, 2, TB * HG, QH])
        nmax = sb("nmax", [P, TB, HG])
        M2 = sb("M2", [P, TB, VW])
        U = sb("U", [P, L])
        rden = sb("rden", [P, TH * HG])
        On = sb("On", [P, TB, D])
        ones = U
        OnT = sb("OnT", [P, L])

        (w_loaded, const_loaded, bias_set, zero_done, x_biased) = sem(
            "w_loaded", "const_loaded", "bias_set", "zero_done", "x_biased")
        (proj_ready, proj_taken, q_high, k_high, k_low, k_copies, q_done, k_done) = sem(
            "proj_ready", "proj_taken", "q_high", "k_high", "k_low", "k_copies", "q_done", "k_done")
        (score_ready, max_taken, max_joined, max_high, aux_in, aux_ready, aux_taken) = sem(
            "score_ready", "max_taken", "max_joined", "max_high", "aux_in", "aux_ready", "aux_taken")
        (tscore_ready, exp_done, pv_done, u_taken) = sem("tscore_ready", "exp_done", "pv_done", "u_taken")
        (ut_ready, rden_done, on_done, ont_ready, ont_taken, y_ready, y_added) = sem(
            "ut_ready", "rden_done", "on_done", "ont_ready", "ont_taken", "y_ready", "y_added")
        (v_ready, v_taken, vp_done) = sem("v_ready", "v_taken", "vp_done")

        S_UNITS = TB * HG * QH
        T_UNITS = QH * TB * HG
        BLOCKS = QH * TB
        PER_BLOCK = S_UNITS // BLOCKS
        AHEAD = 3

        def score_units(k, now, later):
            m = PER_BLOCK * (k + AHEAD)
            ahead, m = 1 + m // S_UNITS, m % S_UNITS
            return [(ahead, m + i) for i in range(PER_BLOCK)] if (now, later)[ahead - 1] else []

        MISC = {1: ("K", 0), 2: ("K", 1), 3: ("Q", 0), 4: ("Q", 1), 5: ("T", 0), 6: ("T", 1),
                8: ("G", 0), 9: ("G", 1), 11: ("Y", 0), 12: ("Y", 1), 14: ("A", 0), 15: ("A", 1)}

        def misc(k, s, project, score, after):
            kind, h = MISC.get(k, (None, 0))
            ok = {"K": project, "Q": project, "A": score, "T": after, "G": after and s == 0,
                  "Y": after and s == 0}.get(kind, False)
            return (kind, h) if ok else None

        weights = ((Wq3[:], w["Wq3"]), (Wk3[:], w["Wk3"]), (bq3[:], w["bq3"]), (bk3[:], w["bk3"]),
                   (WvT[:], w["WvT"]), (WoT[:], w["WoT"]), (masks[:], c["masks"]),
                   (bvb[:], w["bv"].partition_broadcast(P)), (bob[:], w["bo"].partition_broadcast(P)))

        zeros = sb("zeros", [P, BANK])
        zeros_set, cleared = sem("zeros_set", "cleared")

        def load_all(sp, loaded):
            load(sp, loaded)
            for dst, src in weights:
                sp.dma_start(dst, src).then_inc(w_loaded, 16)
            sp.wait_ge(zeros_set, 1)
            for place in scratch.values():
                sp.dma_start(place.rearrange("(p n m) d -> p n (m d)", p=P, m=BANK // D),
                             zeros[:].unsqueeze(1).broadcast_to([P, SLOT_TILES * D // BANK, BANK]))\
                    .then_inc(cleared, 16)
            sp.wait_ge(w_loaded, 16 * len(weights))

        def constants(block):
            @block.gpsimd
            def _(pool):
                for g in range(G):
                    pool.dma_start(K[g][AUX:NROW_T, :, :].rearrange("p h k -> p (h k)"), c["key_aux"][g])\
                        .then_inc(const_loaded, 16)
                count = [0]

                def alone(ins):
                    count[0] += 1
                    ins.then_inc(zero_done, 1)
                    pool.wait_ge(zero_done, count[0])

                nc.gpsimd.memset(zeros[:], 0.0).then_inc(zeros_set, 1)
                pool.wait_ge(zeros_set, 1)
                alone(nc.gpsimd.memset(ones[AUX:P, :], 1.0))
                for g in range(G):
                    alone(nc.gpsimd.tensor_tensor(Q[g][AUX:P, :], ones[AUX:P, :], ones[AUX:P, :], ALU.mult))
                alone(nc.gpsimd.memset(Vp[:].rearrange("p t h c -> p (t h c)"), 0.0))
                alone(nc.gpsimd.memset(M2[:].rearrange("p t c -> p (t c)"), 0.0))
                alone(nc.gpsimd.memset(Vp[:, :, :, HD:HD + 1], 1.0))
                alone(nc.gpsimd.memset(M2[:, :, 0:2], 1.0))
                pool.wait_ge(const_loaded, 16 * G)

        layernorm_phase(nc, "ln0", X, XT, ident, load=load_all, side_job=constants, ident_in=ident_in)

        bankT = [ps(f"bankT{i}", [P, BANK]) for i in range(ROTATE)]
        bankS = [ps(f"bankS{i}", [P, BANK]) for i in range(ROTATE)]
        bankO = ps("bankO", [P, BANK])
        bankM = ps("bankM", [P, BANK])

        PROJECTIONS = (("K", 0), ("K", 1), ("Q", 0), ("Q", 1))

        with nc.Block() as block:
            @block.sync
            def _(sp):
                sp.wait_ge(cleared, 16 * len(scratch))

            @block.tensor
            def _(pe):
                def project(n, g, b, kind, h):
                    W = (Wk3 if kind == "K" else Wq3)
                    tokens = XT[:, b * L + h * BANK:b * L + (h + 1) * BANK] if isinstance(b, int) else \
                        XT[:, ds(b * L + h * BANK, BANK)]
                    nc.tensor.matmul(bankM[0:AUX, :], W[:, g, :], tokens, start=True, stop=True)\
                        .then_inc(proj_ready, 1)

                def aux(n, h):
                    if h == 0:
                        pe.wait_ge(aux_in, n + 1)
                    for t in range(TH):
                        last = nc.tensor.matmul(bankM[AUX:P, t * P:(t + 1) * P], M2[:, h * TH + t, :], ident[:],
                                                start=True, stop=True)
                    last.then_inc(aux_ready, 1)

                def score_unit(n, g, m):
                    qt, j, kh = m // (HG * QH), m // QH % HG, m % QH
                    if m == 0:
                        pe.wait_ge(k_done, n + 1)
                        pe.wait_ge(q_done, n + 1)
                    if not (isinstance(n, int) and n == 0 and m < ROTATE):
                        pe.wait_ge(max_taken, S_UNITS * n + last_user(m, S_UNITS) + 1)
                    nc.tensor.matmul(bankS[m % ROTATE][:], Q[g][0:NROW_S, qt * P:(qt + 1) * P],
                                     K[g][0:NROW_S, j, kh * BANK:(kh + 1) * BANK],
                                     start=True, stop=True).then_inc(score_ready, 1)

                def tscore(n, g, k, j, first):
                    qh, kt, u = k // TB, k % TB, HG * k + j
                    if kt == 0 and j == 0:
                        pe.wait_ge(aux_taken, 2 * n + qh + 1)
                    if not (first and u < ROTATE):
                        pe.wait_ge(exp_done, T_UNITS * n + last_user(u, T_UNITS) + 1)
                    nc.tensor.matmul(bankT[u % ROTATE][:], K[g][0:NROW_T, j, kt * P:(kt + 1) * P],
                                     Q[g][0:NROW_T, qh * BANK:(qh + 1) * BANK], start=True, stop=True)\
                        .then_inc(tscore_ready, 1)

                def value_tiles(q):
                    if q:
                        pe.wait_ge(v_taken, q)
                    for t in range(TH):
                        i = q * TH + t
                        last = nc.tensor.matmul(bankO[:, t * D:(t + 1) * D], XT[:, i * P:(i + 1) * P], WvT[:],
                                                start=True, stop=True)
                    last.then_inc(v_ready, 1)

                def values(n, g, k, b):
                    qh, kt = k // TB, k % TB
                    if k == 0 and g == 0:
                        pe.wait_ge(vp_done, b + 1)
                    if kt == 0:
                        if isinstance(n, int) and n == 0 and qh == 0:
                            pe.wait_ge(v_taken, TILES // TH)
                        else:
                            pe.wait_ge(u_taken, 2 * n + qh)
                    pe.wait_ge(exp_done, HG * (BLOCKS * n + k + 1))
                    for j in range(HG):
                        last = nc.tensor.matmul(bankO[32 * j:32 * j + VW, :], Vp[:, kt, g * HG + j, :],
                                                E[:, k % 2, j, :], start=(kt == 0), stop=(kt == TB - 1))
                    last.then_inc(pv_done, 1)

                def transpose_u(n, h):
                    pe.wait_ge(u_taken, 2 * n + h + 1)
                    for t in range(TH):
                        last = nc.tensor.transpose(bankM[:, t * P:(t + 1) * P],
                                                   U[:, (h * TH + t) * P:(h * TH + t + 1) * P], ident[:])
                    last.then_inc(ut_ready, 1)

                def transpose_on(n, h):
                    if h == 0:
                        pe.wait_ge(on_done, 2 * n + 2)
                    for t in range(TH):
                        last = nc.tensor.transpose(bankM[:, t * P:(t + 1) * P], On[:, h * TH + t, :], ident[:])
                    last.then_inc(ont_ready, 1)

                def out_project(b, h):
                    if h == 0:
                        pe.wait_ge(ont_taken, 2 * b + 2)
                    for t in range(TH):
                        last = nc.tensor.matmul(bankM[:, t * D:(t + 1) * D],
                                                OnT[:, (h * TH + t) * P:(h * TH + t + 1) * P], WoT[:],
                                                start=True, stop=True)
                    last.then_inc(y_ready, 1)

                def step(b, s, project_next, score_next, after, first=False):
                    n = 4 * b + s
                    g2 = (s + 2) % 4
                    b2 = b + (s + 2) // 4
                    for k in range(BLOCKS):
                        units = score_units(k, score_next, project_next)
                        tscore(n, s, k, 0, first)
                        for j in range(HG):
                            if j:
                                tscore(n, s, k, j, first)
                            for ahead, m in units[j:j + 1]:
                                score_unit(n + ahead, (s + ahead) % 4, m)
                            if j == 1 and k > 0:
                                values(n, s, k - 1, b)
                            elif j == 1 and not first:
                                if s == 0:
                                    values(n - 1, 3, BLOCKS - 1, b - 1)
                                else:
                                    values(n - 1, s - 1, BLOCKS - 1, b)
                        unit = misc(k, s, project_next, score_next, after)
                        if unit:
                            kind, h = unit
                            pe.wait_ge(*free_at[0])
                            if kind in "KQ":
                                project(n + 2, g2, b2, kind, h)
                                free_at[0] = (proj_taken, 4 * (n + 2) + (2 if kind == "Q" else 0) + h + 1)
                            elif kind == "A":
                                aux(n + 1, h)
                                free_at[0] = (aux_taken, 2 * (n + 1) + h + 1)
                            elif kind == "T":
                                transpose_u(n - 1, h)
                                free_at[0] = (on_done, 2 * (n - 1) + h + 1)
                            elif kind == "G":
                                transpose_on(n - 1, h)
                                free_at[0] = (ont_taken, 2 * (b - 1) + h + 1)
                            else:
                                out_project(b - 1, h)
                                free_at[0] = (y_added, 2 * (b - 1) + h + 1)

                free_at = [None]

                def project_early(n, i):
                    if free_at[0]:
                        pe.wait_ge(*free_at[0])
                    project(n, n, 0, *PROJECTIONS[i])
                    free_at[0] = (proj_taken, 4 * n + i + 1)

                for i in range(4):
                    project_early(0, i)
                for m in range(S_UNITS):
                    score_unit(0, 0, m)
                    if m % 8 == 7:
                        value_tiles(m // 8)
                    if m % 8 == 3 and 1 <= m // 8 <= 4:
                        project_early(1, m // 8 - 1)
                for h in range(2):
                    pe.wait_ge(*free_at[0])
                    aux(0, h)
                    free_at[0] = (aux_taken, h + 1)
                for m in range(PER_BLOCK * AHEAD):
                    score_unit(1, 1, m)
                step(0, 0, True, True, False, first=True)
                with pe.Fori(0, B - 1) as b:
                    free_at[0] = (aux_taken, 8 * b + 4)
                    step(b, 1, True, True, True)
                    step(b, 2, True, True, True)
                    step(b, 3, True, True, True)
                    step(b + 1, 0, True, True, True)
                free_at[0] = (aux_taken, 2 * 13 + 2)
                step(B - 1, 1, True, True, True)
                step(B - 1, 2, False, True, True)
                step(B - 1, 3, False, False, True)
                n = 4 * B - 1
                values(n, 3, BLOCKS - 1, B - 1)
                for h in range(2):
                    pe.wait_ge(*free_at[0])
                    transpose_u(n, h)
                    free_at[0] = (on_done, 2 * n + h + 1)
                for h in range(2):
                    pe.wait_ge(*free_at[0])
                    transpose_on(n, h)
                    free_at[0] = (ont_taken, 2 * (B - 1) + h + 1)
                for h in range(2):
                    pe.wait_ge(*free_at[0])
                    out_project(B - 1, h)
                    free_at[0] = (y_added, 2 * (B - 1) + h + 1)

            @block.scalar
            def _(act):
                def take_projection(n, g, kind, h):
                    i = (2 if kind == "Q" else 0) + h
                    act.wait_ge(proj_ready, 4 * n + i + 1)
                    T, bias, scale = (Tk, bk3, 1.0) if kind == "K" else (Tq, bq3s, SCORE_SCALE)
                    if h == 0 and not (isinstance(n, int) and n == 0):
                        act.wait_ge(k_low if kind == "K" else q_done, n)
                    nc.scalar.activation(T[:, h * BANK:(h + 1) * BANK], bankM[0:AUX, :], ACT.Identity,
                                         bias=bias[:, g:g + 1], scale=scale).then_inc(proj_taken, 1)

                def take_aux(n, g, h):
                    act.wait_ge(aux_ready, 2 * n + h + 1)
                    nc.scalar.activation(Q[g][AUX:NROW_T, h * BANK:(h + 1) * BANK], bankM[AUX:NROW_T, :], ACT.Copy)\
                        .then_inc(aux_taken, 1)

                def exponential(n, k, j, first):
                    act.wait_ge(tscore_ready, HG * (BLOCKS * n + k) + j + 1)
                    if not (first and k < 2):
                        act.wait_ge(pv_done, BLOCKS * n + k - 1)
                    nc.scalar.activation(E[:, k % 2, j, :], bankT[(HG * k + j) % ROTATE][:], ACT.Exp)\
                        .then_inc(exp_done, 1)

                def take_u(n, h):
                    act.wait_ge(pv_done, BLOCKS * n + TB * (h + 1))
                    nc.scalar.activation(U[:, h * BANK:(h + 1) * BANK], bankO[:], ACT.Copy).then_inc(u_taken, 1)

                def take_ont(b, h):
                    act.wait_ge(ont_ready, 2 * b + h + 1)
                    nc.scalar.activation(OnT[:, h * BANK:(h + 1) * BANK], bankM[:], ACT.Copy).then_inc(ont_taken, 1)

                def step(b, s, project_next, score_next, after, first=False):
                    n = 4 * b + s
                    for k in range(BLOCKS):
                        for j in range(HG):
                            exponential(n, k, j, first)
                        if k == 0 and not first:
                            take_u(n - 1, 1)
                        if k == TB:
                            take_u(n, 0)
                        unit = misc(k, s, project_next, score_next, after)
                        if unit:
                            kind, h = unit
                            if kind in "KQ":
                                take_projection(n + 2, (s + 2) % 4, kind, h)
                            elif kind == "A":
                                take_aux(n + 1, (s + 1) % 4, h)
                            elif kind == "G":
                                take_ont(b - 1, h)

                nc.scalar.mul(bq3s[:], bq3[:], SCORE_SCALE).then_inc(bias_set, 1)
                act.wait_ge(bias_set, 1)
                for kind, h in PROJECTIONS:
                    take_projection(0, 0, kind, h)
                for q in range(TILES // TH):
                    act.wait_ge(v_ready, q + 1)
                    nc.scalar.activation(V[:, q * TH:(q + 1) * TH, :].rearrange("p t e -> p (t e)"), bankO[:],
                                         ACT.Copy).then_inc(v_taken, 1)
                    if q < 4:
                        take_projection(1, 1, *PROJECTIONS[q])
                for h in range(2):
                    take_aux(0, 0, h)
                step(0, 0, True, True, False, first=True)
                with act.Fori(0, B - 1) as b:
                    step(b, 1, True, True, True)
                    step(b, 2, True, True, True)
                    step(b, 3, True, True, True)
                    step(b + 1, 0, True, True, True)
                step(B - 1, 1, True, True, True)
                step(B - 1, 2, False, True, True)
                step(B - 1, 3, False, False, True)
                take_u(4 * B - 1, 1)
                for h in range(2):
                    take_ont(B - 1, h)

            @block.vector
            def _(dve):
                def high_part(n, g, kind):
                    static = isinstance(n, int)
                    dve.wait_ge(proj_taken, 4 * n + (4 if kind == "Q" else 2))
                    if kind == "K":
                        if not (static and n == 0):
                            dve.wait_ge(k_done, n)
                        nc.vector.tensor_copy(Kc[:].bitcast(F32R), Tk[:]).then_inc(k_high, 1)
                    else:
                        if not (static and n < 4):
                            dve.wait_ge(tscore_ready, HG * BLOCKS * (n - 3))
                        nc.vector.tensor_copy(Q[g][0:AUX, :], Tq[:]).then_inc(q_high, 1)

                def take_max(n, g, m):
                    dve.wait_ge(score_ready, S_UNITS * n + m + 1)
                    nc.vector.reduce_max(hmax[:, g % 2, m // QH, m % QH:m % QH + 1], bankS[m % ROTATE][:], AX.X)\
                        .then_inc(max_taken, 1)

                def split_max(n, g):
                    dve.wait_ge(max_taken, S_UNITS * (n + 1))
                    nc.vector.tensor_reduce(nmax[:].rearrange("p t j -> p (t j)"), hmax[:, g % 2], AX.X, ALU.max,
                                            negate=True).then_inc(max_joined, 1)
                    dve.wait_ge(max_joined, n + 1)
                    if not (isinstance(n, int) and n == 0):
                        dve.wait_ge(aux_ready, 2 * n)
                    nc.vector.tensor_copy(M2[:, :, 2:2 + HG].bitcast(F32R), nmax[:]).then_inc(max_high, 1)
                    dve.wait_ge(max_high, n + 1)
                    nc.vector.tensor_tensor(M2[:, :, 2 + HG:2 + 2 * HG], nmax[:], M2[:, :, 2:2 + HG],
                                            ALU.subtract).then_inc(aux_in, 1)

                def normalise(n, g, h):
                    dve.wait_ge(ut_ready, 2 * n + h + 1)
                    u = bankM[:].rearrange("p (tj c) -> p tj c", c=VW)
                    nc.vector.reciprocal(rden[:], u[:, :, HD]).then_inc(rden_done, 1)
                    dve.wait_ge(rden_done, 2 * n + h + 1)
                    out = On[:, h * TH:(h + 1) * TH, g * GE:(g + 1) * GE].rearrange("p t (j e) -> p t j e", e=HD)
                    nc.vector.tensor_tensor(out, u[:, :, 0:HD].rearrange("p (t j) e -> p t j e", t=TH),
                                            rden[:].rearrange("p (t j) -> p t j", t=TH).unsqueeze(3)
                                            .broadcast_to([P, TH, HG, HD]), ALU.mult).then_inc(on_done, 1)
                    dve.wait_ge(on_done, 2 * n + h + 1)

                def add_output(b, h):
                    dve.wait_ge(y_ready, 2 * b + h + 1)
                    dve.wait_ge(x_biased, TILES)
                    x = X[:, ds(b * TB + h * TH, TH), :]
                    nc.vector.tensor_tensor(x, bankM[:].rearrange("p (t e) -> p t e", t=TH), x, ALU.add)\
                        .then_inc(y_added, 1)

                def pad_values(b):
                    if isinstance(b, int) and b == 0:
                        dve.wait_ge(v_taken, TILES // TH)
                    else:
                        dve.wait_ge(pv_done, 4 * BLOCKS * b)
                    heads = lambda a: a.rearrange("p t (h e) -> p t h e", e=HD)
                    nc.vector.tensor_tensor(Vp[:, :, :, 0:HD], heads(V[:, ds(b * TB, TB), :]),
                                            heads(bvb[:].unsqueeze(1).broadcast_to([P, TB, D])), ALU.add)\
                        .then_inc(vp_done, 1)

                def step(b, s, project_next, score_next, after, first=False):
                    n = 4 * b + s
                    for k in range(BLOCKS):
                        units = score_units(k, score_next, project_next)
                        if k == 0 and s == 0 and not first:
                            for ahead, m in units[:1]:
                                take_max(n + ahead, (s + ahead) % 4, m)
                            units = units[1:]
                            pad_values(b)
                        for ahead, m in units:
                            take_max(n + ahead, (s + ahead) % 4, m)
                            if m == S_UNITS - 1:
                                split_max(n + 1, (s + 1) % 4)
                        if project_next and k == 3:
                            high_part(n + 2, (s + 2) % 4, "K")
                        if project_next and k == 5:
                            high_part(n + 2, (s + 2) % 4, "Q")
                        unit = misc(k, s, project_next, score_next, after)
                        if unit and unit[0] == "T":
                            normalise(n - 1, (s - 1) % 4, unit[1])
                        if unit and unit[0] == "Y":
                            add_output(b - 1, unit[1])

                def parts_first():
                    high_part(0, 0, "K")
                    dve.wait_ge(k_high, 1)
                    nc.vector.tensor_tensor(Kc[GE:2 * GE, :], Tk[GE:2 * GE, :], Kc[GE:2 * GE, :], ALU.subtract)\
                        .then_inc(k_low, 1)
                    dve.wait_ge(k_low, 1)
                    for j in range(HG):
                        last = nc.vector.tensor_scalar(K[0][0:AUX, j, :], Kc[:], masks[:, j:j + 1], None, ALU.mult)
                    last.then_inc(k_done, 1)
                    high_part(0, 0, "Q")
                    dve.wait_ge(q_high, 1)
                    nc.vector.tensor_tensor(Q[0][2 * GE:3 * GE, :], Tq[2 * GE:3 * GE, :],
                                            Q[0][2 * GE:3 * GE, :].bitcast(F32), ALU.subtract).then_inc(q_done, 1)

                parts_first()
                for m in range(S_UNITS):
                    take_max(0, 0, m)
                    if m in (24, 40):
                        high_part(1, 1, "K" if m == 24 else "Q")
                split_max(0, 0)
                pad_values(0)
                for m in range(PER_BLOCK * AHEAD):
                    take_max(1, 1, m)
                step(0, 0, True, True, False, first=True)
                with dve.Fori(0, B - 1) as b:
                    step(b, 1, True, True, True)
                    step(b, 2, True, True, True)
                    step(b, 3, True, True, True)
                    step(b + 1, 0, True, True, True)
                step(B - 1, 1, True, True, True)
                step(B - 1, 2, False, True, True)
                step(B - 1, 3, False, False, True)
                for h in range(2):
                    normalise(4 * B - 1, 3, h)
                for h in range(2):
                    add_output(B - 1, h)

            @block.gpsimd
            def _(pool):
                def low_parts(n, g):
                    static = isinstance(n, int)
                    pool.wait_ge(k_high, n + 1)
                    nc.gpsimd.tensor_tensor(Kc[GE:2 * GE, :], Tk[GE:2 * GE, :], Kc[GE:2 * GE, :], ALU.subtract)\
                        .then_inc(k_low, 1)
                    pool.wait_ge(k_low, n + 1)
                    if not (static and n < 4):
                        pool.wait_ge(tscore_ready, HG * BLOCKS * (n - 3))
                    for j in range(HG):
                        last = nc.gpsimd.tensor_tensor(K[g][0:AUX, j, :], Kc[:],
                                                       masks[:, j:j + 1].broadcast_to([AUX, L]), ALU.mult)
                    last.then_inc(k_done, 1)
                    pool.wait_ge(k_done, n + 1)
                    pool.wait_ge(q_high, n + 1)
                    nc.gpsimd.tensor_tensor(Q[g][2 * GE:3 * GE, :], Tq[2 * GE:3 * GE, :],
                                            Q[g][2 * GE:3 * GE, :].bitcast(F32), ALU.subtract).then_inc(q_done, 1)

                low_parts(1, 1)
                pool.wait_ge(q_done, 2)
                for i in range(TILES):
                    nc.gpsimd.tensor_tensor(X[:, i, :], X[:, i, :], bob[:], ALU.add).then_inc(x_biased, 1)
                pool.wait_ge(x_biased, TILES)
                low_parts(2, 2)
                with pool.Fori(0, B - 1) as b:
                    low_parts(4 * b + 3, 3)
                    low_parts(4 * b + 4, 0)
                    low_parts(4 * b + 5, 1)
                    low_parts(4 * b + 6, 2)
                low_parts(15, 3)


def routing_phase(nc, phase, X, XT, XN, share, slots, expert_of, scratch, scatter, ident, c, w, W, first):
    with ExitStack() as ctx:
        sem = Sems(nc, ctx, "ln_" + phase)
        sb = lambda name, shape, dt=F32: ctx.enter_context(nc.sbuf_tensor(f"ln_{phase}_{name}", shape, dt))
        ps = lambda name: ctx.enter_context(nc.psum_tensor(f"ln_{phase}_{name}", [P, BANK], F32))
        stats = sb("stats", [P, TILES, 6])
        meanvar = sb("meanvar", [P, TILES, 2])
        std = sb("std", [P, TILES])
        rstd = sb("rstd", [P, TILES])
        eps = sb("eps", [P, 1])
        BANKS = 4
        banks = [ps(f"t{i}") for i in range(BANKS)]
        logits = [ps(f"logits{i}") for i in range(2)]
        before_bank, total_bank = ps("before"), ps("total")
        gateT = sb("gateT", [D, NE]); gbias = sb("gbias", [P, NE]); number = sb("number", [P, NE])
        earlier = sb("earlier", [P, P]); ones = sb("ones", [P, P])
        steps = sb("steps", [P, HALF])
        tile_number = sb("tile_number", [P, HALF_SLOTS])
        scores = sb("scores", [P, TILES, NE])
        top = sb("top", [P, TILES, 8])
        where = sb("where", [P, TILES, 8], mybir.dt.uint32)
        wheref = sb("wheref", [P, TILES, TOP])
        rsum = sb("rsum", [P, TILES])
        hit = sb("hit", [P, TOP, TILES, NE])
        hits = sb("hits", [P, TILES, NE])
        PAD = HALF // 2
        sums = [sb(f"sums{i}", [P, PAD + HALF, NE]) for i in range(2)]
        rank = sb("rank", [P, HALF, NE])
        EPAD = 8
        ends = [sb(f"ends{i}", [P, EPAD + NE]) for i in range(2)]
        filled = sb("filled", [P, NE, HALF]); tiles_of = sb("tiles_of", [P, NE]); start = sb("start", [P, NE])
        place = sb("place", [P, TOP, HALF, NE]); placef = sb("placef", [P, HALF, TOP])
        passed = sb("passed", [P, HALF_SLOTS, NE - 1]); expertf = sb("expertf", [P, HALF_SLOTS])
        (eps_set, stats_done, aggregated, std_done, inverted, normed, transposed, evacuated) = sem(
            "eps_set", "stats_done", "aggregated", "std_done", "inverted", "normed", "transposed", "evacuated")
        (small_in, routed, biased, scored, found, chain, hits_done, counted, placed) = sem(
            "small_in", "routed", "biased", "scored", "found", "chain", "hits_done", "counted", "placed")
        QB = TB // TH
        quads = lambda b: range(b * QB, (b + 1) * QB)
        small = ((gateT[:], w["gateT"]), (gbias[:], w["gbias"].partition_broadcast(P)),
                 (number[:], c["number"].partition_broadcast(P)), (earlier[:], c["earlier"]),
                 (steps[:], c["steps"].partition_broadcast(P)),
                 (tile_number[:], c["tile_number"].partition_broadcast(P)))

        with nc.Block() as block:
            @block.sync
            def _(sp):
                for dst, src in small:
                    sp.dma_start(dst, src).then_inc(small_in, 16)
                if first:
                    for name in ("w1", "w3", "w2"):
                        sp.dma_start(W[name][:], w[name + "T"]).then_inc(W["in"], 16)

            @block.vector
            def _(dve):
                nc.vector.memset(eps[:], LN_EPS).then_inc(eps_set, 1)
                nc.vector.memset(ones[:], 1.0)
                for i in range(2):
                    nc.vector.memset(sums[i][:, 0:PAD, :], 0.0)
                    nc.vector.memset(ends[i][:, 0:EPAD], 0.0)

                def statistics(b):
                    tiles = range(b * TB, (b + 1) * TB)
                    for i in tiles:
                        nc.vector.bn_stats(stats[:, i, :], X[:, i, :]).then_inc(stats_done, 1)
                    for i in tiles:
                        dve.wait_ge(stats_done, i + 1)
                        nc.vector.bn_aggr(meanvar[:, i, :], stats[:, i, :]).then_inc(aggregated, 1)

                def normalise(b):
                    dve.wait_ge(std_done, b + 1)
                    cols = slice(b * TB, (b + 1) * TB)
                    nc.vector.reciprocal(rstd[:, cols], std[:, cols]).then_inc(inverted, 1)
                    dve.wait_ge(inverted, b + 1)
                    for q in quads(b):
                        for i in range(q * TH, (q + 1) * TH):
                            last = nc.vector.tensor_scalar(XN[:, i, :], X[:, i, :], meanvar[:, i, 0:1],
                                                           rstd[:, i:i + 1], ALU.subtract, ALU.mult)
                        last.then_inc(normed, 1)

                def add_bias(b):
                    if b == 0:
                        dve.wait_ge(small_in, 16 * len(small))
                    dve.wait_ge(routed, b + 1)
                    nc.vector.tensor_tensor(scores[:, b * TB:(b + 1) * TB, :],
                                            logits[b % 2][:, 0:TB * NE].rearrange("p (t e) -> p t e", e=NE),
                                            gbias[:].unsqueeze(1).broadcast_to([P, TB, NE]), ALU.add)\
                        .then_inc(biased, 1)

                def choose(b):
                    dve.wait_ge(scored, b + 1)
                    for i in range(b * TB, (b + 1) * TB):
                        nc.vector.max(top[:, i, :], scores[:, i, :]).then_inc(found, 1)
                    dve.wait_ge(found, (2 * b + 1) * TB)
                    for i in range(b * TB, (b + 1) * TB):
                        nc.vector.max_index(where[:, i, :], top[:, i, :], scores[:, i, :]).then_inc(found, 1)

                count = [0]

                def link(ins):
                    count[0] += 1
                    ins.then_inc(chain, 1)
                    dve.wait_ge(chain, count[0])

                def place_half(h):
                    tiles = slice(h * HALF, (h + 1) * HALF)
                    per_tile = lambda a: a[:, h * HALF * NE:(h + 1) * HALF * NE].rearrange("p (t e) -> p t e", e=NE)
                    dve.wait_ge(found, 2 * HALF * (h + 1))
                    link(nc.vector.tensor_copy(wheref[:, tiles], where[:, tiles, 0:TOP]))
                    for k in range(TOP):
                        last = nc.vector.tensor_tensor(
                            hit[:, k, tiles], wheref[:, tiles, k:k + 1].broadcast_to([P, HALF, NE]),
                            number[:].unsqueeze(1).broadcast_to([P, HALF, NE]), ALU.is_equal)
                    link(last)
                    nc.vector.tensor_tensor(hits[:, tiles], hit[:, 0, tiles], hit[:, 1, tiles], ALU.add)\
                        .then_inc(hits_done, 1)

                    link(nc.vector.tensor_tensor(rsum[:, tiles], top[:, tiles, 0], top[:, tiles, 1], ALU.add))
                    link(nc.vector.tensor_scalar(rsum[:, tiles], rsum[:, tiles], ROUTE_EPS, None, ALU.add))
                    link(nc.vector.reciprocal(rsum[:, tiles], rsum[:, tiles]))
                    nc.vector.tensor_tensor(share[:, tiles], top[:, tiles, 0:TOP], rsum[:, tiles].unsqueeze(2)
                                            .broadcast_to([P, HALF, TOP]), ALU.mult)

                    dve.wait_ge(counted, 2 * h + 2)
                    totals = per_tile(total_bank)
                    link(nc.vector.tensor_copy(sums[0][:, PAD:, :], totals))
                    i, reach = 0, 1
                    while reach < HALF:
                        link(nc.vector.tensor_tensor(sums[1 - i][:, PAD:, :], sums[i][:, PAD:, :],
                                                     sums[i][:, PAD - reach:PAD + HALF - reach, :], ALU.add))
                        i, reach = 1 - i, 2 * reach
                    upto = sums[i]
                    nc.vector.tensor_tensor(rank[:], upto[:, PAD:, :], totals, ALU.subtract)
                    link(nc.vector.tensor_tensor(
                        filled[:], upto[:, PAD + HALF - 1, :].unsqueeze(2).broadcast_to([P, NE, HALF]),
                        steps[:].unsqueeze(1).broadcast_to([P, NE, HALF]), ALU.is_gt))
                    nc.vector.tensor_tensor(rank[:], rank[:], per_tile(before_bank), ALU.add)
                    link(nc.vector.reduce_sum(tiles_of[:], filled[:], AX.X))
                    link(nc.vector.tensor_copy(ends[0][:, EPAD:], tiles_of[:]))
                    i, reach = 0, 1
                    while reach < NE:
                        link(nc.vector.tensor_tensor(ends[1 - i][:, EPAD:], ends[i][:, EPAD:],
                                                     ends[i][:, EPAD - reach:EPAD + NE - reach], ALU.add))
                        i, reach = 1 - i, 2 * reach
                    end = ends[i][:, EPAD:]
                    link(nc.vector.tensor_tensor(start[:], end, tiles_of[:], ALU.subtract))
                    link(nc.vector.tensor_scalar(start[:], start[:], float(h * HALF_SLOTS), float(P),
                                                 ALU.add, ALU.mult))
                    link(nc.vector.tensor_tensor(rank[:], rank[:], start[:].unsqueeze(1)
                                                 .broadcast_to([P, HALF, NE]), ALU.add))
                    for k in range(TOP):
                        last = nc.vector.tensor_tensor(place[:, k], hit[:, k, tiles], rank[:], ALU.mult)
                    link(last)
                    for k in range(TOP):
                        last = nc.vector.reduce_sum(placef[:, :, k], place[:, k], AX.X)
                    link(last)
                    nc.vector.tensor_copy(slots[:, tiles], placef[:]).then_inc(placed, 1)
                    link(nc.vector.tensor_tensor(
                        passed[:], end[:, 0:NE - 1].unsqueeze(1).broadcast_to([P, HALF_SLOTS, NE - 1]),
                        tile_number[:].unsqueeze(2).broadcast_to([P, HALF_SLOTS, NE - 1]), ALU.is_le))
                    link(nc.vector.reduce_sum(expertf[:], passed[:], AX.X))
                    link(nc.vector.tensor_copy(expert_of[:, h * HALF_SLOTS:(h + 1) * HALF_SLOTS], expertf[:]))

                statistics(0)
                statistics(1)
                normalise(0)
                normalise(1)
                statistics(2)
                add_bias(0)
                add_bias(1)
                choose(0)
                choose(1)
                place_half(0)
                statistics(3)
                normalise(2)
                normalise(3)
                add_bias(2)
                add_bias(3)
                choose(2)
                choose(3)
                place_half(1)

            @block.scalar
            def _(act):
                def deviations(b):
                    if b == 0:
                        act.wait_ge(eps_set, 1)
                    act.wait_ge(aggregated, TB * (b + 1))
                    nc.scalar.activation(std[:, b * TB:(b + 1) * TB], meanvar[:, b * TB:(b + 1) * TB, 1], ACT.Sqrt,
                                         bias=eps[:, 0:1]).then_inc(std_done, 1)

                def evacuate(b):
                    for q in quads(b):
                        act.wait_ge(transposed, q + 1)
                        nc.scalar.activation(XT[:, q * BANK:(q + 1) * BANK], banks[q % BANKS][:, :], ACT.Copy)\
                            .then_inc(evacuated, 1)

                def sigmoids(b):
                    act.wait_ge(biased, b + 1)
                    s = scores[:, b * TB:(b + 1) * TB, :].rearrange("p t e -> p (t e)")
                    nc.scalar.activation(s, s, ACT.Sigmoid).then_inc(scored, 1)

                deviations(0)
                deviations(1)
                evacuate(0)
                evacuate(1)
                deviations(2)
                sigmoids(0)
                sigmoids(1)
                deviations(3)
                evacuate(2)
                evacuate(3)
                sigmoids(2)
                sigmoids(3)

            @block.tensor
            def _(pe):
                def transposes(b):
                    for q in quads(b):
                        pe.wait_ge(normed, q + 1)
                        if q >= BANKS:
                            pe.wait_ge(evacuated, q - BANKS + 1)
                        for t in range(TH):
                            last = nc.tensor.transpose(banks[q % BANKS][:, t * P:(t + 1) * P],
                                                       XN[:, q * TH + t, :], ident[:, :])
                        last.then_inc(transposed, 1)

                def route(b):
                    if b == 0:
                        pe.wait_ge(small_in, 16 * len(small))
                    pe.wait_ge(evacuated, (b + 1) * QB)
                    if b >= 2:
                        pe.wait_ge(biased, b - 1)
                    for t in range(TB):
                        i = b * TB + t
                        last = nc.tensor.matmul(logits[b % 2][:, t * NE:(t + 1) * NE], XT[:, i * P:(i + 1) * P],
                                                gateT[:], start=True, stop=True)
                    last.then_inc(routed, 1)

                def count(h):
                    pe.wait_ge(hits_done, h + 1)
                    cols = slice(h * HALF * NE, (h + 1) * HALF * NE)
                    for bank, lhs in ((before_bank, earlier), (total_bank, ones)):
                        nc.tensor.matmul(bank[:, cols], lhs[:], hits[:].rearrange("p t e -> p (t e)")[:, cols],
                                         start=True, stop=True).then_inc(counted, 1)

                transposes(0)
                transposes(1)
                route(0)
                route(1)
                count(0)
                transposes(2)
                transposes(3)
                route(2)
                route(3)
                count(1)

            @block.gpsimd
            def _(pool):
                pool.wait_ge(placed, 1)
                scatter(pool, 0)


def expert_phase(nc, phase, X, XT, scratch, ident, c, w, W, first, store=None):
    with ExitStack() as ctx:
        sem = Sems(nc, ctx, phase)
        sb = lambda name, shape, dt=F32: ctx.enter_context(nc.sbuf_tensor(f"{phase}_{name}", shape, dt))
        share = sb("share", [P, TILES, TOP])
        slots = sb("slots", [P, TILES, TOP], mybir.dt.uint32)
        expert_of = sb("expert_of", [P, SLOT_TILES], mybir.dt.int32)
        XN = sb("XN", [P, TILES, D])
        tokens, results = scratch["tokens"], scratch["results"]
        scattered = sem(*[f"scattered{h}" for h in range(HALVES)])

        def scatter(pool, h):
            for t in range(h * HALF, (h + 1) * HALF):
                for k in range(TOP):
                    pool.indirect_dma_start(tokens[:, :], bass.IndirectOffsetOnAxis(slots[:, t, k:k + 1], 0),
                                            XN[:, t, :], None).then_inc(scattered[h], 16)

        routing_phase(nc, phase, X, XT, XN, share, slots, expert_of, scratch, scatter, ident, c, w, W, first)

        w1, w3, w2 = [W[n][:].rearrange("p (e m) -> p e m", e=NE) for n in ("w1", "w3", "w2")]
        PH = HT * P
        x = sb("x", [P, 2, TH, D])
        xT = sb("xT", [P, 2, BANK])
        gated = sb("gated", [P, 2, HID]); hidden = sb("hidden", [P, 2, PH])
        hT = sb("hT", [P, 2, PH])
        y = sb("y", [P, 2, TH, D])
        ps = lambda name: ctx.enter_context(nc.psum_tensor(f"{phase}_{name}", [P, BANK], F32))
        bankX, bankH = ps("bankX"), ps("bankH")
        bank1, bank3, bankY = [[ps(f"{n}{i}") for i in range(2)] for n in ("bank1", "bank3", "bankY")]
        (turned, x_ready, up_ready, silu_done, hidden_done, ht_ready, ht_taken, y_ready, y_taken) = sem(
            "turned", "x_ready", "up_ready", "silu_done", "hidden_done", "ht_ready", "ht_taken", "y_ready",
            "y_taken")
        x_in, y_stored = sem("x_in0", "x_in1"), sem("y_stored0", "y_stored1")
        GROUPS = SLOT_TILES // TH
        STEP = 2 * TH
        STEPS = SLOT_TILES // STEP
        HALF_STEPS = STEPS // HALVES
        assert HALF_SLOTS % STEP == 0
        RING = 4
        pair = sb("pair", [P, RING, TOP, D])
        gathered = sem(*[f"gathered{i}" for i in range(RING)])
        chain = sem(*[f"chain{h}" for h in range(HALVES)])
        added = sem(*[f"added{h}" for h in range(HALVES)])
        stored = sem("stored")[0]

        of_group = lambda a, g: a[ds(g * TH * P, TH * P), :].rearrange("(t p) d -> p t d", p=P)

        with nc.Block() as block:
            @block.sync
            def _(sp):
                def load(g, p, first=False):
                    if not first:
                        sp.wait_ge(turned, g - 1)
                    sp.dma_start(x[:, p], of_group(tokens, g)).then_inc(x_in[p], 16)

                sp.wait_ge(scattered[0], 16 * HALF * TOP)
                load(0, 0, True)
                load(1, 1, True)
                with sp.Fori(1, HALF_STEPS) as i:
                    load(2 * i, 0)
                    load(2 * i + 1, 1)
                for h in range(1, HALVES):
                    sp.wait_ge(scattered[h], 16 * HALF * TOP)
                    with sp.Fori(h * HALF_STEPS, (h + 1) * HALF_STEPS) as i:
                        load(2 * i, 0)
                        load(2 * i + 1, 1)
                if store is not None:
                    for b in range(B):
                        last = (b + 1) * TB - 1
                        sp.wait_ge(added[last // HALF], last % HALF + 1)
                        store(sp, b, stored)
                    sp.wait_ge(stored, 16 * B)

            @block.tensor
            def _(pe):
                load_expert = lambda j: pe.value_load(expert_of[0:1, ds(j, 1)], min_val=0, max_val=NE - 1)
                experts = [None] * STEP

                def turn(i, p, first=False):
                    g = 2 * i + p
                    pe.wait_ge(x_in[p], 16 * i + 16)
                    if not (first and g == 0):
                        pe.wait_ge(x_ready, g)
                    for t in range(TH):
                        last = nc.tensor.transpose(bankX[:, t * P:(t + 1) * P], x[:, p, t, :], ident[:])
                    last.then_inc(turned, 1)

                def up(i, k, first=False):
                    j, p = STEP * i + k, k // TH
                    if k % TH == 0:
                        pe.wait_ge(x_ready, 2 * i + p + 1)
                    if not (first and k < 2):
                        pe.wait_ge(hidden_done, j - 1)
                    if k == 0:
                        experts[0] = load_expert(j)
                    e = experts[k]
                    for bank, W13 in ((bank1[k % 2], w1), (bank3[k % 2], w3)):
                        last = nc.tensor.matmul(bank[:, 0:HID], xT[:, p, (k % TH) * P:(k % TH + 1) * P],
                                                W13[:, ds(e, 1), :], start=True, stop=True)
                    last.then_inc(up_ready, 1)
                    if k + 1 < STEP:
                        experts[k + 1] = load_expert(j + 1)

                def turn_hidden(j, k, first=False):
                    pe.wait_ge(hidden_done, j + 1)
                    if not (first and k == 0):
                        pe.wait_ge(ht_taken, j)
                    for t in range(HT):
                        last = nc.tensor.transpose(bankH[:, t * P:(t + 1) * P], hidden[:, k % 2, t * P:(t + 1) * P],
                                                   ident[:])
                    last.then_inc(ht_ready, 1)

                def down(j, g, k, e, first=False):
                    pe.wait_ge(ht_taken, j + 1)
                    if k % TH == 0 and not first:
                        pe.wait_ge(y_taken, g - 1)
                    w2e = w2[:, ds(e, 1), :].rearrange("p e m -> p (e m)")
                    for t in range(HT):
                        last = nc.tensor.matmul(bankY[k // TH][:, (k % TH) * P:(k % TH + 1) * P],
                                                hT[:, k % 2, t * P:(t + 1) * P], w2e[:, t * D:(t + 1) * D],
                                                start=(t == 0), stop=(t == HT - 1))
                    last.then_inc(y_ready, 1)

                def step(i, first=False, final=False):
                    for k in range(STEP):
                        j = STEP * i + k
                        up(i, k, first)
                        if k or not first:
                            turn_hidden(j - 1, (k - 1) % STEP, first)
                        if k >= 2:
                            down(j - 2, 2 * i + (k - 2) // TH, k - 2, experts[k - 2], first)
                        elif not first:
                            down(j - 2, 2 * i - 1, STEP + k - 2, load_expert(j - 2))
                        if k == 1:
                            turn(i, 1, first)
                        if k == TH + 1 and not final:
                            turn(i + 1, 0)

                if first:
                    pe.wait_ge(W["in"], 48)
                turn(0, 0, True)
                step(0, first=True)
                with pe.Fori(1, STEPS - 1) as i:
                    step(i)
                step(STEPS - 1, final=True)
                turn_hidden(SLOT_TILES - 1, STEP - 1)
                down(SLOT_TILES - 2, GROUPS - 1, STEP - 2, experts[STEP - 2])
                down(SLOT_TILES - 1, GROUPS - 1, STEP - 1, experts[STEP - 1])

            @block.scalar
            def _(act):
                def take_tokens(g, p, first=False):
                    act.wait_ge(turned, g + 1)
                    if not first:
                        act.wait_ge(up_ready, TH * (g - 1))
                    nc.scalar.copy(xT[:, p, :], bankX[:]).then_inc(x_ready, 1)

                def silu(j, k, first=False):
                    act.wait_ge(up_ready, j + 1)
                    if not (first and k < 2):
                        act.wait_ge(hidden_done, j - 1)
                    nc.scalar.activation(gated[:, k % 2, :], bank1[k % 2][:, 0:HID], ACT.Silu).then_inc(silu_done, 1)

                def take_hidden(j, k, first=False):
                    act.wait_ge(ht_ready, j + 1)
                    if not (first and k < 2):
                        act.wait_ge(y_ready, j - 1)
                    nc.scalar.copy(hT[:, k % 2, :], bankH[:, 0:PH]).then_inc(ht_taken, 1)

                def store(g, p):
                    act.wait_ge(y_taken, g + 1)
                    act.dma_start(of_group(results, g), y[:, p]).then_inc(y_stored[p], 16)

                def step(i, first=False, final=False):
                    for k in range(STEP):
                        j = STEP * i + k
                        silu(j, k, first)
                        if k == TH - 1 and not first:
                            store(2 * i - 1, 1)
                        if k == STEP - 1:
                            store(2 * i, 0)
                        if k or not first:
                            take_hidden(j - 1, (k - 1) % STEP, first)
                        if k == 1:
                            take_tokens(2 * i + 1, 1, first)
                        if k == TH + 1 and not final:
                            take_tokens(2 * i + 2, 0)

                take_tokens(0, 0, True)
                step(0, first=True)
                with act.Fori(1, STEPS - 1) as i:
                    step(i)
                step(STEPS - 1, final=True)
                take_hidden(SLOT_TILES - 1, STEP - 1)
                store(GROUPS - 1, 1)

            @block.vector
            def _(dve):
                def multiply(j, k, first=False):
                    dve.wait_ge(silu_done, j + 1)
                    if not (first and k < 2):
                        dve.wait_ge(ht_ready, j - 1)
                    nc.vector.tensor_tensor(hidden[:, k % 2, 0:HID], bank3[k % 2][:, 0:HID], gated[:, k % 2, :],
                                            ALU.mult).then_inc(hidden_done, 1)

                def take_results(i, p, first=False):
                    dve.wait_ge(y_ready, TH * (2 * i + p) + TH)
                    if not first:
                        dve.wait_ge(y_stored[p], 16 * i)
                    nc.vector.tensor_copy(y[:, p].rearrange("p t d -> p (t d)"), bankY[p][:]).then_inc(y_taken, 1)

                def step(i, first=False):
                    for k in range(STEP):
                        multiply(STEP * i + k, k, first)
                        if k == TH + 2:
                            take_results(i, 0, first)
                        if k == 2 and not first:
                            take_results(i - 1, 1, isinstance(i, int) and i == 1)

                for k in range(2):
                    nc.vector.memset(hidden[:, k, HID:PH], 0.0)
                step(0, first=True)
                step(1)
                with dve.Fori(2, STEPS) as i:
                    step(i)
                take_results(STEPS - 1, 1)

                for t in range(HALF, TILES):
                    dve.wait_ge(gathered[t % RING], 16 * TOP * (t // RING + 1))
                    for k in range(TOP):
                        if k:
                            dve.wait_ge(chain[1], t - HALF + 1)
                        nc.vector.scalar_tensor_tensor(out=X[:, t, :], in0=pair[:, t % RING, k, :],
                                                       scalar=share[:, t, k:k + 1], in1=X[:, t, :],
                                                       op0=ALU.mult, op1=ALU.add).then_inc(
                            added[1] if k else chain[1], 1)

            @block.gpsimd
            def _(pool):
                for h in range(1, HALVES):
                    scatter(pool, h)

                def gather(t):
                    if t >= RING:
                        pool.wait_ge(added[(t - RING) // HALF], (t - RING) % HALF + 1)
                    for k in range(TOP):
                        pool.indirect_dma_start(pair[:, t % RING, k, :], None, results[:, :],
                                                bass.IndirectOffsetOnAxis(slots[:, t, k:k + 1], 0))\
                            .then_inc(gathered[t % RING], 16)

                def add(t):
                    rows = pair[:, t % RING]
                    pool.wait_ge(gathered[t % RING], 16 * TOP * (t // RING + 1))
                    nc.gpsimd.tensor_tensor(rows, rows, share[:, t, :].unsqueeze(2).broadcast_to([P, TOP, D]),
                                            ALU.mult).then_inc(chain[0], 1)
                    pool.wait_ge(chain[0], 2 * t + 1)
                    nc.gpsimd.tensor_tensor(rows[:, 0, :], rows[:, 0, :], rows[:, 1, :], ALU.add)\
                        .then_inc(chain[0], 1)
                    pool.wait_ge(chain[0], 2 * t + 2)
                    nc.gpsimd.tensor_tensor(X[:, t, :], X[:, t, :], rows[:, 0, :], ALU.add).then_inc(added[0], 1)

                def half_stored(h):
                    for p in range(2):
                        pool.wait_ge(y_stored[p], 16 * HALF_STEPS * (h + 1))

                half_stored(0)
                for t in range(HALF):
                    gather(t)
                    if t >= RING - 1:
                        add(t - RING + 1)
                for t in range(HALF - RING + 1, HALF):
                    add(t)
                half_stored(1)
                for t in range(HALF, TILES):
                    gather(t)


def decay_phase(nc, X, XT, ident, c, w):
    R = B * P
    with ExitStack() as ctx:
        sem = Sems(nc, ctx, "decay")
        sb = lambda name, shape, dt=F32: ctx.enter_context(nc.sbuf_tensor(f"decay_{name}", shape, dt))
        ps = lambda name: ctx.enter_context(nc.psum_tensor(f"decay_{name}", [P, BANK], F32))
        WqT = sb("WqT", [D, D]); WkT = sb("WkT", [D, D]); WvT = sb("WvT", [D, D]); WoT = sb("WoT", [D, D])
        masks = sb("masks", [P, HG])
        same = sb("same", [P, D])
        lag = sb("lag", [P, P])
        causal = sb("causal", [P, P])
        ahead = sb("ahead", [P, P])
        behind = sb("behind", [P, 1])
        lgr = sb("lgr", [P, H]); lgc = sb("lgc", [P, 1])
        tr = sb("tr", [P, 2, H]); tc = sb("tc", [P, 2])
        eps = sb("eps", [P, 1])
        Dm = sb("Dm", [P, HG, G, P])
        Gq = sb("Gq", [P, P])
        Gk = sb("Gk", [P, H])
        Gs = sb("Gs", [P, 1])
        XTc = sb("XTc", [D, 2, R])
        qT = sb("qT", [P, R]); qg = sb("qg", [P, 2, R])
        qm = sb("qm", [P, 2, G, R])
        kraw = sb("kraw", [P, R]); kc = sb("kc", [P, R]); ksq = sb("ksq", [P, R])
        kmean = sb("kmean", [P, B * H]); kstd = sb("kstd", [P, B * H])
        kn = sb("kn", [P, R]); kg = sb("kg", [P, 2, R]); v = sb("v", [P, 2, R])
        km = sb("km", [P, 2, HG, R])
        Am = sb("Am", [P, 2, G, P])
        S = sb("S", [P, 2, R]); Sadd = sb("Sadd", [P, R])
        vj = sb("vj", [P, 2, HG, R])
        yT = sb("yT", [P, R])
        (loaded, act_setup, pool_setup, chain) = sem("loaded", "act_setup", "pool_setup", "chain")
        (x_in, q_ready, k_ready, v_ready, q_taken, k_taken, v_taken, qg_done) = sem(
            "x_in", "q_ready", "k_ready", "v_ready", "q_taken", "k_taken", "v_taken", "qg_done")
        (ksum_done, kmean_done, kc_done, ksq_done, kvar_done, kstd_done, krstd_done, kn_done, kg_done) = sem(
            "ksum_done", "kmean_done", "kc_done", "ksq_done", "kvar_done", "kstd_done", "krstd_done", "kn_done",
            "kg_done")
        (kt_ready, km_done, a_ready, am_done, am_used, s_ready, sadd_done, s_done, y_taken) = sem(
            "kt_ready", "km_done", "a_ready", "am_done", "am_used", "s_ready", "sadd_done", "s_done",
            "y_taken")
        (o_ready, o_added) = sem("o_ready", "o_added")
        XTv = XT[:].rearrange("d (b c t) -> d b c t", b=B, c=TB)
        Xv = X[:].rearrange("p (b c) e -> p b c e", b=B)
        heads = lambda a: a.rearrange("p (n e) -> p n e", e=HD)

        loads = ((WqT[:], w["b_WqT"]), (WkT[:], w["b_WkT"]), (WvT[:], w["b_WvT"]), (WoT[:], w["b_WoT"]),
                 (masks[:], c["masks_b"]), (same[:], c["same_head"]), (lag[:], c["lag"]),
                 (causal[:], c["causal"]), (ahead[:], c["ahead"]), (behind[:], c["behind"]),
                 (lgr[:], w["log_gamma"].partition_broadcast(P)), (lgc[:], w["log_gamma_rows"]))

        def constants(block):
            @block.sync
            def _(sp):
                for dst, src in loads:
                    sp.dma_start(dst, src).then_inc(loaded, 16)

            @block.gpsimd
            def _(pool):
                count = [0]

                def link(ins):
                    count[0] += 1
                    ins.then_inc(chain, 1)
                    pool.wait_ge(chain, count[0])

                link(nc.gpsimd.memset(eps[:], LN_EPS))
                pool.wait_ge(loaded, 16 * len(loads))
                layouts = ((lgr[:], tr[:, 0, :], tr[:, 1, :]), (lgc[:], tc[:, 0:1], tc[:, 1:2]))
                for x, above, below in layouts:
                    link(nc.gpsimd.tensor_scalar(below, x, 0.0, None, ALU.min))
                    link(nc.gpsimd.tensor_scalar(above, x, 0.0, None, ALU.max))
                    nc.gpsimd.tensor_tensor(above, below, above, ALU.subtract).then_inc(pool_setup, 1)
                link(nc.gpsimd.memset(vj[:], 0.0))
                link(nc.gpsimd.memset(qm[:], 0.0))
                link(nc.gpsimd.memset(S[:, 0, :], 0.0))
                pool.wait_ge(act_setup, 2)
                for x, above, below in layouts:
                    nc.gpsimd.tensor_tensor(x, below, above, ALU.subtract).then_inc(pool_setup, 1)
                for j in range(HG):
                    pool.wait_ge(act_setup, 5 + j)
                    nc.gpsimd.tensor_tensor(Dm[:, j], Dm[:, j], causal[:].unsqueeze(1).broadcast_to([P, G, P]),
                                            ALU.mult)

        def powers(act):
            act.wait_ge(pool_setup, 2)
            nc.scalar.activation(tr[:, 0, :], tr[:, 0, :], ACT.Exp).then_inc(exps, 1)
            nc.scalar.activation(tc[:, 0:1], tc[:, 0:1], ACT.Exp).then_inc(exps, 1)
            act.wait_ge(exps, 2)
            nc.scalar.activation(tr[:, 0, :], tr[:, 0, :], ACT.Ln, bias=1.0).then_inc(act_setup, 1)
            nc.scalar.activation(tc[:, 0:1], tc[:, 0:1], ACT.Ln, bias=1.0).then_inc(act_setup, 1)
            act.wait_ge(pool_setup, 4)
            nc.scalar.activation(Gq[:], ahead[:], ACT.Exp, scale=lgc[:, 0:1]).then_inc(act_setup, 1)
            nc.scalar.activation(Gs[:], lgc[:], ACT.Exp, scale=float(P))
            nc.scalar.activation(Gk[:], lgr[:], ACT.Exp, scale=behind[:, 0:1]).then_inc(act_setup, 1)
            for j in range(HG):
                for g in range(G):
                    h = g * HG + j
                    last = nc.scalar.activation(Dm[:, j, g, :], lag[:], ACT.Exp, scale=lgr[:, h:h + 1])
                last.then_inc(act_setup, 1)

        exps = sem("exps")[0]
        layernorm_phase(nc, "ln2", X, XT, ident, side_job=constants, act_job=powers)
        bankA = [ps("bankA0"), ps("bankA1")]
        bankY, bankS, bankQ, bankK, bankV, bankT = [ps("bank" + n) for n in "YSQKVT"]

        with nc.Block() as block:
            def steps(eng, prepare, work):
                prepare(0, 0)
                work(0, 0)
                with eng.Fori(0, (TB - 2) // 2) as i:
                    work(2 * i + 1, 1)
                    work(2 * i + 2, 0)
                work(TB - 1, 1)

            static = lambda n, below: isinstance(n, int) and n < below
            final = lambda n: isinstance(n, int) and n == TB - 1
            UNITS = B * HG

            @block.tensor
            def _(pe):
                def project(n, p):
                    pe.wait_ge(x_in, n + 1)
                    for bank, W, ready, free in ((bankK, WkT, k_ready, k_taken), (bankV, WvT, v_ready, v_taken)):
                        if not static(n, 1):
                            pe.wait_ge(free, n)
                        for b in range(B):
                            last = nc.tensor.matmul(bank[:, b * P:(b + 1) * P], XTc[:, p, b * P:(b + 1) * P], W[:],
                                                    start=True, stop=True)
                        last.then_inc(ready, 1)
                    if not static(n, 1):
                        pe.wait_ge(q_taken, n)
                    nc.tensor.matmul(bankQ[:], WqT[:], XTc[:, p, :], start=True, stop=True).then_inc(q_ready, 1)

                def transpose_keys(n, p):
                    pe.wait_ge(kn_done, n + 1)
                    if not static(n, 1):
                        pe.wait_ge(km_done, n)
                        if not static(n, 2):
                            pe.wait_ge(o_added, n - 1)
                    for b in range(B):
                        last = nc.tensor.transpose(bankT[:, b * P:(b + 1) * P], kn[:, b * P:(b + 1) * P], ident[:])
                    last.then_inc(kt_ready, 1)

                def scores(n, p, u):
                    b, j = u // HG, u % HG
                    if u == 0:
                        pe.wait_ge(km_done, n + 1)
                        pe.wait_ge(q_taken, n + 1)
                    if not (static(n, 1) and u < 2):
                        pe.wait_ge(am_done, UNITS * n + u - 1)
                    nc.tensor.matmul(bankA[u % 2][:], km[:, p, j, b * P:(b + 1) * P], qm[:, p, :, b * P:(b + 1) * P],
                                     start=True, stop=True).then_inc(a_ready, 1)

                def past(n, p, b):
                    if b == 0:
                        pe.wait_ge(qg_done, n + 1)
                        if not static(n, 1):
                            pe.wait_ge(s_done, n)
                            pe.wait_ge(y_taken, n)
                    nc.tensor.matmul(bankY[:, b * P:(b + 1) * P], S[:, p, b * P:(b + 1) * P],
                                     qg[:, p, b * P:(b + 1) * P], start=True, stop=False)

                def within(n, p, u):
                    b, j = u // HG, u % HG
                    if u == 0:
                        pe.wait_ge(v_taken, n + 1)
                    pe.wait_ge(am_done, UNITS * n + u + 1)
                    for g in range(G):
                        rows = slice(g * GE, (g + 1) * GE)
                        last = nc.tensor.matmul(bankY[rows, b * P:(b + 1) * P],
                                                vj[:, p, j, b * P + g * GE:b * P + (g + 1) * GE], Am[:, u % 2, g, :],
                                                start=False, stop=(j == HG - 1), tile_position=(0, g * GE))
                    last.then_inc(am_used, 1)

                def state(n, p):
                    pe.wait_ge(kg_done, n + 1)
                    if not static(n, 1):
                        pe.wait_ge(sadd_done, n)
                    for b in range(B):
                        cols = slice(b * P, (b + 1) * P)
                        last = nc.tensor.matmul(bankS[:, cols], kg[:, p, cols], v[:, p, cols], start=True, stop=True)
                    last.then_inc(s_ready, 1)

                def project_output(n):
                    pe.wait_ge(y_taken, n + 1)
                    for b in range(B):
                        last = nc.tensor.matmul(bankT[:, b * P:(b + 1) * P], yT[:, b * P:(b + 1) * P], WoT[:],
                                                start=True, stop=True)
                    last.then_inc(o_ready, 1)

                def work(n, p):
                    scores(n, p, 0)
                    for u in range(UNITS):
                        if u + 1 < UNITS:
                            scores(n, p, u + 1)
                        if u % HG == 0:
                            past(n, p, u // HG)
                        within(n, p, u)
                        if u == 3 and not static(n, 1):
                            project_output(n - 1)
                        if not final(n):
                            if u == 1:
                                project(n + 1, 1 - p)
                            if u == 13:
                                transpose_keys(n + 1, 1 - p)
                        if u == 5:
                            state(n, p)

                def prepare(n, p):
                    project(n, p)
                    transpose_keys(n, p)

                steps(pe, prepare, work)
                project_output(TB - 1)

            @block.scalar
            def _(act):
                def take_projections(n, p):
                    act.wait_ge(k_ready, n + 1)
                    if not static(n, 1):
                        act.wait_ge(kc_done, n)
                        act.wait_ge(ksum_done, n)
                    nc.scalar.copy(kraw[:], bankK[:]).then_inc(k_taken, 1)
                    act.wait_ge(v_ready, n + 1)
                    nc.scalar.copy(v[:, p, :], bankV[:])
                    by_head = lambda a, j: a.rearrange("p (n j e) -> p n j e", j=HG, e=HD)[:, :, j, :]
                    for j in range(HG):
                        last = nc.scalar.copy(by_head(vj[:, p, j, :], j), by_head(bankV[:], j))
                    last.then_inc(v_taken, 1)
                    act.wait_ge(q_ready, n + 1)
                    if not static(n, 1):
                        act.wait_ge(qg_done, n)
                    nc.scalar.copy(qT[:], bankQ[:])
                    for g in range(G):
                        rows = slice(g * GE, (g + 1) * GE)
                        last = nc.scalar.copy(qm[rows, p, g, :], bankQ[rows, :])
                    last.then_inc(q_taken, 1)

                def deviations(n, p):
                    act.wait_ge(kvar_done, n + 1)
                    nc.scalar.activation(kstd[:], kstd[:], ACT.Sqrt, scale=1.0 / HD, bias=eps[:, 0:1])\
                        .then_inc(kstd_done, 1)

                def mask_keys(n, p):
                    act.wait_ge(kt_ready, n + 1)
                    for j in range(HG):
                        last = nc.scalar.activation(km[:, p, j, :], bankT[:], ACT.Copy, scale=masks[:, j:j + 1])
                    last.then_inc(km_done, 1)

                def take_y(n):
                    act.wait_ge(am_used, UNITS * (n + 1))
                    if not static(n, 1):
                        act.wait_ge(o_ready, n)
                    nc.scalar.copy(yT[:], bankY[:]).then_inc(y_taken, 1)

                def prepare(n, p):
                    take_projections(n, p)
                    deviations(n, p)
                    mask_keys(n, p)

                def work(n, p):
                    if not final(n):
                        prepare(n + 1, 1 - p)
                    take_y(n)

                steps(act, prepare, work)

            @block.vector
            def _(dve):
                def take_tokens(n, p):
                    if not static(n, 2):
                        dve.wait_ge(q_ready, n - 1)
                    nc.vector.tensor_copy(XTc[:, p, :].rearrange("d (b t) -> d b t", b=B),
                                          XTv[:, :, ds(n, 1), :].rearrange("d b c t -> d b (c t)")).then_inc(x_in, 1)

                def key_means(n):
                    dve.wait_ge(k_taken, n + 1)
                    if not static(n, 1):
                        dve.wait_ge(kc_done, n)
                    nc.vector.reduce_sum(kmean[:], heads(kraw[:]), AX.X).then_inc(ksum_done, 1)
                    dve.wait_ge(ksum_done, n + 1)
                    nc.vector.tensor_scalar(kmean[:], kmean[:], 1.0 / HD, None, ALU.mult).then_inc(kmean_done, 1)

                def key_squares(n):
                    dve.wait_ge(ksq_done, n + 1)
                    nc.vector.reduce_sum(kstd[:], heads(ksq[:]), AX.X).then_inc(kvar_done, 1)

                def key_inverses(n):
                    dve.wait_ge(kstd_done, n + 1)
                    nc.vector.reciprocal(kstd[:], kstd[:]).then_inc(krstd_done, 1)

                def decay(n, u):
                    dve.wait_ge(a_ready, UNITS * n + u + 1)
                    if not (static(n, 1) and u < 2):
                        dve.wait_ge(am_used, UNITS * n + u - 1)
                    nc.vector.tensor_tensor(Am[:, u % 2].rearrange("p g t -> p (g t)"), bankA[u % 2][:],
                                            Dm[:, u % HG].rearrange("p g t -> p (g t)"),
                                            ALU.mult).then_inc(am_done, 1)

                def next_state(n, p):
                    dve.wait_ge(s_ready, n + 1)
                    nc.vector.tensor_tensor(Sadd[:].rearrange("p (b e) -> p b e", b=B),
                                            bankS[:].rearrange("p (b e) -> p b e", b=B),
                                            same[:].unsqueeze(1).broadcast_to([P, B, D]), ALU.mult)\
                        .then_inc(sadd_done, 1)
                    dve.wait_ge(sadd_done, n + 1)
                    if not static(n, 1):
                        dve.wait_ge(am_used, UNITS * n)
                    nc.vector.scalar_tensor_tensor(out=S[:, 1 - p, :], in0=S[:, p, :], scalar=Gs[:, 0:1],
                                                   in1=Sadd[:], op0=ALU.mult, op1=ALU.add).then_inc(s_done, 1)

                def add_output(n):
                    dve.wait_ge(o_ready, n + 1)
                    x = Xv[:, :, ds(n, 1), :].rearrange("p b c e -> p b (c e)")
                    nc.vector.tensor_tensor(x, bankT[:].rearrange("p (b e) -> p b e", b=B), x, ALU.add)\
                        .then_inc(o_added, 1)

                def prepare(n, p):
                    take_tokens(n, p)
                    key_means(n)
                    key_squares(n)
                    key_inverses(n)

                def work(n, p):
                    if not final(n):
                        take_tokens(n + 1, 1 - p)
                    for u in range(UNITS):
                        decay(n, u)
                        if not final(n):
                            if u == 4:
                                key_means(n + 1)
                            if u == 8:
                                key_squares(n + 1)
                            if u == 10:
                                key_inverses(n + 1)
                        if u == 5 and not static(n, 1):
                            add_output(n - 1)
                        if u == 7:
                            next_state(n, p)

                steps(dve, prepare, work)
                add_output(TB - 1)

            @block.gpsimd
            def _(pool):
                def prepare(n, p):
                    pool.wait_ge(kmean_done, n + 1)
                    spread = lambda a: a.unsqueeze(2).broadcast_to([P, B * H, HD])
                    if not static(n, 1):
                        pool.wait_ge(kvar_done, n)
                    nc.gpsimd.tensor_tensor(heads(kc[:]), heads(kraw[:]), spread(kmean[:]), ALU.subtract)\
                        .then_inc(kc_done, 1)
                    pool.wait_ge(kc_done, n + 1)
                    nc.gpsimd.tensor_tensor(ksq[:], kc[:], kc[:], ALU.mult).then_inc(ksq_done, 1)
                    pool.wait_ge(q_taken, n + 1)
                    if not static(n, 2):
                        pool.wait_ge(am_used, UNITS * (n - 1))
                        pool.wait_ge(s_ready, n - 1)
                    nc.gpsimd.tensor_tensor(qg[:, p, :].rearrange("p (b t) -> p b t", b=B),
                                            qT[:].rearrange("p (b t) -> p b t", b=B),
                                            Gq[:].unsqueeze(1).broadcast_to([P, B, P]), ALU.mult).then_inc(qg_done, 1)
                    pool.wait_ge(krstd_done, n + 1)
                    if not static(n, 1):
                        pool.wait_ge(kt_ready, n)
                    nc.gpsimd.tensor_tensor(heads(kn[:]), heads(kc[:]), spread(kstd[:]), ALU.mult).then_inc(kn_done, 1)
                    pool.wait_ge(kn_done, n + 1)
                    nc.gpsimd.tensor_tensor(kg[:, p, :].rearrange("p (b h e) -> p b h e", b=B, h=H),
                                            kn[:].rearrange("p (b h e) -> p b h e", b=B, h=H),
                                            Gk[:].unsqueeze(1).unsqueeze(3).broadcast_to([P, B, H, HD]),
                                            ALU.mult).then_inc(kg_done, 1)

                steps(pool, prepare, lambda n, p: None if final(n) else prepare(n + 1, 1 - p))


def build_program(nc, x, c, w, out):
    nc.disable_value_cache = True
    with ExitStack() as ctx:
        sb = lambda name, shape, dt=F32: ctx.enter_context(nc.sbuf_tensor(name, shape, dt))
        X = sb("X", [P, TILES, D])
        XT = sb("XT", [P, B * L])
        ident = sb("ident", [P, P])
        ident_in = ctx.enter_context(nc.semaphore("ident_in"))
        x_tiles = x.rearrange("b (t p) d -> p (b t) d", p=P)

        def load(sp, loaded):
            for b in range(B):
                sp.dma_start(X[:, b * TB:(b + 1) * TB, :], x_tiles[:, b * TB:(b + 1) * TB, :]).then_inc(loaded[b], 16)
            sp.dma_start(ident[:], c["ident"]).then_inc(ident_in, 16)

        def store(sp, b, stored):
            out_tiles = out.rearrange("b (t p) d -> p (b t) d", p=P)
            sp.dma_start(out_tiles[:, b * TB:(b + 1) * TB, :], X[:, b * TB:(b + 1) * TB, :]).then_inc(stored, 16)

        scratch = {name: nc.dram_tensor(name, (SLOT_TILES * P, D), F32, kind="Internal").ap()
                   for name in ("tokens", "results")}

        attention_phase(nc, X, XT, ident, ident_in, c, w, load, scratch)
        W = {name: sb(name, [P, n]) for name, n in (("w1", NE * HID), ("w3", NE * HID), ("w2", NE * HT * D))}
        W["in"] = ctx.enter_context(nc.semaphore("weights_in"))
        expert_phase(nc, "ffn1", X, XT, scratch, ident, c, w, W, first=True)
        decay_phase(nc, X, XT, ident, c, w)
        expert_phase(nc, "ffn2", X, XT, scratch, ident, c, w, W, first=False, store=store)


def shape_constants():
    import numpy as np
    rows = np.arange(3 * GE)
    masks = (rows[:, None] % GE // HD == np.arange(HG)[None, :]).astype(np.float32)
    slopes = np.power(np.float32(2.0), np.linspace(-4.0, -0.3, H, dtype=np.float32)).astype(np.float32)
    bias = -(slopes[:, None] * np.arange(L, dtype=np.float32)[None, :]).astype(np.float32)
    high = (bias.view(np.uint32) & np.uint32(0xFFFFF000)).view(np.float32)
    low = bias - high
    aux = np.zeros((G, 2 + 2 * HG, HG, L), np.float32)
    for g in range(G):
        for j in range(HG):
            aux[g, 0, j], aux[g, 1, j] = high[g * HG + j], low[g * HG + j]
            aux[g, 2 + j, j] = 1.0
            aux[g, 2 + HG + j, j] = 1.0
    row = np.arange(P)
    more = {"masks_b": (row[:, None] % GE // HD == np.arange(HG)[None, :]),
            "same_head": row[:, None] // HD == row[None, :] // HD,
            "lag": np.maximum(row[None, :] - row[:, None], 0), "causal": row[None, :] >= row[:, None],
            "ahead": np.broadcast_to(row[None, :] + 1, (P, P)), "behind": (P - 1 - row)[:, None],
            "number": np.arange(NE), "earlier": row[:, None] < row[None, :], "steps": P * np.arange(HALF),
            "tile_number": np.arange(HALF_SLOTS)}
    more = {k: np.ascontiguousarray(v.astype(np.float32)) for k, v in more.items()}
    return more | {"masks": masks, "key_aux": aux.reshape(G, 2 + 2 * HG, HG * L), "ident": np.eye(P, dtype=np.float32)}


def lay_out(inputs):
    import numpy as np
    a = {k: np.asarray(v) for k, v in inputs.items()}
    thrice = lambda W: np.ascontiguousarray(np.tile(W.T.reshape(D, G, 1, GE), (1, 1, 3, 1)).reshape(D, G, 3 * GE))
    thrice_b = lambda v: np.ascontiguousarray(np.tile(v.reshape(G, 1, GE), (1, 3, 1)).reshape(G, 3 * GE).T)
    return {"Wq3": thrice(a["L0_attn_a_Wq"]), "Wk3": thrice(a["L0_attn_a_Wk"]),
            "bq3": thrice_b(a["L0_attn_a_bq"]), "bk3": thrice_b(a["L0_attn_a_bk"]),
            "WvT": np.ascontiguousarray(a["L0_attn_a_Wv"].T), "WoT": np.ascontiguousarray(a["L0_attn_a_Wo"].T),
            "bv": a["L0_attn_a_bv"], "bo": a["L0_attn_a_bo"]} | lay_out_rest(a)


def lay_out_rest(a):
    import numpy as np
    cat = lambda x, y: np.concatenate([a["L0_ffn_" + x], a["L0_ffn_" + y]], axis=0)
    up = lambda W: np.ascontiguousarray(W.transpose(2, 0, 1).reshape(D, NE * HID))
    w2 = np.zeros((P, NE, HT, D), np.float32)
    down = cat("w2", "new_w2").transpose(2, 0, 1)
    for t in range(HT):
        rows = min(P, HID - t * P)
        w2[:rows, :, t] = down[t * P:t * P + rows]
    Wqkv = a["L0_attn_b_W_qkv"]
    turn = lambda W: np.ascontiguousarray(W.T)
    log_gamma = a["L0_attn_b_log_gamma"]
    return {"w1T": up(cat("w1", "new_w1")), "w3T": up(cat("w3", "new_w3")), "w2T": w2.reshape(P, -1),
            "gateT": turn(cat("gate_weight", "new_gate_weight")),
            "gbias": np.concatenate([np.zeros(NE - 1, np.float32), a["L0_ffn_gate_bias"]]),
            "b_WqT": turn(Wqkv[0:D]), "b_WkT": turn(Wqkv[D:2 * D]), "b_WvT": turn(Wqkv[2 * D:3 * D]),
            "b_WoT": turn(a["L0_attn_b_W_o"]), "log_gamma": log_gamma,
            "log_gamma_rows": np.ascontiguousarray(np.repeat(log_gamma, HD)[:, None])}


def kernel(**inputs):
    import numpy as _np
    import concourse.bacc as _bacc
    from concourse import mybir as _mybir
    from concourse.bass_utils import run_bass_kernel_spmd as _run

    nc = _bacc.Bacc("TRN2", target_bir_lowering=False, num_devices=1)
    arrays = {}

    def declare(prefix, named):
        aps = {}
        for name, a in named.items():
            a = _np.ascontiguousarray(a)
            arrays[prefix + name] = a
            aps[name] = nc.dram_tensor(prefix + name, a.shape, _mybir.dt.from_np(a.dtype), kind="ExternalInput").ap()
        return aps

    x = declare("in_", {"x": _np.asarray(inputs["L0_attn_a_x"])})["x"]
    c = declare("const_", shape_constants())
    w = declare("weight_", lay_out(inputs))
    out = nc.dram_tensor("out_dram", (B, L, D), _mybir.dt.float32, kind="ExternalOutput").ap()
    build_program(nc, x, c, w, out)
    r = _run(nc, [arrays], core_ids=[0])
    return r.results[0]["out_dram"]
```
